# Optimizing a Trainium2 kernel written in Bass

```python
import numpy as np
import jax
import jax.numpy as jnp

def _softmax(x, axis=-1):
    return jax.nn.softmax(x, axis=axis)

def _gelu(x):
    return jax.nn.gelu(x, approximate=True)

def _silu(x):
    return jax.nn.silu(x)

def _sigmoid(x):
    return jax.nn.sigmoid(x)

def _layernorm(x, axis=-1, eps=1e-05):
    m = jnp.mean(x, axis=axis, keepdims=True)
    v = jnp.var(x, axis=axis, keepdims=True)
    return (x - m) / jnp.sqrt(v + eps)

def _scatter_add(tgt, idx, src, axis=0):
    return tgt.at[idx].add(src)

def _segment_sum(src, seg, n):
    return jax.ops.segment_sum(src, seg, n)
kernel_name = 'mk_prb_d2_jaxref_r8_1ea637'

def setup_inputs(seed: int=0):
    np.random.seed(seed)
    _w = jnp.asarray

    def _L0_attn_setup():
        import jax, jax.numpy as jnp
        import numpy as np
        D_MODEL = 128
        D_STATE = 16
        D_CONV = 4
        EXPAND = 2
        D_INNER = EXPAND * D_MODEL
        DT_RANK = D_MODEL // 16
        BATCH, SEQ = (8, 256)
        EPS = 1e-12

        def _layernorm(x, g, b):
            m = x.mean(-1, keepdims=True)
            v = ((x - m) ** 2).mean(-1, keepdims=True)
            return (x - m) / jnp.sqrt(v + EPS) * g + b

        def _l2norm(x, axis):
            n = jnp.sqrt((x * x).sum(axis, keepdims=True))
            return x / jnp.maximum(n, EPS)

        def _mamba(x, in_proj_w, conv_w, conv_b, x_proj_w, dt_proj_w, dt_proj_b, A_log, D_skip, out_proj_w):
            B, L, _ = x.shape
            xz = x @ in_proj_w.T
            u, res = jnp.split(xz, 2, axis=-1)
            xp = jnp.pad(u, ((0, 0), (D_CONV - 1, 0), (0, 0)))
            conv = conv_b + sum((xp[:, k:k + L, :] * conv_w[:, k] for k in range(D_CONV)))
            u = jax.nn.silu(conv)
            x_dbl = u @ x_proj_w.T
            dt, Bm, C = jnp.split(x_dbl, [DT_RANK, DT_RANK + D_STATE], axis=-1)
            delta = jax.nn.softplus(dt @ dt_proj_w.T + dt_proj_b)
            A = -jnp.exp(A_log)

            def step(h, t):
                delta_t, B_t, C_t, u_t = t
                dA = jnp.exp(delta_t[..., None] * A)
                h = dA * h + delta_t[..., None] * B_t[:, None, :] * u_t[..., None]
                y = jnp.einsum('bdn,bn->bd', h, C_t)
                return (h, y)
            xs = (jnp.swapaxes(delta, 0, 1), jnp.swapaxes(Bm, 0, 1), jnp.swapaxes(C, 0, 1), jnp.swapaxes(u, 0, 1))
            h0 = jnp.zeros((B, D_INNER, D_STATE), x.dtype)
            _, ys = jax.lax.scan(step, h0, xs)
            y = jnp.swapaxes(ys, 0, 1) + u * D_skip
            y = y * jax.nn.silu(res)
            return y @ out_proj_w.T

        def _forward(input_tensor, in_proj_w, conv_w, conv_b, x_proj_w, dt_proj_w, dt_proj_b, A_log, D_skip, out_proj_w, ln0_g, ln0_b, q_w, q_b, k_w, k_b, w_g, proj_w, proj_b, fl_w, fl_b, lni_g, lni_b, ln1_g, ln1_b, d1_w, d1_b, d2_w, d2_b, ln2_g, ln2_b):
            m = _mamba(input_tensor, in_proj_w, conv_w, conv_b, x_proj_w, dt_proj_w, dt_proj_b, A_log, D_skip, out_proj_w)
            h = _layernorm(m + input_tensor, ln0_g, ln0_b)
            q = jax.nn.gelu(_l2norm(h @ q_w.T + q_b, -1), approximate=False)
            k = _l2norm(h @ k_w.T + k_b, -1)
            qw = q @ w_g * D_MODEL ** (-0.5)
            Aw = _l2norm(qw, 1)
            G = (Aw * q).sum(1)
            hs = G[:, None, :] * k @ proj_w.T + proj_b
            hs = hs * _layernorm(h, lni_g, lni_b) @ fl_w.T + fl_b
            h2 = _layernorm(hs + h, ln1_g, ln1_b)
            f = jax.nn.gelu(h2 @ d1_w.T + d1_b, approximate=False) @ d2_w.T + d2_b
            return _layernorm(f + h2, ln2_g, ln2_b)
        key = jax.random.key(seed)
        ks = iter(jax.random.split(key, 40))

        def p(shape, scale=0.02):
            return jax.random.normal(next(ks), shape, jnp.float32) * scale
        inp = {}
        inp['input_tensor'] = jax.random.normal(next(ks), (BATCH, SEQ, D_MODEL), jnp.float32)
        inp['in_proj_w'] = p((2 * D_INNER, D_MODEL))
        inp['conv_w'] = p((D_INNER, D_CONV), 0.1)
        inp['conv_b'] = jnp.zeros((D_INNER,), jnp.float32)
        inp['x_proj_w'] = p((DT_RANK + 2 * D_STATE, D_INNER))
        inp['dt_proj_w'] = p((D_INNER, DT_RANK), 0.1)
        inp['dt_proj_b'] = jnp.full((D_INNER,), -2.0, jnp.float32)
        inp['A_log'] = jnp.broadcast_to(jnp.log(jnp.arange(1, D_STATE + 1, dtype=jnp.float32)), (D_INNER, D_STATE)).copy()
        inp['D_skip'] = jnp.ones((D_INNER,), jnp.float32)
        inp['out_proj_w'] = p((D_MODEL, D_INNER))
        inp['ln0_g'] = jnp.ones((D_MODEL,), jnp.float32)
        inp['ln0_b'] = jnp.zeros((D_MODEL,), jnp.float32)
        inp['q_w'] = p((D_MODEL, D_MODEL))
        inp['q_b'] = jnp.zeros((D_MODEL,), jnp.float32)
        inp['k_w'] = p((D_MODEL, D_MODEL))
        inp['k_b'] = jnp.zeros((D_MODEL,), jnp.float32)
        inp['w_g'] = p((D_MODEL, 1), 1.0)
        inp['proj_w'] = p((D_MODEL, D_MODEL))
        inp['proj_b'] = jnp.zeros((D_MODEL,), jnp.float32)
        inp['fl_w'] = p((D_MODEL, D_MODEL))
        inp['fl_b'] = jnp.zeros((D_MODEL,), jnp.float32)
        inp['lni_g'] = jnp.ones((D_MODEL,), jnp.float32)
        inp['lni_b'] = jnp.zeros((D_MODEL,), jnp.float32)
        inp['ln1_g'] = jnp.ones((D_MODEL,), jnp.float32)
        inp['ln1_b'] = jnp.zeros((D_MODEL,), jnp.float32)
        inp['d1_w'] = p((4 * D_MODEL, D_MODEL))
        inp['d1_b'] = jnp.zeros((4 * D_MODEL,), jnp.float32)
        inp['d2_w'] = p((D_MODEL, 4 * D_MODEL))
        inp['d2_b'] = jnp.zeros((D_MODEL,), jnp.float32)
        inp['ln2_g'] = jnp.ones((D_MODEL,), jnp.float32)
        inp['ln2_b'] = jnp.zeros((D_MODEL,), jnp.float32)
        return inp
    _L0_attn_in = _L0_attn_setup()

    def _L0_ffn_setup():
        import jax, jax.numpy as jnp
        import numpy as np
        B, S, D, F, E, TOP_K = (4, 256, 128, 512, 8, 2)
        LN_EPS = 1e-05
        key = jax.random.key(seed)
        ks = jax.random.split(key, 4)
        sc = lambda fan_in: 1.0 / np.sqrt(fan_in)
        return {'x': jax.random.normal(ks[0], (B, S, D), jnp.float32), 'W1': jax.random.normal(ks[1], (E, D, F), jnp.float32) * sc(D), 'b1': jnp.zeros((E, F), jnp.float32), 'W2': jax.random.normal(ks[2], (E, F, D), jnp.float32) * sc(F), 'b2': jnp.zeros((E, D), jnp.float32), 'Wr': jax.random.normal(ks[3], (D, E), jnp.float32) * sc(D), 'br': jnp.zeros((E,), jnp.float32), 'gamma': jnp.ones((D,), jnp.float32), 'beta': jnp.zeros((D,), jnp.float32)}
    _L0_ffn_in = _L0_ffn_setup()

    def _L1_attn_setup():
        import jax, jax.numpy as jnp
        import numpy as np
        import math
        B, S, E = (2, 256, 128)
        H, DK, DV = (16, 64, 64)

        def _rope(q, k):
            D = q.shape[-1]
            theta = 10000.0 ** (jnp.arange(0, D, 2, dtype=jnp.float32) / D)
            pos = jnp.arange(q.shape[-2], dtype=jnp.float32)
            freqs = pos[:, None] * (1.0 / theta)[None, :]
            emb = jnp.concatenate([freqs, freqs], axis=-1)
            cos = jnp.cos(emb)[None, None]
            sin = jnp.sin(emb)[None, None]

            def rotate(x):
                x1 = x[..., ::2]
                x2 = x[..., 1::2]
                return jnp.stack([-x2, x1], axis=-1).reshape(x.shape)
            return (q * cos + rotate(q) * sin, k * cos + rotate(k) * sin)
        key = jax.random.key(seed)
        ks = jax.random.split(key, 9)
        sE = 1.0 / math.sqrt(E)
        sV = 1.0 / math.sqrt(H * DV)
        return {'x': jax.random.normal(ks[0], (B, S, E), dtype=jnp.float32), 'wq': jax.random.uniform(ks[1], (H * DK, E), jnp.float32, -sE, sE), 'bq': jax.random.uniform(ks[2], (H * DK,), jnp.float32, -sE, sE), 'wk': jax.random.uniform(ks[3], (H * DK, E), jnp.float32, -sE, sE), 'bk': jax.random.uniform(ks[4], (H * DK,), jnp.float32, -sE, sE), 'wv': jax.random.uniform(ks[5], (H * DV, E), jnp.float32, -sE, sE), 'bv': jax.random.uniform(ks[6], (H * DV,), jnp.float32, -sE, sE), 'wo': jax.random.uniform(ks[7], (E, H * DV), jnp.float32, -sV, sV), 'bo': jax.random.uniform(ks[8], (E,), jnp.float32, -sV, sV)}
    _L1_attn_in = _L1_attn_setup()

    def _L1_ffn_setup():
        import jax, jax.numpy as jnp
        import numpy as np
        B, T, D = (1, 128, 128)
        E, S, H = (8, 2, 512)
        key = jax.random.key(seed)
        kx, kg, k1, k2, k3 = jax.random.split(key, 5)
        X = jax.random.normal(kx, (B, T, D), jnp.float32)
        Wg = jax.random.normal(kg, (D, E), jnp.float32) * 0.02
        bg = jnp.zeros((E,), jnp.float32)
        W1 = jax.random.normal(k1, (E, D, H), jnp.float32) * 0.02
        W3 = jax.random.normal(k3, (E, D, H), jnp.float32) * 0.02
        W2 = jax.random.normal(k2, (E, H, D), jnp.float32) * 0.02
        return {'X': X, 'Wg': Wg, 'bg': bg, 'W1': W1, 'W2': W2, 'W3': W3}
    _L1_ffn_in = _L1_ffn_setup()
    _d = {'L0_attn_input_tensor': _L0_attn_in['input_tensor'], 'L0_attn_in_proj_w': _L0_attn_in['in_proj_w'], 'L0_attn_conv_w': _L0_attn_in['conv_w'], 'L0_attn_conv_b': _L0_attn_in['conv_b'], 'L0_attn_x_proj_w': _L0_attn_in['x_proj_w'], 'L0_attn_dt_proj_w': _L0_attn_in['dt_proj_w'], 'L0_attn_dt_proj_b': _L0_attn_in['dt_proj_b'], 'L0_attn_A_log': _L0_attn_in['A_log'], 'L0_attn_D_skip': _L0_attn_in['D_skip'], 'L0_attn_out_proj_w': _L0_attn_in['out_proj_w'], 'L0_attn_ln0_g': _L0_attn_in['ln0_g'], 'L0_attn_ln0_b': _L0_attn_in['ln0_b'], 'L0_attn_q_w': _L0_attn_in['q_w'], 'L0_attn_q_b': _L0_attn_in['q_b'], 'L0_attn_k_w': _L0_attn_in['k_w'], 'L0_attn_k_b': _L0_attn_in['k_b'], 'L0_attn_w_g': _L0_attn_in['w_g'], 'L0_attn_proj_w': _L0_attn_in['proj_w'], 'L0_attn_proj_b': _L0_attn_in['proj_b'], 'L0_attn_fl_w': _L0_attn_in['fl_w'], 'L0_attn_fl_b': _L0_attn_in['fl_b'], 'L0_attn_lni_g': _L0_attn_in['lni_g'], 'L0_attn_lni_b': _L0_attn_in['lni_b'], 'L0_attn_ln1_g': _L0_attn_in['ln1_g'], 'L0_attn_ln1_b': _L0_attn_in['ln1_b'], 'L0_attn_d1_w': _L0_attn_in['d1_w'], 'L0_attn_d1_b': _L0_attn_in['d1_b'], 'L0_attn_d2_w': _L0_attn_in['d2_w'], 'L0_attn_d2_b': _L0_attn_in['d2_b'], 'L0_attn_ln2_g': _L0_attn_in['ln2_g'], 'L0_attn_ln2_b': _L0_attn_in['ln2_b'], 'L0_ffn_W1': _L0_ffn_in['W1'], 'L0_ffn_b1': _L0_ffn_in['b1'], 'L0_ffn_W2': _L0_ffn_in['W2'], 'L0_ffn_b2': _L0_ffn_in['b2'], 'L0_ffn_Wr': _L0_ffn_in['Wr'], 'L0_ffn_br': _L0_ffn_in['br'], 'L0_ffn_gamma': _L0_ffn_in['gamma'], 'L0_ffn_beta': _L0_ffn_in['beta'], 'L1_attn_wq': _L1_attn_in['wq'], 'L1_attn_bq': _L1_attn_in['bq'], 'L1_attn_wk': _L1_attn_in['wk'], 'L1_attn_bk': _L1_attn_in['bk'], 'L1_attn_wv': _L1_attn_in['wv'], 'L1_attn_bv': _L1_attn_in['bv'], 'L1_attn_wo': _L1_attn_in['wo'], 'L1_attn_bo': _L1_attn_in['bo'], 'L1_ffn_Wg': _L1_ffn_in['Wg'], 'L1_ffn_bg': _L1_ffn_in['bg'], 'L1_ffn_W1': _L1_ffn_in['W1'], 'L1_ffn_W2': _L1_ffn_in['W2'], 'L1_ffn_W3': _L1_ffn_in['W3']}
    _x0 = _d['L0_attn_input_tensor']
    _d['L0_attn_input_tensor'] = jax.random.normal(jax.random.fold_in(jax.random.key(seed), 1), (8, 512, 128), dtype=_x0.dtype)
    del _x0
    return _d

def reference(L0_attn_input_tensor, L0_attn_in_proj_w, L0_attn_conv_w, L0_attn_conv_b, L0_attn_x_proj_w, L0_attn_dt_proj_w, L0_attn_dt_proj_b, L0_attn_A_log, L0_attn_D_skip, L0_attn_out_proj_w, L0_attn_ln0_g, L0_attn_ln0_b, L0_attn_q_w, L0_attn_q_b, L0_attn_k_w, L0_attn_k_b, L0_attn_w_g, L0_attn_proj_w, L0_attn_proj_b, L0_attn_fl_w, L0_attn_fl_b, L0_attn_lni_g, L0_attn_lni_b, L0_attn_ln1_g, L0_attn_ln1_b, L0_attn_d1_w, L0_attn_d1_b, L0_attn_d2_w, L0_attn_d2_b, L0_attn_ln2_g, L0_attn_ln2_b, L0_ffn_W1, L0_ffn_b1, L0_ffn_W2, L0_ffn_b2, L0_ffn_Wr, L0_ffn_br, L0_ffn_gamma, L0_ffn_beta, L1_attn_wq, L1_attn_bq, L1_attn_wk, L1_attn_bk, L1_attn_wv, L1_attn_bv, L1_attn_wo, L1_attn_bo, L1_ffn_Wg, L1_ffn_bg, L1_ffn_W1, L1_ffn_W2, L1_ffn_W3):

    def _L0_attn_ref(input_tensor, in_proj_w, conv_w, conv_b, x_proj_w, dt_proj_w, dt_proj_b, A_log, D_skip, out_proj_w, ln0_g, ln0_b, q_w, q_b, k_w, k_b, w_g, proj_w, proj_b, fl_w, fl_b, lni_g, lni_b, ln1_g, ln1_b, d1_w, d1_b, d2_w, d2_b, ln2_g, ln2_b):
        import jax, jax.numpy as jnp
        import numpy as np
        D_MODEL = 128
        D_STATE = 16
        D_CONV = 4
        EXPAND = 2
        D_INNER = EXPAND * D_MODEL
        DT_RANK = D_MODEL // 16
        BATCH, SEQ = (8, 256)
        EPS = 1e-12

        def _layernorm(x, g, b):
            m = x.mean(-1, keepdims=True)
            v = ((x - m) ** 2).mean(-1, keepdims=True)
            return (x - m) / jnp.sqrt(v + EPS) * g + b

        def _l2norm(x, axis):
            n = jnp.sqrt((x * x).sum(axis, keepdims=True))
            return x / jnp.maximum(n, EPS)

        def _mamba(x, in_proj_w, conv_w, conv_b, x_proj_w, dt_proj_w, dt_proj_b, A_log, D_skip, out_proj_w):
            B, L, _ = x.shape
            xz = x @ in_proj_w.T
            u, res = jnp.split(xz, 2, axis=-1)
            xp = jnp.pad(u, ((0, 0), (D_CONV - 1, 0), (0, 0)))
            conv = conv_b + sum((xp[:, k:k + L, :] * conv_w[:, k] for k in range(D_CONV)))
            u = jax.nn.silu(conv)
            x_dbl = u @ x_proj_w.T
            dt, Bm, C = jnp.split(x_dbl, [DT_RANK, DT_RANK + D_STATE], axis=-1)
            delta = jax.nn.softplus(dt @ dt_proj_w.T + dt_proj_b)
            A = -jnp.exp(A_log)

            def step(h, t):
                delta_t, B_t, C_t, u_t = t
                dA = jnp.exp(delta_t[..., None] * A)
                h = dA * h + delta_t[..., None] * B_t[:, None, :] * u_t[..., None]
                y = jnp.einsum('bdn,bn->bd', h, C_t)
                return (h, y)
            xs = (jnp.swapaxes(delta, 0, 1), jnp.swapaxes(Bm, 0, 1), jnp.swapaxes(C, 0, 1), jnp.swapaxes(u, 0, 1))
            h0 = jnp.zeros((B, D_INNER, D_STATE), x.dtype)
            _, ys = jax.lax.scan(step, h0, xs)
            y = jnp.swapaxes(ys, 0, 1) + u * D_skip
            y = y * jax.nn.silu(res)
            return y @ out_proj_w.T

        def _forward(input_tensor, in_proj_w, conv_w, conv_b, x_proj_w, dt_proj_w, dt_proj_b, A_log, D_skip, out_proj_w, ln0_g, ln0_b, q_w, q_b, k_w, k_b, w_g, proj_w, proj_b, fl_w, fl_b, lni_g, lni_b, ln1_g, ln1_b, d1_w, d1_b, d2_w, d2_b, ln2_g, ln2_b):
            m = _mamba(input_tensor, in_proj_w, conv_w, conv_b, x_proj_w, dt_proj_w, dt_proj_b, A_log, D_skip, out_proj_w)
            h = _layernorm(m + input_tensor, ln0_g, ln0_b)
            q = jax.nn.gelu(_l2norm(h @ q_w.T + q_b, -1), approximate=False)
            k = _l2norm(h @ k_w.T + k_b, -1)
            qw = q @ w_g * D_MODEL ** (-0.5)
            Aw = _l2norm(qw, 1)
            G = (Aw * q).sum(1)
            hs = G[:, None, :] * k @ proj_w.T + proj_b
            hs = hs * _layernorm(h, lni_g, lni_b) @ fl_w.T + fl_b
            h2 = _layernorm(hs + h, ln1_g, ln1_b)
            f = jax.nn.gelu(h2 @ d1_w.T + d1_b, approximate=False) @ d2_w.T + d2_b
            return _layernorm(f + h2, ln2_g, ln2_b)
        return _forward(input_tensor, in_proj_w, conv_w, conv_b, x_proj_w, dt_proj_w, dt_proj_b, A_log, D_skip, out_proj_w, ln0_g, ln0_b, q_w, q_b, k_w, k_b, w_g, proj_w, proj_b, fl_w, fl_b, lni_g, lni_b, ln1_g, ln1_b, d1_w, d1_b, d2_w, d2_b, ln2_g, ln2_b)

    def _L0_ffn_ref(x, W1, b1, W2, b2, Wr, br, gamma, beta):
        import jax, jax.numpy as jnp
        import numpy as np
        B, S, D, F, E, TOP_K = (4, 256, 128, 512, 8, 2)
        LN_EPS = 1e-05
        b, s, d = x.shape
        e = Wr.shape[1]
        rw = jax.nn.softmax(x.mean(axis=1) @ Wr + br, axis=-1)
        x_flat = x.reshape(-1, d)
        rw_tok = jnp.repeat(rw, s, axis=0)
        tk_w, tk_i = jax.lax.top_k(rw_tok, TOP_K)
        tk_w = jax.nn.softmax(tk_w, axis=-1)
        h = jax.nn.gelu(jnp.einsum('nd,edf->enf', x_flat, W1) + b1[:, None, :], approximate=False)
        expert_out = jnp.einsum('enf,efd->end', h, W2) + b2[:, None, :]
        onehot = jax.nn.one_hot(tk_i, e, dtype=x.dtype)
        cw = jnp.einsum('nk,nke->ne', tk_w, onehot)
        out = jnp.einsum('ne,end->nd', cw, expert_out).reshape(b, s, d)
        y = out + x
        mu = y.mean(axis=-1, keepdims=True)
        var = y.var(axis=-1, keepdims=True)
        return (y - mu) / jnp.sqrt(var + LN_EPS) * gamma + beta

    def _L1_attn_ref(x, wq, bq, wk, bk, wv, bv, wo, bo):
        import jax, jax.numpy as jnp
        import numpy as np
        import math
        B, S, E = (2, 256, 128)
        H, DK, DV = (16, 64, 64)

        def _rope(q, k):
            D = q.shape[-1]
            theta = 10000.0 ** (jnp.arange(0, D, 2, dtype=jnp.float32) / D)
            pos = jnp.arange(q.shape[-2], dtype=jnp.float32)
            freqs = pos[:, None] * (1.0 / theta)[None, :]
            emb = jnp.concatenate([freqs, freqs], axis=-1)
            cos = jnp.cos(emb)[None, None]
            sin = jnp.sin(emb)[None, None]

            def rotate(x):
                x1 = x[..., ::2]
                x2 = x[..., 1::2]
                return jnp.stack([-x2, x1], axis=-1).reshape(x.shape)
            return (q * cos + rotate(q) * sin, k * cos + rotate(k) * sin)
        Bx, Sx, Ex = x.shape
        q = (x @ wq.T + bq).reshape(Bx, Sx, H, DK).transpose(0, 2, 1, 3)
        k = (x @ wk.T + bk).reshape(Bx, Sx, H, DK).transpose(0, 2, 1, 3)
        v = (x @ wv.T + bv).reshape(Bx, Sx, H, DV).transpose(0, 2, 1, 3)
        q, k = _rope(q, k)
        scores = jnp.einsum('bhqd,bhkd->bhqk', q, k)
        causal = jnp.triu(jnp.ones((Sx, Sx), dtype=bool), k=1)
        scores = jnp.where(causal[None, None], -jnp.inf, scores)
        attn = jax.nn.softmax(scores / math.sqrt(DK), axis=-1)
        out = jnp.einsum('bhqk,bhkd->bhqd', attn, v)
        out = out.transpose(0, 2, 1, 3).reshape(Bx, Sx, H * DV)
        return out @ wo.T + bo

    def _L1_ffn_ref(X, Wg, bg, W1, W2, W3):
        import jax, jax.numpy as jnp
        import numpy as np
        B, T, D = (1, 128, 128)
        E, S, H = (8, 2, 512)
        logits = jnp.einsum('btd,de->bte', X, Wg) + bg
        topv, topi = jax.lax.top_k(logits, S)
        w = jax.nn.softmax(topv, axis=-1)
        xs = X[:, :, None, :] * w[..., None]
        out = X
        for e in range(E):
            h = jax.nn.silu(jnp.einsum('btsd,dh->btsh', xs, W1[e])) * jnp.einsum('btsd,dh->btsh', xs, W3[e])
            y = jnp.einsum('btsh,hd->btsd', h, W2[e])
            mask = (topi == e)[..., None]
            out = out + jnp.where(mask, y, 0.0).sum(axis=2)
        return out
    x = L0_attn_input_tensor
    xn = _layernorm(x, axis=-1)
    x = x + _L0_attn_ref(xn, L0_attn_in_proj_w, L0_attn_conv_w, L0_attn_conv_b, L0_attn_x_proj_w, L0_attn_dt_proj_w, L0_attn_dt_proj_b, L0_attn_A_log, L0_attn_D_skip, L0_attn_out_proj_w, L0_attn_ln0_g, L0_attn_ln0_b, L0_attn_q_w, L0_attn_q_b, L0_attn_k_w, L0_attn_k_b, L0_attn_w_g, L0_attn_proj_w, L0_attn_proj_b, L0_attn_fl_w, L0_attn_fl_b, L0_attn_lni_g, L0_attn_lni_b, L0_attn_ln1_g, L0_attn_ln1_b, L0_attn_d1_w, L0_attn_d1_b, L0_attn_d2_w, L0_attn_d2_b, L0_attn_ln2_g, L0_attn_ln2_b) + _L0_ffn_ref(xn, L0_ffn_W1, L0_ffn_b1, L0_ffn_W2, L0_ffn_b2, L0_ffn_Wr, L0_ffn_br, L0_ffn_gamma, L0_ffn_beta)
    xn = _layernorm(x, axis=-1)
    x = x + _L1_attn_ref(xn, L1_attn_wq, L1_attn_bq, L1_attn_wk, L1_attn_bk, L1_attn_wv, L1_attn_bv, L1_attn_wo, L1_attn_bo) + _L1_ffn_ref(xn, L1_ffn_Wg, L1_ffn_bg, L1_ffn_W1, L1_ffn_W2, L1_ffn_W3)
    return x

_drawn_inputs = setup_inputs


def setup_inputs(seed=0):
    import zlib

    import numpy as np

    out = dict(_drawn_inputs(seed))
    spreads = {'L0_attn_conv_b': (0.0, 0.8),
     'L0_attn_dt_proj_b': (-2.0, 0.6),
     'L0_attn_D_skip': (1.0, 0.6),
     'L0_attn_ln0_g': (1.0, 0.2),
     'L0_attn_ln0_b': (0.0, 0.295),
     'L0_attn_q_b': (0.0, 0.8),
     'L0_attn_k_b': (0.0, 2.0),
     'L0_attn_proj_b': (0.0, 0.8),
     'L0_attn_fl_b': (0.0, 0.1),
     'L0_attn_lni_g': (1.0, 0.6),
     'L0_attn_lni_b': (0.0, 0.8),
     'L0_attn_ln1_g': (1.0, 0.2),
     'L0_attn_ln1_b': (0.0, 0.1),
     'L0_attn_d1_b': (0.0, 0.8),
     'L0_attn_d2_b': (0.0, 0.1),
     'L0_attn_ln2_g': (1.0, 0.2),
     'L0_attn_ln2_b': (0.0, 0.1),
     'L0_ffn_b1': (0.0, 0.508),
     'L0_ffn_b2': (0.0, 0.416),
     'L0_ffn_br': (0.0, 0.1),
     'L0_ffn_gamma': (1.0, 0.2),
     'L0_ffn_beta': (0.0, 0.1),
     'L1_ffn_bg': (0.0, 0.8)}
    factors = {'L0_attn_in_proj_w': 8.0,
     'L0_attn_conv_w': 8.0,
     'L0_attn_x_proj_w': 8.0,
     'L0_attn_dt_proj_w': 8.0,
     'L0_attn_A_log': 8.0,
     'L0_attn_out_proj_w': 8.0,
     'L0_attn_q_w': 8.0,
     'L0_attn_k_w': 8.0,
     'L0_attn_w_g': 8.0,
     'L0_attn_proj_w': 8.0,
     'L0_attn_fl_w': 7.145,
     'L0_attn_d1_w': 3.026,
     'L0_attn_d2_w': 2.755,
     'L1_attn_wq': 8.0,
     'L1_attn_bq': 8.0,
     'L1_attn_wk': 8.0,
     'L1_attn_bk': 8.0,
     'L1_attn_wv': 4.256,
     'L1_attn_bv': 7.218,
     'L1_attn_wo': 3.858,
     'L1_attn_bo': 22.618,
     'L1_ffn_Wg': 8.0,
     'L1_ffn_W1': 8.0,
     'L1_ffn_W2': 8.0,
     'L1_ffn_W3': 8.0}
    for name, (base, spread) in spreads.items():
        noise = np.random.default_rng([zlib.crc32(name.encode()), seed]).standard_normal(out[name].shape)
        drawn = base * np.exp(spread * noise) if base else spread * noise
        out[name] = jnp.asarray(drawn.astype(out[name].dtype))
    for name, factor in factors.items():
        out[name] = (out[name] * factor).astype(out[name].dtype)
    return out
```

```python
from contextlib import ExitStack

import numpy as np
import concourse.bass as bass
from concourse import mybir

ALU = mybir.AluOpType
ACT = mybir.ActivationFunctionType
AX = mybir.AxisListType
F32 = mybir.dt.float32
BF16 = mybir.dt.bfloat16
U32 = mybir.dt.uint32

B, S, D = 8, 512, 128
P = 128
TILES = S // P
INNER = 2 * D
HALVES = INNER // P
STATES = 16
RANK = D // 16
TAPS = 4
PAD = TAPS - 1
HEADS, DK = 16, 64
PAIRS = HEADS // 2
EXPERTS = 8
HID = 4 * D
CHUNKS = HID // P
PICKS = 2
EXPERT_COLS = HID + CHUNKS * D + CHUNKS + 1
TINY = 1e-24
LIFT = float(2 ** 20)
MASKED = -1e30

VECS = {}
for _name, _n in (("conv_b", 2), ("dt_b", 2), ("D_skip", 2), ("ln0_g", 1), ("ln0_b", 1), ("q_b", 1), ("k_b", 1),
                  ("proj_b", 1), ("fl_b", 1), ("lni_g", 1), ("lni_b", 1), ("ln1_g", 1), ("ln1_b", 1),
                  ("d1_b", 4), ("d2_b", 1), ("ln2_g", 1), ("ln2_b", 1), ("gamma", 1), ("beta", 1),
                  ("bq", PAIRS), ("bq_swap", PAIRS), ("bk", PAIRS), ("bk_swap", PAIRS), ("bv", PAIRS), ("bo", 1),
                  ("w_g", 1)):
    VECS[_name] = (sum(n for _, n in VECS.values()), _n)
N_VECS = sum(n for _, n in VECS.values())

WEIGHTS = {}
for _name, _n in (("in_res", INNER), ("x_bc", HALVES * 96), ("x_dt", HALVES * RANK),
                  ("out_proj", HALVES * D), ("q", D), ("k", D), ("proj", D), ("fl", D), ("d1", HID),
                  ("d2", CHUNKS * D), ("router", EXPERTS), ("gate", EXPERTS),
                  ("wq", HEADS * DK), ("wq_swap", HEADS * DK), ("wk", HEADS * DK), ("wk_swap", HEADS * DK),
                  ("wv", HEADS * DK), ("wo", PAIRS * D)):
    WEIGHTS[_name] = (sum(n for _, n in WEIGHTS.values()), _n)
N_WEIGHTS = sum(n for _, n in WEIGHTS.values())


class Signal:

    def __init__(self, ctx, nc, name, per, unit=1):
        self.sem, self.per, self.unit = ctx.enter_context(nc.semaphore(name)), per, unit

    def at(self, b, k=None):
        k = self.per if k is None else k
        return b * (self.per * self.unit) + (self.per + k) * self.unit

    def head_start(self, engine):
        engine.sem_inc(self.sem, self.per * self.unit)


class Norm:

    def __init__(self, ctx, nc, name, x, ready, mean, var, eps, centred, square, rstd):
        self.name, self.x, self.ready, self.mean, self.var, self.eps = name, x, ready, mean, var, eps
        self.centred, self.square, self.rstd = centred, square, rstd
        self.s_mean = Signal(ctx, nc, f"{name}_mean", 1)
        self.s_centred = Signal(ctx, nc, f"{name}_centred", 1)
        self.s_square = Signal(ctx, nc, f"{name}_square", 1)
        self.s_var = Signal(ctx, nc, f"{name}_var", 1)
        self.s_rstd = Signal(ctx, nc, f"{name}_rstd", 2)


def build(nc, xT, weights, vecs, conv_rows, dt_w, a_log, moe_up, moe_gate, moe_down, experts,
          row_biases, cos, sin, identity, causal, row_of, in_u_w, outT):
    ctx = ExitStack()
    with ctx:
        def sb(name, shape, dt=F32):
            return ctx.enter_context(nc.sbuf_tensor(name, shape, dt))

        def signal(name, per=1, unit=1):
            return Signal(ctx, nc, name, per, unit)

        W = sb("W", [P, N_WEIGHTS])
        V_ = sb("V_", [P, N_VECS])

        def w(name, lo=0, n=P):
            at = WEIGHTS[name][0] + lo
            return W[:, at:at + n]

        def vec(name, k=0):
            at = VECS[name][0] + k
            return V_[:, at:at + 1]

        conv_w = sb("conv_w", [P, TAPS, INNER])
        dt_lhs = sb("dt_lhs", [RANK, INNER])
        a_neg = sb("a_neg", [P, HALVES, STATES])
        up_w = sb("up_w", [P, EXPERTS, HID])
        gate_w = sb("gate_w", [P, EXPERTS, HID])
        down_w = sb("down_w", [P, EXPERTS, CHUNKS, D])
        cos_t, sin_t = sb("cos_t", [P, S]), sb("sin_t", [P, S])
        ident = sb("ident", [P, P])
        ident_bf = sb("ident_bf", [P, P], BF16)
        causal_bf = sb("causal_bf", [P, P], BF16)
        row_of_sb = sb("row_of_sb", [96, 2 * STATES])
        pick = sb("pick", [96, 2 * STATES, P], BF16)
        row_bias = sb("row_bias", [P, 3 * EXPERTS])
        avg = sb("avg", [P, P])
        ones = sb("ones", [P, P])
        wg_cols = sb("wg_cols", [P, P])
        eps5, eps12 = sb("eps5", [P, 1]), sb("eps12", [P, 1])
        lift_back = sb("lift_back", [P, 1])

        X = sb("X", [P, S])
        XN = sb("XN", [P, PAD + S])
        xn = XN[:, PAD:PAD + S]
        US = sb("US", [P, HALVES, S])
        SR = sb("SR", [P, HALVES, S])
        DELTA = sb("DELTA", [P, HALVES, S])
        DU = sb("DU", [P, HALVES, S])
        DA = sb("DA", [P, 2, HALVES, S])
        D1 = sb("D1", [P, HALVES, S])
        HS = sb("HS", [P, HALVES, S])
        HC = sb("HC", [P, 2, HALVES, S])
        Y = sb("Y", [P, HALVES, S])
        S3 = sb("S3", [96, S], BF16)
        S3B = HC[0:96, 0, 0, :].bitcast(BF16)[:, 0:S]
        DT = HC[0:RANK, 0, 1, :]
        R1 = HC[0:96, 1, 1, :]
        causal_f = D1[:, 0, 0:P]
        in_u = Y[:, 0, 0:INNER]
        M0 = sb("M0", [P, S])
        XNB = sb("XNB", [P, S])
        X2 = sb("X2", [P, S])
        XN2 = sb("XN2", [P, S])
        EW = sb("EW", [P, PICKS, EXPERT_COLS])
        REG = sb("REG", [P, 20, S])

        def reg(k):
            return REG[:, k, :]

        CX, CSQ, CR, H, QP, KP, Q, RK, LNI = (reg(k) for k in range(9))
        GK, M1, H2 = reg(9), reg(10), reg(11)
        F1 = REG[:, 12:16, :]
        L0A, XB, YF, TMP = (reg(k) for k in range(16, 20))
        M2, CR2 = QP, YF
        V = REG[:, 0:8, :].rearrange("p (t h) s -> p t (h s)", t=TILES)
        ROT, ROT2 = reg(8), reg(9)
        QK = REG[:, 10:14, :].rearrange("p (r a) s -> p r a s", r=2)
        PR = REG[:, 14:16, :]
        PT = REG[:, 16:18, :]
        O, OT = reg(18), reg(19)
        XS = REG[:, 8:10, :]
        SL = REG[:, 10:12, :]
        HH = REG[:, 12:15, :]
        small = sb("small", [P, 64])
        gate_s = reg(16)[:, 0:TILES * 64].rearrange("p (t c) -> p t c", t=TILES)
        gate_i = sb("gate_i", [P, TILES, 8], U32)
        pick_i = sb("pick_i", [1, 8], U32)
        maxes = sb("maxes", [P, 2, 8])
        rows = sb("rows", [P, 2, 8])

        FB, FC, FM = (ctx.enter_context(nc.psum_tensor(n, [P, S], F32)) for n in ("FB", "FC", "FM"))
        G = [ctx.enter_context(nc.psum_tensor(f"G{k}", [P, S], F32)) for k in range(5)]

        N_CONST = 15
        n_loads = 16 * N_CONST
        dve_passed, pool_passed, sp_passed = (ctx.enter_context(nc.semaphore(f"{e}_passed")) for e in ("dve", "pool", "sp"))
        s_const = ctx.enter_context(nc.semaphore("const_loaded"))
        s_made = ctx.enter_context(nc.semaphore("const_made"))
        s_alog = ctx.enter_context(nc.semaphore("alog_exp"))
        s_made_pool = ctx.enter_context(nc.semaphore("const_made_pool"))
        x_in = signal("x_in", 1, 16)
        xb_in = signal("xb_in", 1, 16)
        ew_in = [signal(f"ew_in{k}", 1, 16) for k in range(PICKS)]
        out_st = signal("out_st", 1, 16)
        xn_done = signal("xn_done")
        u_mm = signal("u_mm", 2)
        r_mm = signal("r_mm", 2)
        u_silu = signal("u_silu", 2)
        r_silu = signal("r_silu", 2)
        dt_mm, bc_mm = signal("dt_mm"), signal("bc_mm")
        dt_copy = signal("dt_copy")
        bc_split = signal("bc_split", 6)
        dp_mm = signal("dp_mm", 2)
        soft = signal("soft", 4)
        relu_d = signal("relu_d", 2)
        delta_d = signal("delta_d")
        wide_d = signal("wide_d", 3)
        du_d = signal("du_d")
        skip_y = signal("skip_y", 2)
        b_mm, c_mm = signal("b_mm", STATES), signal("c_mm", STATES)
        da_exp = signal("da_exp", 2 * STATES)
        db_mul = signal("db_mul", STATES)
        scan_d = signal("scan_d", STATES)
        hc_mul = signal("hc_mul", STATES)
        y_add = signal("y_add", STATES)
        y_gate = signal("y_gate")
        m_mm = signal("m_mm")
        m0_d = signal("m0_d")
        xnb_d = signal("xnb_d")

        h_d = signal("h_d", 2)
        q_mm, k_mm = signal("q_mm"), signal("k_mm")
        qp_d, qsq_d, kp_d, ksq_d = signal("qp_d"), signal("qsq_d"), signal("kp_d"), signal("ksq_d")
        qss_mm, kss_mm = signal("qss_mm"), signal("kss_mm")
        qk_cl = signal("qk_cl", 2)
        qk_rs = signal("qk_rs", 4)
        qn_d = signal("qn_d")
        q_gelu = signal("q_gelu")
        qw_mm = signal("qw_mm")
        gu_d = signal("gu_d", 3)
        g_act = signal("g_act", 3)
        gk_d = signal("gk_d")
        proj_mm = signal("proj_mm")
        lni_d = signal("lni_d", 2)
        hsm_d = signal("hsm_d")
        fl_mm = signal("fl_mm")
        m1_d = signal("m1_d")
        h2_d = signal("h2_d", 2)
        d1_mm, d1_gelu = signal("d1_mm", CHUNKS), signal("d1_gelu", CHUNKS)
        d2_mm = signal("d2_mm")
        m2_d = signal("m2_d")
        l0a_d = signal("l0a_d", 3)

        xm_d = signal("xm_d", 2)
        lg_mm = signal("lg_mm")
        rt_d = signal("rt_d", 10)
        rt_act = signal("rt_act", 2)
        wb_mm = signal("wb_mm")
        wb_d = signal("wb_d")
        idx_rd = signal("idx_rd")
        e1_mm, e1_gelu = signal("e1_mm", PICKS * CHUNKS), signal("e1_gelu", PICKS * CHUNKS)
        e2_mm = signal("e2_mm", PICKS)
        yf_d = signal("yf_d", 5)
        l0f_d = signal("l0f_d", 2)
        x2_d = signal("x2_d")
        xn2_d = signal("xn2_d")

        v_mm, v_copy = signal("v_mm", 2 * TILES), signal("v_copy", 2 * TILES)
        pj_mm = signal("pj_mm", 4 * PAIRS)
        rot_d = signal("rot_d", 4 * PAIRS)
        rope_d = signal("rope_d", 2 * PAIRS)
        sc_mm = signal("sc_mm", HEADS * TILES)
        mx_d = signal("mx_d", HEADS * TILES)
        nm_d = signal("nm_d", HEADS * TILES)
        p_exp = signal("p_exp", HEADS * TILES)
        pt_mm = signal("pt_mm", HEADS * TILES)
        pt_copy = signal("pt_copy", HEADS * TILES)
        pv_mm = signal("pv_mm", HEADS * TILES)
        rec_d = signal("rec_d", PAIRS)
        o_d = signal("o_d", PAIRS)
        ot_mm = signal("ot_mm", PAIRS)
        ot_copy = signal("ot_copy", PAIRS)
        wo_mm = signal("wo_mm", PAIRS)
        x3_d = signal("x3_d", 2)

        gl_mm = signal("gl_mm")
        gt_d = signal("gt_d", 13)
        gt_act = signal("gt_act")
        wt_mm = signal("wt_mm", EXPERTS)
        xs_d = signal("xs_d", EXPERTS)
        ug_mm = signal("ug_mm", EXPERTS * CHUNKS)
        sl_act = signal("sl_act", EXPERTS * CHUNKS)
        hh_d = signal("hh_d", EXPERTS * CHUNKS)
        dn_mm = signal("dn_mm", EXPERTS * CHUNKS)
        out_d = signal("out_d")

        n1 = Norm(ctx, nc, "norm_x", X[:, :], lambda b: (x_in, b, 1), FM, FM, eps5, HC[:, 0, 0, :], HC[:, 0, 1, :], HC[:, 1, 0, :])
        n0 = Norm(ctx, nc, "norm_0", M0[:, :], lambda b: (m0_d, b, 1), G[0], G[1], eps12, CX, CSQ, CR)
        ni = Norm(ctx, nc, "norm_i", H, lambda b: (h_d, b, 2), G[2], G[3], eps12, CX, CSQ, CR2)
        n_1 = Norm(ctx, nc, "norm_1", M1, lambda b: (m1_d, b, 1), G[2], G[3], eps12, CX, CSQ, CR)
        n_2 = Norm(ctx, nc, "norm_2", M2, lambda b: (m2_d, b, 1), G[0], G[1], eps12, CX, CSQ, CR)
        nf = Norm(ctx, nc, "norm_f", YF, lambda b: (yf_d, b, 5), G[0], G[1], eps5, CX, CSQ, CR)
        nx = Norm(ctx, nc, "norm_x2", X2[:, :], lambda b: (x2_d, b, 1), G[0], G[1], eps5, CX, CSQ, CR)
        norms = (n1, n0, ni, n_1, n_2, nf, nx)

        by_pe = [u_mm, r_mm, dt_mm, bc_mm, dp_mm, b_mm, c_mm, m_mm, q_mm, k_mm, qss_mm, kss_mm, qw_mm, proj_mm, fl_mm,
                 d1_mm, d2_mm, lg_mm, wb_mm, e1_mm, e2_mm, v_mm, pj_mm, sc_mm, pt_mm, pv_mm, ot_mm, wo_mm, gl_mm,
                 wt_mm, ug_mm, dn_mm] + [s for n in norms for s in (n.s_mean, n.s_var)]
        by_act = [u_silu, r_silu, soft, da_exp, qp_d, qsq_d, kp_d, ksq_d, qk_rs, q_gelu, g_act, d1_gelu, rt_act,
                  e1_gelu, v_copy, p_exp, pt_copy, ot_copy, gt_act, sl_act] + [s for n in norms for s in (n.s_square, n.s_rstd)]
        by_dve = [xn_done, dt_copy, bc_split, relu_d, delta_d, wide_d, db_mul, scan_d, hc_mul, m0_d, h_d, qk_cl, qn_d, gu_d,
                  gk_d, lni_d, hsm_d, m1_d, h2_d, m2_d, l0a_d, xm_d, rt_d, wb_d, yf_d, l0f_d, x2_d, xn2_d, rot_d,
                  mx_d, nm_d, rec_d, o_d, x3_d, gt_d, xs_d, hh_d, out_d] + [n.s_centred for n in norms]
        by_pool = [du_d, skip_y, y_add, y_gate, xnb_d, rope_d]
        by_sp = [x_in, xb_in, *ew_in, out_st, idx_rd]

        block = ctx.enter_context(nc.Block())

        def laps(eng, front, back, lap):
            front(0)
            with eng.Fori(0, B - 1) as b:
                lap(b)
            back(B - 1)

        @block.sync
        def _(sp):
            for s in by_sp:
                s.head_start(sp)
            for dst, src in ((W[:, :], weights), (V_[:, :], vecs), (dt_lhs[:, :], dt_w), (a_neg[:, :, :], a_log),
                             (ident[:, :], identity), (causal_f, causal), (in_u, in_u_w), (row_of_sb[:, :], row_of),
                             (row_bias[:, :], row_biases.partition_broadcast(P)),
                             (conv_w[:, :, :], conv_rows.partition_broadcast(P)),
                             (cos_t[:, :], cos), (sin_t[:, :], sin), (up_w[:, :, :], moe_up),
                             (gate_w[:, :, :], moe_gate), (down_w[:, :, :, :], moe_down)):
                sp.dma_start(dst, src).then_inc(s_const, 16)

            def load_x(b):
                sp.wait_ge(n1.s_centred.sem, n1.s_centred.at(b - 1))
                sp.dma_start(X[:, :], xT[b]).then_inc(x_in.sem, 16)

            def back(b):
                sp.wait_ge(out_d.sem, out_d.at(b - 1))
                sp.dma_start(XB, xT[b]).then_inc(xb_in.sem, 16)
                for k in range(PICKS):
                    sp.wait_ge(e2_mm.sem, e2_mm.at(b - 1, k + 1))
                    sp.sem_inc(sp_passed, 1)
                    sp.wait_ge(e1_gelu.sem, e1_gelu.at(b - 1, CHUNKS * (k + 1)))
                    sp.wait_ge(rt_d.sem, rt_d.at(b, 7))
                    sp.sem_inc(sp_passed, 1)
                    e = sp.value_load(pick_i[0:1, k:k + 1], min_val=0, max_val=EXPERTS - 1)
                    sp.dma_start(EW[:, k, :], experts[bass.ds(e, 1), :, :].rearrange("a p c -> (a p) c")).then_inc(ew_in[k].sem, 16)
                sp.sem_inc(idx_rd.sem, 1)
                sp.wait_ge(out_d.sem, out_d.at(b))
                sp.dma_start(outT[b], TMP).then_inc(out_st.sem, 16)

            load_x(0)
            with sp.Fori(0, B - 1) as b:
                load_x(b + 1)
                back(b)
            back(B - 1)
            sp.wait_ge(out_st.sem, out_st.at(B - 1))

        @block.tensor
        def _(pe):
            for s in by_pe:
                s.head_start(pe)
            pe.wait_ge(s_const, n_loads)
            pe.wait_ge(s_made, 15)
            pe.wait_ge(s_made_pool, 1)

            def mean(n, b):
                sig, at, k = n.ready(b)
                pe.wait_ge(sig.sem, sig.at(at, k))
                pe.matmul(n.mean[:, :], avg[:, :], n.x, start=True, stop=True).then_inc(n.s_mean.sem, 1)

            def var(n, b):
                pe.wait_ge(n.s_square.sem, n.s_square.at(b))
                pe.matmul(n.var[:, :], avg[:, :], n.square, start=True, stop=True).then_inc(n.s_var.sem, 1)

            def front_start(b):
                pe.wait_ge(m0_d.sem, m0_d.at(b - 1))
                mean(n1, b)
                var(n1, b)
                pe.wait_ge(xn_done.sem, xn_done.at(b))
                pe.wait_ge(hc_mul.sem, hc_mul.at(b - 1))
                for h, bank in ((0, FB), (1, FC)):
                    for tap in range(TAPS):
                        mm = pe.matmul(bank[:, :], conv_w[:, tap, h * P:(h + 1) * P], XN[:, tap:tap + S],
                                       start=tap == 0, stop=tap == TAPS - 1)
                    mm.then_inc(u_mm.sem, 1)
                pe.wait_ge(n1.s_rstd.sem, n1.s_rstd.at(b))
                for h in range(HALVES):
                    if h:
                        pe.wait_ge(r_silu.sem, r_silu.at(b, h))
                    pe.matmul(FM[:, :], w("in_res", h * P), xn, start=True, stop=True).then_inc(r_mm.sem, 1)
                pe.wait_ge(u_silu.sem, u_silu.at(b))
                for h in range(HALVES):
                    mm = pe.matmul(FB[0:96, :], w("x_bc", h * 96, 96), US[:, h, :], start=h == 0, stop=h == 1)
                mm.then_inc(bc_mm.sem, 1)
                pe.wait_ge(r_silu.sem, r_silu.at(b))
                for h in range(HALVES):
                    mm = pe.matmul(FM[0:RANK, :], w("x_dt", h * RANK, RANK), US[:, h, :], start=h == 0, stop=h == 1)
                mm.then_inc(dt_mm.sem, 1)
                pe.wait_ge(dt_copy.sem, dt_copy.at(b))
                pe.matmul(FC[:, :], dt_lhs[:, 0:P], DT, start=True, stop=True).then_inc(dp_mm.sem, 1)
                pe.matmul(FM[:, :], dt_lhs[:, P:INNER], DT, start=True, stop=True).then_inc(dp_mm.sem, 1)
                pe.wait_ge(bc_split.sem, bc_split.at(b))
                pe.wait_ge(soft.sem, soft.at(b, 2))
                pe.wait_ge(relu_d.sem, relu_d.at(b))

            def front_step(b, n):
                if n:
                    pe.wait_ge(db_mul.sem, db_mul.at(b, n))
                pe.matmul(FB[:, :], pick[:, n, :], S3[:, :], start=True, stop=True).then_inc(b_mm.sem, 1)
                if n:
                    pe.wait_ge(hc_mul.sem, hc_mul.at(b, n))
                pe.matmul(FC[:, :], pick[:, STATES + n, :], S3[:, :], start=True, stop=True).then_inc(c_mm.sem, 1)

            def front_end(b):
                pe.wait_ge(y_gate.sem, y_gate.at(b))
                for h in range(HALVES):
                    mm = pe.matmul(FM[:, :], w("out_proj", h * D), Y[:, h, :], start=h == 0, stop=h == 1)
                mm.then_inc(m_mm.sem, 1)

            def back_start(b):
                pe.wait_ge(out_d.sem, out_d.at(b - 1))
                mean(n0, b)
                var(n0, b)
                pe.wait_ge(xm_d.sem, xm_d.at(b))
                pe.matmul(G[4][0:1, 0:EXPERTS], small[:, 0:1], w("router", 0, EXPERTS), start=True, stop=True).then_inc(lg_mm.sem, 1)
                pe.wait_ge(h_d.sem, h_d.at(b))
                pe.matmul(G[0][:, :], w("q"), H, start=True, stop=True).then_inc(q_mm.sem, 1)
                pe.matmul(G[1][:, :], w("k"), H, start=True, stop=True).then_inc(k_mm.sem, 1)
                mean(ni, b)
                pe.wait_ge(rt_d.sem, rt_d.at(b, 10))
                pe.matmul(G[4][:, 16:18], ones[0:1, :], small[0:1, 40:42], start=True, stop=True).then_inc(wb_mm.sem, 1)
                pe.wait_ge(qsq_d.sem, qsq_d.at(b))
                pe.matmul(G[3][:, :], ones[:, :], TMP, start=True, stop=True).then_inc(qss_mm.sem, 1)
                pe.wait_ge(qk_cl.sem, qk_cl.at(b, 1))
                pe.wait_ge(ksq_d.sem, ksq_d.at(b))
                pe.matmul(G[3][:, :], ones[:, :], M1, start=True, stop=True).then_inc(kss_mm.sem, 1)
                pe.wait_ge(qk_cl.sem, qk_cl.at(b, 2))
                var(ni, b)
                pe.wait_ge(q_gelu.sem, q_gelu.at(b))
                pe.wait_ge(wb_d.sem, wb_d.at(b))
                pe.matmul(G[4][:, :], wg_cols[:, :], Q, start=True, stop=True).then_inc(qw_mm.sem, 1)
                pe.wait_ge(gk_d.sem, gk_d.at(b))
                pe.matmul(G[0][:, :], w("proj"), GK, start=True, stop=True).then_inc(proj_mm.sem, 1)
                pe.wait_ge(hsm_d.sem, hsm_d.at(b))
                pe.matmul(G[1][:, :], w("fl"), TMP, start=True, stop=True).then_inc(fl_mm.sem, 1)
                mean(n_1, b)
                var(n_1, b)
                pe.wait_ge(h2_d.sem, h2_d.at(b))
                for c in range(CHUNKS):
                    pe.matmul(G[c][:, :], w("d1", c * P), H2, start=True, stop=True).then_inc(d1_mm.sem, 1)
                for c in range(CHUNKS):
                    pe.wait_ge(d1_gelu.sem, d1_gelu.at(b, c + 1))
                    mm = pe.matmul(G[4][:, :], w("d2", c * D), F1[:, c, :], start=c == 0, stop=c == CHUNKS - 1)
                mm.then_inc(d2_mm.sem, 1)
                mean(n_2, b)
                var(n_2, b)

            def back_experts(b):
                pe.wait_ge(n_2.s_rstd.sem, n_2.s_rstd.at(b))
                for k in range(PICKS):
                    pe.wait_ge(ew_in[k].sem, ew_in[k].at(b))
                    for c in range(CHUNKS):
                        if k:
                            pe.wait_ge(e1_gelu.sem, e1_gelu.at(b, c + 1))
                        pe.matmul(G[c][:, :], EW[:, k, c * P:(c + 1) * P], XNB[:, :], start=True, stop=True).then_inc(e1_mm.sem, 1)
                    if k:
                        pe.wait_ge(yf_d.sem, yf_d.at(b, 4))
                    for c in range(CHUNKS):
                        pe.wait_ge(e1_gelu.sem, e1_gelu.at(b, k * CHUNKS + c + 1))
                        mm = pe.matmul(G[4][:, :], EW[:, k, HID + c * D:HID + (c + 1) * D], F1[:, c, :],
                                       start=c == 0, stop=c == CHUNKS - 1)
                    mm.then_inc(e2_mm.sem, 1)
                mean(nf, b)
                var(nf, b)
                mean(nx, b)
                var(nx, b)

            def back_values(b):
                pe.wait_ge(xn2_d.sem, xn2_d.at(b))
                for t in range(TILES):
                    for c in range(2):
                        n = 2 * t + c
                        if n >= 2:
                            pe.wait_ge(v_copy.sem, v_copy.at(b, n - 1))
                        pe.matmul(G[n % 2][:, :], XN2[:, t * P:(t + 1) * P], w("wv", c * S, S), start=True, stop=True).then_inc(v_mm.sem, 1)

            def back_pair(b, j):
                for a, name in enumerate(("wq", "wk")):
                    n = 4 * j + 2 * a
                    if a == 0:
                        if j == 0:
                            pe.wait_ge(v_copy.sem, v_copy.at(b))
                        else:
                            pe.wait_ge(p_exp.sem, p_exp.at(b, 8 * j))
                    else:
                        pe.wait_ge(rot_d.sem, rot_d.at(b, n))
                    pe.matmul(G[0][:, :], w(name, j * P), XN2[:, :], start=True, stop=True).then_inc(pj_mm.sem, 1)
                    pe.matmul(G[1][:, :], w(name + "_swap", j * P), XN2[:, :], start=True, stop=True).then_inc(pj_mm.sem, 1)
                pe.wait_ge(rot_d.sem, rot_d.at(b, 4 * j + 4))
                pe.wait_ge(rope_d.sem, rope_d.at(b, 2 * j + 2))

                def score(i):
                    n, t, lo = 8 * j + i, i % TILES, (i // TILES) * DK
                    width = (t + 1) * P
                    if i >= 2:
                        pe.wait_ge(p_exp.sem, p_exp.at(b, n - 1))
                    pe.matmul(G[i % 2][:, 0:width], QK[lo:lo + DK, j % 2, 0, t * P:(t + 1) * P],
                              QK[lo:lo + DK, j % 2, 1, 0:width], start=True, stop=False)
                    pe.matmul(G[i % 2][:, t * P:width], ident_bf[:, :], causal_bf[:, :], start=False, stop=True).then_inc(sc_mm.sem, 1)

                def turn(i):
                    n, t = 8 * j + i, i % TILES
                    pe.wait_ge(p_exp.sem, p_exp.at(b, n + 1))
                    if n:
                        pe.wait_ge(pt_copy.sem, pt_copy.at(b, n))
                    if j and i == 0:
                        pe.wait_ge(ot_copy.sem, ot_copy.at(b, j))
                    for c in range(t + 1):
                        mm = pe.transpose(G[2][:, c * P:(c + 1) * P], PR[:, n % 2, c * P:(c + 1) * P], ident[:, :])
                    mm.then_inc(pt_mm.sem, 1)

                def values(i):
                    n, t, h = 8 * j + i, i % TILES, i // TILES
                    pe.wait_ge(pt_copy.sem, pt_copy.at(b, n + 1))
                    if i == 0 and j:
                        pe.wait_ge(o_d.sem, o_d.at(b, j))
                    col = t * P + h * DK
                    for c in range(t + 1):
                        mm = pe.matmul(G[3][:, col:col + DK], PT[:, n % 2, c * P:(c + 1) * P],
                                       V[:, c, j * P + h * DK:j * P + (h + 1) * DK], start=c == 0, stop=c == t)
                    mm.then_inc(pv_mm.sem, 1)

                n_sc = 2 * TILES
                score(0)
                score(1)
                for i in range(n_sc):
                    turn(i)
                    if i + 2 < n_sc:
                        score(i + 2)
                    values(i)
                pe.wait_ge(o_d.sem, o_d.at(b, j + 1))
                pe.wait_ge(pt_copy.sem, pt_copy.at(b, 8 * j + 8))
                for t in range(TILES):
                    mm = pe.transpose(G[2][:, t * P:(t + 1) * P], O[:, t * P:(t + 1) * P], ident[:, :])
                mm.then_inc(ot_mm.sem, 1)
                pe.wait_ge(ot_copy.sem, ot_copy.at(b, j + 1))
                pe.matmul(G[4][:, :], w("wo", j * D), OT, start=j == 0, stop=j == PAIRS - 1,
                          skip_group_check=True).then_inc(wo_mm.sem, 1)

            def back_gate(b):
                for t in range(TILES):
                    mm = pe.matmul(G[3][:, t * 8:(t + 1) * 8], XN2[:, t * P:(t + 1) * P], w("gate", 0, EXPERTS), start=True, stop=True)
                mm.then_inc(gl_mm.sem, 1)
                pe.wait_ge(x3_d.sem, x3_d.at(b))
                pe.wait_ge(gt_d.sem, gt_d.at(b))

            def back_expert(b, e):
                first = 5 * e
                def ring(k):
                    return 2 * (k % 2)
                g = ring(first)
                if e:
                    pe.wait_ge(hh_d.sem, hh_d.at(b, 4 * e - 1))
                for t in range(TILES):
                    mm = pe.matmul(G[g][:, t * P:(t + 1) * P], gate_s[:, t, 48 + e:49 + e].to_broadcast([P, P]), ident[:, :],
                                   start=True, stop=True)
                mm.then_inc(wt_mm.sem, 1)
                if e:
                    down(b, e - 1, 3)
                pe.wait_ge(xs_d.sem, xs_d.at(b, e + 1))
                for c in range(CHUNKS):
                    n = e * CHUNKS + c
                    g = ring(first + 1 + c)
                    if n >= 1 and c == 0:
                        pe.wait_ge(hh_d.sem, hh_d.at(b, n))
                    if c >= 2:
                        pe.wait_ge(hh_d.sem, hh_d.at(b, n - 1))
                    pe.matmul(G[g][:, :], up_w[:, e, c * P:(c + 1) * P], XS[:, e % 2, :], start=True, stop=True)
                    pe.matmul(G[g + 1][:, :], gate_w[:, e, c * P:(c + 1) * P], XS[:, e % 2, :], start=True, stop=True).then_inc(ug_mm.sem, 1)
                    if c:
                        down(b, e, c - 1)

            def down(b, e, c):
                n = e * CHUNKS + c
                pe.wait_ge(hh_d.sem, hh_d.at(b, n + 1))
                pe.matmul(G[4][:, :], down_w[:, e, c, :], HH[:, n % 3, :], start=n == 0, stop=n == EXPERTS * CHUNKS - 1,
                          skip_group_check=True).then_inc(dn_mm.sem, 1)

            def front(b):
                front_start(b)
                for n in range(STATES):
                    front_step(b, n)
                front_end(b)

            def lap(b, f=None):
                back_start(b)
                if f is not None:
                    front_start(f)
                back_experts(b)
                back_values(b)
                for j in range(PAIRS):
                    if f is not None:
                        front_step(f, j)
                    back_pair(b, j)
                back_gate(b)
                for e in range(EXPERTS):
                    if f is not None:
                        front_step(f, PAIRS + e)
                    back_expert(b, e)
                down(b, EXPERTS - 1, CHUNKS - 1)
                if f is not None:
                    front_end(f)

            laps(pe, front, lap, lambda b: lap(b, b + 1))

        @block.scalar
        def _(act):
            for s in by_act:
                s.head_start(act)
            act.wait_ge(s_const, n_loads)
            act.activation(a_neg[:, :, :], a_neg[:, :, :], ACT.Exp).then_inc(s_alog, 1)
            act.wait_ge(s_made, 15)

            def square(n, b):
                act.wait_ge(n.s_centred.sem, n.s_centred.at(b))
                act.activation(n.square, n.centred, ACT.Square).then_inc(n.s_square.sem, 1)

            def rstd(n, b):
                act.wait_ge(n.s_var.sem, n.s_var.at(b))
                act.activation(n.rstd, n.var[:, :], ACT.Ln, bias=n.eps[:, 0:1]).then_inc(n.s_rstd.sem, 1)
                act.wait_ge(n.s_rstd.sem, n.s_rstd.at(b, 1))
                act.activation(n.rstd, n.rstd, ACT.Exp, scale=-0.5).then_inc(n.s_rstd.sem, 1)

            def front_start(b):
                act.wait_ge(y_add.sem, y_add.at(b - 1))
                square(n1, b)
                rstd(n1, b)
                act.wait_ge(y_gate.sem, y_gate.at(b - 1))
                for h, bank in ((0, FB), (1, FC)):
                    act.wait_ge(u_mm.sem, u_mm.at(b, h + 1))
                    act.activation(US[:, h, :], bank[:, :], ACT.Silu, bias=vec("conv_b", h)).then_inc(u_silu.sem, 1)
                for h in range(HALVES):
                    act.wait_ge(r_mm.sem, r_mm.at(b, h + 1))
                    act.activation(SR[:, h, :], FM[:, :], ACT.Silu).then_inc(r_silu.sem, 1)
                act.wait_ge(scan_d.sem, scan_d.at(b - 1))
                for h, bank in ((0, FC), (1, FM)):
                    act.wait_ge(dp_mm.sem, dp_mm.at(b, h + 1))
                    act.activation(D1[:, h, :], bank[:, :], ACT.Abs, bias=vec("dt_b", h)).then_inc(soft.sem, 1)
                act.wait_ge(soft.sem, soft.at(b, 2))
                act.activation(D1[:, :, :], D1[:, :, :], ACT.Exp, scale=-1.0).then_inc(soft.sem, 1)
                act.wait_ge(wide_d.sem, wide_d.at(b, 2))
                act.activation(DELTA[:, :, :], DELTA[:, :, :], ACT.Ln).then_inc(soft.sem, 1)
                act.wait_ge(delta_d.sem, delta_d.at(b))

            def front_step(b, n):
                if n >= 2:
                    act.wait_ge(scan_d.sem, scan_d.at(b, n - 1))
                for h in range(HALVES):
                    act.activation(DA[:, n % 2, h, 1:S], DELTA[:, h, 1:S], ACT.Exp,
                                   scale=a_neg[:, h, n:n + 1]).then_inc(da_exp.sem, 1)

            def front_end(b):
                pass

            def back_start(b):
                act.wait_ge(out_d.sem, out_d.at(b - 1))
                square(n0, b)
                rstd(n0, b)
                act.wait_ge(q_mm.sem, q_mm.at(b))
                act.activation(QP, G[0][:, :], ACT.Identity, bias=vec("q_b")).then_inc(qp_d.sem, 1)
                act.activation(TMP, G[0][:, :], ACT.Square, bias=vec("q_b")).then_inc(qsq_d.sem, 1)
                act.wait_ge(k_mm.sem, k_mm.at(b))
                act.activation(KP, G[1][:, :], ACT.Identity, bias=vec("k_b")).then_inc(kp_d.sem, 1)
                act.activation(M1, G[1][:, :], ACT.Square, bias=vec("k_b")).then_inc(ksq_d.sem, 1)
                act.wait_ge(rt_d.sem, rt_d.at(b, 3))
                act.activation(small[0:1, 16:24], small[0:1, 8:16], ACT.Exp, bias=small[0:1, 5:6], accum_out=small[0:1, 6:7]).then_inc(rt_act.sem, 1)
                act.wait_ge(rt_d.sem, rt_d.at(b, 8))
                act.activation(small[0:1, 38:40], small[0:1, 24:26], ACT.Exp, bias=small[0:1, 7:8], accum_out=small[0:1, 36:37]).then_inc(rt_act.sem, 1)
                for k, buf in ((0, CR), (1, RK)):
                    act.wait_ge(qk_cl.sem, qk_cl.at(b, k + 1))
                    act.activation(buf, buf, ACT.Ln, scale=LIFT).then_inc(qk_rs.sem, 1)
                    act.wait_ge(qk_rs.sem, qk_rs.at(b, 2 * k + 1))
                    act.activation(buf, buf, ACT.Exp, scale=-0.5, bias=lift_back[:, 0:1]).then_inc(qk_rs.sem, 1)
                square(ni, b)
                rstd(ni, b)
                act.wait_ge(qn_d.sem, qn_d.at(b))
                act.activation(Q, CR, ACT.Gelu).then_inc(q_gelu.sem, 1)
                act.wait_ge(gu_d.sem, gu_d.at(b, 1))
                act.activation(GK, G[4][:, :], ACT.Square, accum_out=small[:, 43:44]).then_inc(g_act.sem, 1)
                act.wait_ge(gu_d.sem, gu_d.at(b, 2))
                act.activation(small[:, 45:46], small[:, 44:45], ACT.Ln, scale=LIFT).then_inc(g_act.sem, 1)
                act.wait_ge(g_act.sem, g_act.at(b, 2))
                act.activation(small[:, 46:47], small[:, 45:46], ACT.Exp, scale=-0.5, bias=lift_back[:, 0:1]).then_inc(g_act.sem, 1)
                square(n_1, b)
                rstd(n_1, b)
                for c in range(CHUNKS):
                    act.wait_ge(d1_mm.sem, d1_mm.at(b, c + 1))
                    act.activation(F1[:, c, :], G[c][:, :], ACT.Gelu, bias=vec("d1_b", c)).then_inc(d1_gelu.sem, 1)
                square(n_2, b)
                rstd(n_2, b)

            def back_experts(b):
                for k in range(PICKS):
                    for c in range(CHUNKS):
                        act.wait_ge(e1_mm.sem, e1_mm.at(b, k * CHUNKS + c + 1))
                        if k == 0:
                            act.wait_ge(d2_mm.sem, d2_mm.at(b))
                        elif c == 0:
                            act.wait_ge(e2_mm.sem, e2_mm.at(b, 1))
                        at = HID + CHUNKS * D + c
                        act.activation(F1[:, c, :], G[c][:, :], ACT.Gelu, bias=EW[:, k, at:at + 1]).then_inc(e1_gelu.sem, 1)
                square(nf, b)
                rstd(nf, b)
                square(nx, b)
                rstd(nx, b)

            def back_values(b):
                act.wait_ge(xn2_d.sem, xn2_d.at(b))
                for n in range(2 * TILES):
                    act.wait_ge(v_mm.sem, v_mm.at(b, n + 1))
                    act.activation(V[:, n // 2, (n % 2) * S:(n % 2 + 1) * S], G[n % 2][:, :], ACT.Copy).then_inc(v_copy.sem, 1)

            def back_pair(b, j):
                def weights_of(i):
                    n, t = 8 * j + i, i % TILES
                    width = (t + 1) * P
                    act.wait_ge(nm_d.sem, nm_d.at(b, n + 1))
                    if n >= 2:
                        act.wait_ge(pt_mm.sem, pt_mm.at(b, n - 1))
                    act.activation(PR[:, n % 2, 0:width], G[i % 2][:, 0:width], ACT.Exp, scale=DK ** -0.5,
                                   bias=maxes[:, 1, i:i + 1], accum_out=rows[:, 0, i:i + 1]).then_inc(p_exp.sem, 1)

                def copy_turned(i):
                    n, t = 8 * j + i, i % TILES
                    width = (t + 1) * P
                    act.wait_ge(pt_mm.sem, pt_mm.at(b, n + 1))
                    if n >= 2:
                        act.wait_ge(pv_mm.sem, pv_mm.at(b, n - 1))
                    act.activation(PT[:, n % 2, 0:width], G[2][:, 0:width], ACT.Copy).then_inc(pt_copy.sem, 1)

                n_sc = 2 * TILES
                if j:
                    act.wait_ge(rec_d.sem, rec_d.at(b, j))
                weights_of(0)
                for i in range(n_sc):
                    if i + 1 < n_sc:
                        weights_of(i + 1)
                    copy_turned(i)
                act.wait_ge(ot_mm.sem, ot_mm.at(b, j + 1))
                if j:
                    act.wait_ge(wo_mm.sem, wo_mm.at(b, j))
                act.activation(OT, G[2][:, :], ACT.Identity, bias=vec("bv", j)).then_inc(ot_copy.sem, 1)

            def back_gate(b):
                act.wait_ge(gt_d.sem, gt_d.at(b, 7))
                act.activation(gate_s[:, :, 26:27], gate_s[:, :, 25:26], ACT.Exp).then_inc(gt_act.sem, 1)

            def back_expert(b, e):
                for c in range(CHUNKS):
                    n = e * CHUNKS + c
                    act.wait_ge(ug_mm.sem, ug_mm.at(b, n + 1))
                    if n >= 2:
                        act.wait_ge(hh_d.sem, hh_d.at(b, n - 1))
                    g = 2 * ((5 * e + 1 + c) % 2)
                    act.activation(SL[:, n % 2, :], G[g][:, :], ACT.Silu).then_inc(sl_act.sem, 1)

            def front(b):
                front_start(b)
                for n in range(STATES):
                    front_step(b, n)
                front_end(b)

            def lap(b, f=None):
                back_start(b)
                if f is not None:
                    front_start(f)
                back_experts(b)
                back_values(b)
                for j in range(PAIRS):
                    if f is not None:
                        front_step(f, j)
                    back_pair(b, j)
                back_gate(b)
                for e in range(EXPERTS):
                    if f is not None:
                        front_step(f, PAIRS + e)
                    back_expert(b, e)

            laps(act, front, lap, lambda b: lap(b, b + 1))

        @block.vector
        def _(dve):
            for s in by_dve:
                s.head_start(dve)
            dve.wait_ge(s_const, n_loads)
            dve.memset(avg[:, :], 1.0 / P).then_inc(s_made, 1)
            dve.memset(ones[:, :], 1.0).then_inc(s_made, 1)
            dve.memset(eps5[:, :], 1e-5).then_inc(s_made, 1)
            dve.memset(eps12[:, :], 1e-12).then_inc(s_made, 1)
            dve.memset(lift_back[:, :], 0.5 * float(np.log(LIFT))).then_inc(s_made, 1)
            dve.memset(XN[:, 0:PAD], 0.0).then_inc(s_made, 1)
            dve.memset(DA[:, :, :, 0:1], 0.0).then_inc(s_made, 1)
            dve.tensor_copy(ident_bf[:, :], ident[:, :]).then_inc(s_made, 1)
            dve.tensor_copy(causal_bf[:, :], causal_f).then_inc(s_made, 1)
            dve.tensor_copy(pick[:, :, :], row_of_sb[:, :].unsqueeze(2).to_broadcast([96, 2 * STATES, P])).then_inc(s_made, 1)
            dve.tensor_copy(wg_cols[:, :], vec("w_g").to_broadcast([P, P])).then_inc(s_made, 1)
            for tap in range(TAPS - 1):
                dve.tensor_tensor(conv_w[:, tap, :], conv_w[:, tap, :], in_u, ALU.mult).then_inc(s_made, 1)
            dve.wait_ge(s_alog, 1)
            dve.tensor_scalar(a_neg[:, :, :], a_neg[:, :, :], -1.0, None, ALU.mult).then_inc(s_made, 1)

            def centre(n, b):
                dve.wait_ge(n.s_mean.sem, n.s_mean.at(b))
                dve.tensor_tensor(n.centred, n.x, n.mean[:, :], ALU.subtract).then_inc(n.s_centred.sem, 1)

            def affine(n, b, out, gain, bias, done):
                dve.wait_ge(n.s_rstd.sem, n.s_rstd.at(b))
                dve.scalar_tensor_tensor(out, n.centred, gain, n.rstd, ALU.mult, ALU.mult).then_inc(done.sem, 1)
                dve.wait_ge(done.sem, done.at(b, 1))
                dve.tensor_scalar(out, out, bias, None, ALU.add).then_inc(done.sem, 1)

            def front_start(b):
                dve.wait_ge(y_add.sem, y_add.at(b - 1))
                centre(n1, b)
                dve.wait_ge(n1.s_rstd.sem, n1.s_rstd.at(b))
                dve.wait_ge(xnb_d.sem, xnb_d.at(b - 1))
                dve.tensor_tensor(xn, n1.centred, n1.rstd, ALU.mult).then_inc(xn_done.sem, 1)
                dve.wait_ge(c_mm.sem, c_mm.at(b - 1))
                dve.wait_ge(bc_mm.sem, bc_mm.at(b))
                dve.tensor_copy(S3[:, :], FB[0:96, :]).then_inc(bc_split.sem, 1)
                dve.wait_ge(bc_split.sem, bc_split.at(b, 1))
                dve.tensor_tensor(R1, FB[0:96, :], S3[:, :], ALU.subtract).then_inc(bc_split.sem, 1)
                dve.wait_ge(dt_mm.sem, dt_mm.at(b))
                dve.tensor_copy(DT, FM[0:RANK, :]).then_inc(dt_copy.sem, 1)
                dve.wait_ge(bc_split.sem, bc_split.at(b, 2))
                dve.tensor_copy(S3B, R1).then_inc(bc_split.sem, 1)
                dve.wait_ge(bc_split.sem, bc_split.at(b, 3))
                dve.tensor_tensor(R1[64:96, :], R1[64:96, :], S3B[64:96, :], ALU.subtract).then_inc(bc_split.sem, 1)
                dve.tensor_copy(S3[32:64, :], S3B[32:64, :]).then_inc(bc_split.sem, 1)
                dve.wait_ge(bc_split.sem, bc_split.at(b, 5))
                dve.tensor_copy(S3[64:96, :], R1[64:96, :]).then_inc(bc_split.sem, 1)
                for h, bank in ((0, FC), (1, FM)):
                    dve.wait_ge(soft.sem, soft.at(b, h + 1))
                    dve.tensor_scalar(HS[:, h, :], bank[:, :], vec("dt_b", h), 0.0, ALU.add, ALU.max).then_inc(relu_d.sem, 1)
                dve.wait_ge(soft.sem, soft.at(b, 3))
                dve.tensor_scalar(DELTA[:, :, :], D1[:, :, :], 1.0, None, ALU.add).then_inc(wide_d.sem, 1)
                dve.wait_ge(wide_d.sem, wide_d.at(b, 1))
                dve.scalar_tensor_tensor(D1[:, :, :], DELTA[:, :, :], -1.0, D1[:, :, :], ALU.add, ALU.subtract).then_inc(wide_d.sem, 1)
                dve.wait_ge(wide_d.sem, wide_d.at(b, 2))
                dve.wait_ge(relu_d.sem, relu_d.at(b))
                dve.tensor_tensor(HS[:, :, :], HS[:, :, :], D1[:, :, :], ALU.subtract).then_inc(wide_d.sem, 1)
                dve.wait_ge(soft.sem, soft.at(b, 4))
                dve.wait_ge(wide_d.sem, wide_d.at(b, 3))
                dve.tensor_tensor(DELTA[:, :, :], HS[:, :, :], DELTA[:, :, :], ALU.add).then_inc(delta_d.sem, 1)

            def front_step(b, n):
                dve.wait_ge(b_mm.sem, b_mm.at(b, n + 1))
                if n == 0:
                    dve.wait_ge(du_d.sem, du_d.at(b))
                    dve.wait_ge(delta_d.sem, delta_d.at(b))
                dve.tensor_tensor(D1[:, :, :], DU[:, :, :], FB[:, :].unsqueeze(1).to_broadcast([P, HALVES, S]), ALU.mult).then_inc(db_mul.sem, 1)
                dve.wait_ge(db_mul.sem, db_mul.at(b, n + 1))
                dve.wait_ge(da_exp.sem, da_exp.at(b, 2 * n + 2))
                dve.tensor_tensor_scan(HS[:, :, :].rearrange("p h s -> p (h s)"), DA[:, n % 2, :, :].rearrange("p h s -> p (h s)"),
                                       D1[:, :, :].rearrange("p h s -> p (h s)"), 0.0, ALU.mult, ALU.add).then_inc(scan_d.sem, 1)
                dve.wait_ge(scan_d.sem, scan_d.at(b, n + 1))
                dve.wait_ge(c_mm.sem, c_mm.at(b, n + 1))
                if n >= 2:
                    dve.wait_ge(y_add.sem, y_add.at(b, n - 1))
                dve.tensor_tensor(HC[:, n % 2, :, :], HS[:, :, :], FC[:, :].unsqueeze(1).to_broadcast([P, HALVES, S]), ALU.mult).then_inc(hc_mul.sem, 1)

            def front_end(b):
                dve.wait_ge(m_mm.sem, m_mm.at(b))
                dve.tensor_tensor(M0[:, :], xn, FM[:, :], ALU.add).then_inc(m0_d.sem, 1)

            def back_start(b):
                dve.wait_ge(out_st.sem, out_st.at(b - 1))
                centre(n0, b)
                dve.wait_ge(xnb_d.sem, xnb_d.at(b))
                dve.tensor_reduce(small[:, 1:2], XNB[:, :], AX.X, ALU.add).then_inc(xm_d.sem, 1)
                dve.wait_ge(xm_d.sem, xm_d.at(b, 1))
                dve.tensor_scalar(small[:, 0:1], small[:, 1:2], 1.0 / S, None, ALU.mult).then_inc(xm_d.sem, 1)
                affine(n0, b, H, vec("ln0_g"), vec("ln0_b"), h_d)

                dve.wait_ge(lg_mm.sem, lg_mm.at(b))
                dve.tensor_tensor(small[0:1, 8:16], G[4][0:1, 0:8], row_bias[0:1, 0:8], ALU.add).then_inc(rt_d.sem, 1)
                dve.wait_ge(rt_d.sem, rt_d.at(b, 1))
                dve.sem_inc(dve_passed, 1)
                dve.tensor_reduce(small[0:1, 4:5], small[0:1, 8:16], AX.X, ALU.max).then_inc(rt_d.sem, 1)
                dve.wait_ge(rt_d.sem, rt_d.at(b, 2))
                dve.sem_inc(dve_passed, 1)
                dve.tensor_scalar(small[0:1, 5:6], small[0:1, 4:5], -1.0, None, ALU.mult).then_inc(rt_d.sem, 1)
                dve.wait_ge(rt_d.sem, rt_d.at(b, 3))
                dve.sem_inc(dve_passed, 1)
                dve.wait_ge(rt_act.sem, rt_act.at(b, 1))
                dve.reciprocal(small[0:1, 3:4], small[0:1, 6:7]).then_inc(rt_d.sem, 1)
                dve.wait_ge(rt_d.sem, rt_d.at(b, 4))
                dve.sem_inc(dve_passed, 1)
                dve.tensor_scalar(small[0:1, 48:56], small[0:1, 16:24], small[0:1, 3:4], None, ALU.mult).then_inc(rt_d.sem, 1)
                dve.wait_ge(rt_d.sem, rt_d.at(b, 5))
                dve.sem_inc(dve_passed, 1)
                dve.wait_ge(idx_rd.sem, idx_rd.at(b - 1))
                dve.sem_inc(dve_passed, 1)
                dve.max(small[0:1, 24:32], small[0:1, 48:56]).then_inc(rt_d.sem, 1)
                dve.wait_ge(rt_d.sem, rt_d.at(b, 6))
                dve.sem_inc(dve_passed, 1)
                dve.max_index(pick_i[0:1, :], small[0:1, 24:32], small[0:1, 48:56]).then_inc(rt_d.sem, 1)
                dve.wait_ge(rt_d.sem, rt_d.at(b, 7))
                dve.sem_inc(dve_passed, 1)
                dve.tensor_scalar(small[0:1, 7:8], small[0:1, 24:25], -1.0, None, ALU.mult).then_inc(rt_d.sem, 1)
                dve.wait_ge(rt_d.sem, rt_d.at(b, 8))
                dve.sem_inc(dve_passed, 1)
                dve.wait_ge(rt_act.sem, rt_act.at(b, 2))
                dve.reciprocal(small[0:1, 37:38], small[0:1, 36:37]).then_inc(rt_d.sem, 1)
                dve.wait_ge(rt_d.sem, rt_d.at(b, 9))
                dve.sem_inc(dve_passed, 1)
                dve.tensor_scalar(small[0:1, 40:42], small[0:1, 38:40], small[0:1, 37:38], None, ALU.mult).then_inc(rt_d.sem, 1)
                dve.wait_ge(rt_d.sem, rt_d.at(b, 10))
                dve.sem_inc(dve_passed, 1)
                dve.wait_ge(wb_mm.sem, wb_mm.at(b))
                dve.tensor_copy(small[:, 32:34], G[4][:, 16:18]).then_inc(wb_d.sem, 1)
                dve.wait_ge(qss_mm.sem, qss_mm.at(b))
                dve.tensor_scalar(CR, G[3][:, :], TINY, None, ALU.max).then_inc(qk_cl.sem, 1)
                dve.wait_ge(kss_mm.sem, kss_mm.at(b))
                dve.tensor_scalar(RK, G[3][:, :], TINY, None, ALU.max).then_inc(qk_cl.sem, 1)
                centre(ni, b)
                dve.wait_ge(qk_rs.sem, qk_rs.at(b, 2))
                dve.wait_ge(qp_d.sem, qp_d.at(b))
                dve.tensor_tensor(CR, CR, QP, ALU.mult).then_inc(qn_d.sem, 1)
                affine(ni, b, LNI, vec("lni_g"), vec("lni_b"), lni_d)
                dve.wait_ge(qw_mm.sem, qw_mm.at(b))
                dve.tensor_tensor_reduce(out=YF, in0=Q, in1=G[4][:, :], scale=1.0, scalar=0.0, op0=ALU.mult, op1=ALU.add,
                                         accum_out=small[:, 42:43]).then_inc(gu_d.sem, 1)
                dve.wait_ge(g_act.sem, g_act.at(b, 1))
                dve.tensor_scalar(small[:, 44:45], small[:, 43:44], 1.0 / D, TINY, ALU.mult, ALU.max).then_inc(gu_d.sem, 1)
                dve.wait_ge(g_act.sem, g_act.at(b, 3))
                dve.wait_ge(gu_d.sem, gu_d.at(b, 1))
                dve.tensor_scalar(small[:, 47:48], small[:, 42:43], float(D) ** -0.5, small[:, 46:47], ALU.mult, ALU.mult).then_inc(gu_d.sem, 1)
                dve.wait_ge(gu_d.sem, gu_d.at(b, 3))
                dve.wait_ge(kp_d.sem, kp_d.at(b))
                dve.wait_ge(qk_rs.sem, qk_rs.at(b, 4))
                dve.scalar_tensor_tensor(GK, KP, small[:, 47:48], RK, ALU.mult, ALU.mult).then_inc(gk_d.sem, 1)
                dve.wait_ge(proj_mm.sem, proj_mm.at(b))
                dve.wait_ge(lni_d.sem, lni_d.at(b))
                dve.scalar_tensor_tensor(TMP, G[0][:, :], vec("proj_b"), LNI, ALU.add, ALU.mult).then_inc(hsm_d.sem, 1)
                dve.wait_ge(fl_mm.sem, fl_mm.at(b))
                dve.scalar_tensor_tensor(M1, G[1][:, :], vec("fl_b"), H, ALU.add, ALU.add).then_inc(m1_d.sem, 1)
                centre(n_1, b)
                affine(n_1, b, H2, vec("ln1_g"), vec("ln1_b"), h2_d)
                dve.wait_ge(d2_mm.sem, d2_mm.at(b))
                dve.scalar_tensor_tensor(M2, G[4][:, :], vec("d2_b"), H2, ALU.add, ALU.add).then_inc(m2_d.sem, 1)
                centre(n_2, b)
                affine(n_2, b, L0A, vec("ln2_g"), vec("ln2_b"), l0a_d)
                dve.wait_ge(xb_in.sem, xb_in.at(b))
                dve.wait_ge(l0a_d.sem, l0a_d.at(b, 2))
                dve.tensor_tensor(L0A, L0A, XB, ALU.add).then_inc(l0a_d.sem, 1)

            def back_experts(b):
                w0, w1 = small[:, 32:33], small[:, 33:34]
                at = EXPERT_COLS - 1
                dve.wait_ge(wb_d.sem, wb_d.at(b))
                for k in range(PICKS):
                    dve.wait_ge(ew_in[k].sem, ew_in[k].at(b))
                dve.tensor_scalar(small[:, 34:35], EW[:, 0, at:at + 1], w0, None, ALU.mult).then_inc(yf_d.sem, 1)
                dve.wait_ge(yf_d.sem, yf_d.at(b, 1))
                dve.scalar_tensor_tensor(small[:, 35:36], EW[:, 1, at:at + 1], w1, small[:, 34:35], ALU.mult, ALU.add).then_inc(yf_d.sem, 1)
                dve.wait_ge(yf_d.sem, yf_d.at(b, 2))
                dve.tensor_scalar(YF, XNB[:, :], small[:, 35:36], None, ALU.add).then_inc(yf_d.sem, 1)
                for k, wk in ((0, w0), (1, w1)):
                    dve.wait_ge(e2_mm.sem, e2_mm.at(b, k + 1))
                    dve.wait_ge(yf_d.sem, yf_d.at(b, 3 + k))
                    dve.scalar_tensor_tensor(YF, G[4][:, :], wk, YF, ALU.mult, ALU.add).then_inc(yf_d.sem, 1)
                centre(nf, b)
                affine(nf, b, YF, vec("gamma"), vec("beta"), l0f_d)
                dve.wait_ge(l0f_d.sem, l0f_d.at(b))
                dve.tensor_tensor(X2[:, :], YF, L0A, ALU.add).then_inc(x2_d.sem, 1)
                centre(nx, b)
                dve.wait_ge(nx.s_rstd.sem, nx.s_rstd.at(b))
                dve.tensor_tensor(XN2[:, :], nx.centred, nx.rstd, ALU.mult).then_inc(xn2_d.sem, 1)

            def back_values(b):
                pass

            def back_pair(b, j):
                for a, name in enumerate(("bq", "bk")):
                    n = 4 * j + 2 * a
                    if n:
                        dve.wait_ge(rope_d.sem, rope_d.at(b, n // 2))
                    dve.wait_ge(pj_mm.sem, pj_mm.at(b, n + 1))
                    dve.scalar_tensor_tensor(ROT, G[0][:, :], vec(name, j), cos_t[:, :], ALU.add, ALU.mult).then_inc(rot_d.sem, 1)
                    dve.wait_ge(pj_mm.sem, pj_mm.at(b, n + 2))
                    dve.scalar_tensor_tensor(ROT2, G[1][:, :], vec(name + "_swap", j), sin_t[:, :], ALU.add, ALU.mult).then_inc(rot_d.sem, 1)
                if j:
                    dve.wait_ge(p_exp.sem, p_exp.at(b, 8 * j))
                for i in range(2 * TILES):
                    n, width = 8 * j + i, (i % TILES + 1) * P
                    dve.wait_ge(sc_mm.sem, sc_mm.at(b, n + 1))
                    dve.tensor_reduce(maxes[:, 0, i:i + 1], G[i % 2][:, 0:width], AX.X, ALU.max).then_inc(mx_d.sem, 1)
                    dve.wait_ge(mx_d.sem, mx_d.at(b, n + 1))
                    dve.tensor_scalar(maxes[:, 1, i:i + 1], maxes[:, 0, i:i + 1], -DK ** -0.5, None, ALU.mult).then_inc(nm_d.sem, 1)
                dve.wait_ge(p_exp.sem, p_exp.at(b, 8 * j + 8))
                dve.reciprocal(rows[:, 1, :], rows[:, 0, :]).then_inc(rec_d.sem, 1)
                dve.wait_ge(rec_d.sem, rec_d.at(b, j + 1))
                dve.wait_ge(pv_mm.sem, pv_mm.at(b, 8 * j + 8))
                if j:
                    dve.wait_ge(ot_mm.sem, ot_mm.at(b, j))
                dve.tensor_tensor(O.rearrange("p (t h d) -> p t h d", t=TILES, h=2),
                                  G[3][:, :].rearrange("p (t h d) -> p t h d", t=TILES, h=2),
                                  rows[:, 1, :].rearrange("p (h t) -> p t h", h=2).unsqueeze(3).to_broadcast([P, TILES, 2, DK]),
                                  ALU.mult).then_inc(o_d.sem, 1)

            def back_gate(b):

                gs = gate_s
                dve.wait_ge(gl_mm.sem, gl_mm.at(b))
                dve.tensor_tensor(gs[:, :, 0:8], G[3][:, 0:32].rearrange("p (t e) -> p t e", e=8),
                                        row_bias[:, 8:16].unsqueeze(1).to_broadcast([P, TILES, 8]), ALU.add).then_inc(gt_d.sem, 1)
                dve.wait_ge(gt_d.sem, gt_d.at(b, 1))
                dve.sem_inc(dve_passed, 1)
                for t in range(TILES):
                    dve.max(gs[:, t, 8:16], gs[:, t, 0:8]).then_inc(gt_d.sem, 1)
                dve.wait_ge(gt_d.sem, gt_d.at(b, 5))
                dve.sem_inc(dve_passed, 1)
                for t in range(TILES):
                    ins = dve.max_index(gate_i[:, t, :], gs[:, t, 8:16], gs[:, t, 0:8])
                ins.then_inc(gt_d.sem, 1)
                dve.wait_ge(gt_d.sem, gt_d.at(b, 6))
                dve.sem_inc(dve_passed, 1)
                dve.tensor_tensor(gs[:, :, 25:26], gs[:, :, 9:10], gs[:, :, 8:9], ALU.subtract).then_inc(gt_d.sem, 1)
                dve.wait_ge(gt_d.sem, gt_d.at(b, 7))
                dve.sem_inc(dve_passed, 1)
                dve.tensor_copy(gs[:, :, 16:24], gate_i[:, :, :]).then_inc(gt_d.sem, 1)
                dve.wait_ge(gt_d.sem, gt_d.at(b, 8))
                dve.sem_inc(dve_passed, 1)
                dve.wait_ge(gt_act.sem, gt_act.at(b))
                dve.tensor_scalar(gs[:, :, 24:25], gs[:, :, 26:27], 1.0, None, ALU.add).then_inc(gt_d.sem, 1)
                dve.wait_ge(gt_d.sem, gt_d.at(b, 9))
                dve.sem_inc(dve_passed, 1)
                dve.reciprocal(gs[:, :, 27:28], gs[:, :, 24:25]).then_inc(gt_d.sem, 1)
                dve.wait_ge(gt_d.sem, gt_d.at(b, 10))
                dve.sem_inc(dve_passed, 1)
                dve.tensor_tensor(gs[:, :, 28:29], gs[:, :, 27:28], gs[:, :, 26:27], ALU.mult).then_inc(gt_d.sem, 1)
                dve.wait_ge(gt_d.sem, gt_d.at(b, 11))
                dve.sem_inc(dve_passed, 1)
                numbers = row_bias[:, 16:24]
                for t in range(TILES):
                    dve.tensor_scalar(gs[:, t, 32:40], numbers, gs[:, t, 16:17], gs[:, t, 27:28], ALU.is_equal, ALU.mult)
                    ins = dve.tensor_scalar(gs[:, t, 40:48], numbers, gs[:, t, 17:18], gs[:, t, 28:29], ALU.is_equal, ALU.mult)
                ins.then_inc(gt_d.sem, 1)
                dve.wait_ge(gt_d.sem, gt_d.at(b, 12))
                dve.sem_inc(dve_passed, 1)
                dve.tensor_tensor(gs[:, :, 48:56], gs[:, :, 32:40], gs[:, :, 40:48], ALU.add).then_inc(gt_d.sem, 1)
                dve.wait_ge(gt_d.sem, gt_d.at(b, 13))
                dve.sem_inc(dve_passed, 1)
                dve.wait_ge(wo_mm.sem, wo_mm.at(b))
                dve.scalar_tensor_tensor(X2[:, :], G[4][:, :], vec("bo"), X2[:, :], ALU.add, ALU.add).then_inc(x3_d.sem, 1)
                dve.wait_ge(x3_d.sem, x3_d.at(b, 1))
                dve.tensor_tensor(X2[:, :], X2[:, :], XN2[:, :], ALU.add).then_inc(x3_d.sem, 1)

            def back_expert(b, e):
                dve.wait_ge(wt_mm.sem, wt_mm.at(b, e + 1))
                g = 2 * ((5 * e) % 2)
                if e >= 2:
                    dve.wait_ge(ug_mm.sem, ug_mm.at(b, CHUNKS * (e - 1)))
                dve.tensor_tensor(XS[:, e % 2, :], XN2[:, :], G[g][:, :], ALU.mult).then_inc(xs_d.sem, 1)
                for c in range(CHUNKS):
                    n = e * CHUNKS + c
                    dve.wait_ge(sl_act.sem, sl_act.at(b, n + 1))
                    dve.wait_ge(ug_mm.sem, ug_mm.at(b, n + 1))
                    if n >= 3:
                        dve.wait_ge(dn_mm.sem, dn_mm.at(b, n - 2))
                    g = 2 * ((5 * e + 1 + c) % 2) + 1
                    dve.tensor_tensor(HH[:, n % 3, :], SL[:, n % 2, :], G[g][:, :], ALU.mult).then_inc(hh_d.sem, 1)

            def back_end(b):
                dve.wait_ge(dn_mm.sem, dn_mm.at(b))
                dve.wait_ge(x3_d.sem, x3_d.at(b))
                dve.tensor_tensor(TMP, X2[:, :], G[4][:, :], ALU.add).then_inc(out_d.sem, 1)

            def front(b):
                front_start(b)
                for n in range(STATES):
                    front_step(b, n)
                front_end(b)

            def lap(b, f=None):
                back_start(b)
                if f is not None:
                    front_start(f)
                back_experts(b)
                back_values(b)
                for j in range(PAIRS):
                    if f is not None:
                        front_step(f, j)
                    back_pair(b, j)
                back_gate(b)
                for e in range(EXPERTS):
                    if f is not None:
                        front_step(f, PAIRS + e)
                    back_expert(b, e)
                back_end(b)
                if f is not None:
                    front_end(f)

            laps(dve, front, lap, lambda b: lap(b, b + 1))

        @block.gpsimd
        def _(pool):
            for s in by_pool:
                s.head_start(pool)
            pool.wait_ge(s_const, n_loads)
            pool.tensor_tensor(conv_w[:, TAPS - 1, :], conv_w[:, TAPS - 1, :], in_u, ALU.mult).then_inc(s_made_pool, 1)

            def front_start(b):
                pool.wait_ge(u_silu.sem, u_silu.at(b))
                pool.sem_inc(pool_passed, 1)
                for h in range(HALVES):
                    pool.tensor_scalar(Y[:, h, :], US[:, h, :], vec("D_skip", h), None, ALU.mult).then_inc(skip_y.sem, 1)
                pool.wait_ge(delta_d.sem, delta_d.at(b))
                pool.wait_ge(db_mul.sem, db_mul.at(b - 1))
                pool.tensor_tensor(DU[:, :, :], DELTA[:, :, :], US[:, :, :], ALU.mult).then_inc(du_d.sem, 1)

            def front_step(b, n):
                pool.wait_ge(hc_mul.sem, hc_mul.at(b, n + 1))
                if n == 0:
                    pool.wait_ge(skip_y.sem, skip_y.at(b))
                else:
                    pool.wait_ge(y_add.sem, y_add.at(b, n))
                pool.tensor_tensor(Y[:, :, :], Y[:, :, :], HC[:, n % 2, :, :], ALU.add).then_inc(y_add.sem, 1)

            def front_end(b):
                pool.wait_ge(y_add.sem, y_add.at(b))
                pool.wait_ge(r_silu.sem, r_silu.at(b))
                pool.tensor_tensor(Y[:, :, :], Y[:, :, :], SR[:, :, :], ALU.mult).then_inc(y_gate.sem, 1)
                pool.wait_ge(yf_d.sem, yf_d.at(b - 1))
                pool.wait_ge(m0_d.sem, m0_d.at(b))
                pool.sem_inc(pool_passed, 1)
                pool.tensor_copy(XNB[:, :], xn).then_inc(xnb_d.sem, 1)

            def back_pair(b, j):
                for a in range(2):
                    n = 2 * j + a
                    pool.wait_ge(rot_d.sem, rot_d.at(b, 2 * n + 2))
                    if j >= 2:
                        pool.wait_ge(sc_mm.sem, sc_mm.at(b, 8 * (j - 1)))
                    pool.tensor_tensor(QK[:, j % 2, a, :], ROT, ROT2, ALU.add).then_inc(rope_d.sem, 1)

            def front(b):
                front_start(b)
                for n in range(STATES):
                    front_step(b, n)
                front_end(b)

            def lap(b, f=None):
                if f is not None:
                    front_start(f)
                for j in range(PAIRS):
                    if f is not None:
                        front_step(f, j)
                    back_pair(b, j)
                if f is not None:
                    for e in range(EXPERTS):
                        front_step(f, PAIRS + e)
                    front_end(f)

            laps(pool, front, lap, lambda b: lap(b, b + 1))


def lay_out(inputs):
    L0, L1 = "L0_attn_", "L1_attn_"
    g = {k: np.asarray(v) for k, v in inputs.items()}

    def stack_rows(t):
        n = t.shape[0] // P
        return t.reshape(n, P, -1).transpose(1, 0, 2).reshape(P, -1)

    swap = np.arange(HEADS * DK).reshape(-1, 2)[:, ::-1].reshape(-1)
    in_w, x_w = g[L0 + "in_proj_w"].T, g[L0 + "x_proj_w"].T
    bc = x_w[:, RANK:]
    named = {
        "in_res": in_w[:, INNER:],
        "x_bc": stack_rows(np.concatenate([bc, bc, bc], 1)), "x_dt": stack_rows(x_w[:, :RANK]),
        "out_proj": stack_rows(g[L0 + "out_proj_w"].T), "q": g[L0 + "q_w"].T, "k": g[L0 + "k_w"].T,
        "proj": g[L0 + "proj_w"].T, "fl": g[L0 + "fl_w"].T, "d1": g[L0 + "d1_w"].T, "d2": stack_rows(g[L0 + "d2_w"].T),
        "router": g["L0_ffn_Wr"], "gate": g["L1_ffn_Wg"],
        "wq": g[L1 + "wq"].T, "wq_swap": g[L1 + "wq"][swap].T, "wk": g[L1 + "wk"].T, "wk_swap": g[L1 + "wk"][swap].T,
        "wv": g[L1 + "wv"].T, "wo": stack_rows(g[L1 + "wo"].T),
    }
    weights = np.concatenate([named[k] for k in WEIGHTS], 1)
    vecs = {"dt_b": g[L0 + "dt_proj_b"], "gamma": g["L0_ffn_gamma"], "beta": g["L0_ffn_beta"],
            "bq_swap": g[L1 + "bq"][swap], "bk_swap": g[L1 + "bk"][swap]}
    for k in VECS:
        if k not in vecs:
            vecs[k] = g[(L1 if k in ("bq", "bk", "bv", "bo") else L0) + k]
    columns = np.concatenate([vecs[k].reshape(-1, P).T for k in VECS], 1)
    e_w1, e_w2 = g["L0_ffn_W1"], g["L0_ffn_W2"]
    experts = np.concatenate([
        e_w1, e_w2.reshape(EXPERTS, CHUNKS, P, D).transpose(0, 2, 1, 3).reshape(EXPERTS, P, -1),
        g["L0_ffn_b1"].reshape(EXPERTS, CHUNKS, P).transpose(0, 2, 1), g["L0_ffn_b2"][:, :, None]], 2)
    row_biases = np.concatenate([g["L0_ffn_br"], g["L1_ffn_bg"], np.arange(EXPERTS, dtype=np.float32)])
    theta = np.float32(10000.0) ** (np.arange(0, DK, 2, dtype=np.float32) / np.float32(DK))
    freqs = np.arange(S, dtype=np.float32)[:, None] * (np.float32(1.0) / theta)[None, :]
    angle = np.concatenate([freqs, freqs], -1).T
    sign = np.where(np.arange(DK) % 2 == 0, np.float32(-1), np.float32(1))[:, None]
    cos = np.tile(np.cos(angle), (2, 1)).astype(np.float32)
    sin = np.tile(np.sin(angle) * sign, (2, 1)).astype(np.float32)
    causal = np.where(np.arange(P)[None, :] > np.arange(P)[:, None], np.float32(MASKED), np.float32(0))
    row_of = (np.arange(96)[:, None] % 32 == np.arange(2 * STATES)[None, :]).astype(np.float32)
    arrays = {
        "xT": g[L0 + "input_tensor"].transpose(0, 2, 1), "weights": weights, "vecs": columns,
        "conv_rows": g[L0 + "conv_w"].T, "dt_w": g[L0 + "dt_proj_w"].T,
        "a_log": g[L0 + "A_log"].reshape(HALVES, P, STATES).transpose(1, 0, 2),
        "moe_up": g["L1_ffn_W1"].transpose(1, 0, 2), "moe_gate": g["L1_ffn_W3"].transpose(1, 0, 2),
        "moe_down": g["L1_ffn_W2"].reshape(EXPERTS, CHUNKS, P, D).transpose(2, 0, 1, 3),
        "experts": experts, "row_biases": row_biases, "cos": cos, "sin": sin,
        "identity": np.eye(P, dtype=np.float32), "causal": causal, "row_of": row_of, "in_u_w": in_w[:, :INNER],
    }
    return {k: np.ascontiguousarray(v) for k, v in arrays.items()}


def program(nc, shapes):
    args = [nc.dram_tensor(k, s, F32, kind="ExternalInput").ap() for k, s in shapes.items()]
    out = nc.dram_tensor("outT", (B, D, S), F32, kind="ExternalOutput").ap()
    build(nc, *args, out)


def kernel(**inputs):
    import concourse.bacc as bacc
    from concourse.bass_utils import run_bass_kernel_spmd

    arrays = lay_out(inputs)
    nc = bacc.Bacc("TRN2", target_bir_lowering=False, num_devices=1)
    program(nc, {k: v.shape for k, v in arrays.items()})
    r = run_bass_kernel_spmd(nc, [arrays], core_ids=[0])
    return np.ascontiguousarray(r.results[0]["outT"].transpose(0, 2, 1))
```

```python
from contextlib import ExitStack

import numpy as np
import concourse.bass as bass
from concourse import mybir

ALU = mybir.AluOpType
ACT = mybir.ActivationFunctionType
AX = mybir.AxisListType
F32 = mybir.dt.float32
BF16 = mybir.dt.bfloat16
U32 = mybir.dt.uint32

B, S, D = 8, 512, 128
P = 128
TILES = S // P
INNER = 2 * D
HALVES = INNER // P
STATES = 16
RANK = D // 16
TAPS = 4
PAD = TAPS - 1
HEADS, DK = 16, 64
PAIRS = HEADS // 2
EXPERTS = 8
HID = 4 * D
CHUNKS = HID // P
PICKS = 2
EXPERT_COLS = HID + CHUNKS * D + CHUNKS + 1
TINY = 1e-24
MASKED = -1e30

VECS = {}
for _name, _n in (("conv_b", 2), ("dt_b", 2), ("D_skip", 2), ("ln0_g", 1), ("ln0_b", 1), ("q_b", 1), ("k_b", 1),
                  ("proj_b", 1), ("fl_b", 1), ("lni_g", 1), ("lni_b", 1), ("ln1_g", 1), ("ln1_b", 1),
                  ("d1_b", 4), ("d2_b", 1), ("ln2_g", 1), ("ln2_b", 1), ("gamma", 1), ("beta", 1),
                  ("bq", PAIRS), ("bq_swap", PAIRS), ("bk", PAIRS), ("bk_swap", PAIRS), ("bv", PAIRS), ("bo", 1),
                  ("w_g", 1)):
    VECS[_name] = (sum(n for _, n in VECS.values()), _n)
N_VECS = sum(n for _, n in VECS.values())

WEIGHTS = {}
for _name, _n in (("in_res", INNER), ("x_bc", HALVES * 96), ("x_dt", HALVES * RANK),
                  ("out_proj", HALVES * D), ("q", D), ("k", D), ("proj", D), ("fl", D), ("d1", HID),
                  ("d2", CHUNKS * D), ("router", EXPERTS), ("gate", EXPERTS),
                  ("wq", HEADS * DK), ("wq_swap", HEADS * DK), ("wk", HEADS * DK), ("wk_swap", HEADS * DK),
                  ("wv", HEADS * DK), ("wo", PAIRS * D)):
    WEIGHTS[_name] = (sum(n for _, n in WEIGHTS.values()), _n)
N_WEIGHTS = sum(n for _, n in WEIGHTS.values())


class Signal:

    def __init__(self, ctx, nc, name, per, unit=1):
        self.sem, self.per, self.unit = ctx.enter_context(nc.semaphore(name)), per, unit

    def at(self, b, k=None):
        k = self.per if k is None else k
        return b * (self.per * self.unit) + (2 * self.per + k) * self.unit

    def head_start(self, engine):
        engine.sem_inc(self.sem, 2 * self.per * self.unit)


class Norm:

    def __init__(self, ctx, nc, name, x, ready, mean, var, eps, centred, square, rstd):
        self.x, self.ready, self.mean, self.var, self.eps = x, ready, mean, var, eps
        self.centred, self.square, self.rstd = centred, square, rstd
        self.s_mean = Signal(ctx, nc, f"{name}_mean", 1)
        self.s_centred = Signal(ctx, nc, f"{name}_centred", 1)
        self.s_square = Signal(ctx, nc, f"{name}_square", 1)
        self.s_var = Signal(ctx, nc, f"{name}_var", 1)
        self.s_std = Signal(ctx, nc, f"{name}_std", 1)
        self.s_rstd = Signal(ctx, nc, f"{name}_rstd", 1)


def build(nc, xT, weights, vecs, conv_rows, dt_w, a_log, moe_up, moe_gate, moe_down, experts,
          row_biases, cos, sin, identity, causal, row_of, in_u_w, outT):
    ctx = ExitStack()
    with ctx:
        def sb(name, shape, dt=F32):
            return ctx.enter_context(nc.sbuf_tensor(name, shape, dt))

        def signal(name, per=1, unit=1):
            return Signal(ctx, nc, name, per, unit)

        W = sb("W", [P, N_WEIGHTS])
        V_ = sb("V_", [P, N_VECS])

        def w(name, lo=0, n=P):
            at = WEIGHTS[name][0] + lo
            return W[:, at:at + n]

        def vec(name, k=0):
            at = VECS[name][0] + k
            return V_[:, at:at + 1]

        conv_w = sb("conv_w", [P, TAPS, INNER])
        dt_lhs = sb("dt_lhs", [RANK, INNER])
        a_neg = sb("a_neg", [P, HALVES, STATES])
        up_w = sb("up_w", [P, EXPERTS, HID])
        gate_w = sb("gate_w", [P, EXPERTS, HID])
        down_w = sb("down_w", [P, EXPERTS, CHUNKS, D])
        cos_t, sin_t = sb("cos_t", [P, S]), sb("sin_t", [P, S])
        ident = sb("ident", [P, P])
        ident_bf = sb("ident_bf", [P, P], BF16)
        causal_bf = sb("causal_bf", [P, P], BF16)
        row_of_sb = sb("row_of_sb", [96, 2 * STATES])
        pick = sb("pick", [96, 2 * STATES, P], BF16)
        row_bias = sb("row_bias", [P, 3 * EXPERTS])
        avg = sb("avg", [P, P])
        ones = sb("ones", [P, P])
        wg_cols = sb("wg_cols", [P, P])
        eps5, eps12 = sb("eps5", [P, 1]), sb("eps12", [P, 1])

        X = sb("X", [P, S])
        XN = sb("XN", [P, PAD + S])
        xn = XN[:, PAD:PAD + S]
        US = sb("US", [P, HALVES, S])
        SR = sb("SR", [P, HALVES, S])
        DELTA = sb("DELTA", [P, HALVES, S])
        DU = sb("DU", [P, HALVES, S])
        DA = sb("DA", [P, 2, HALVES, S])
        D1 = sb("D1", [P, HALVES, S])
        HS = sb("HS", [P, HALVES, S])
        HC = sb("HC", [P, 2, HALVES, S])
        Y = sb("Y", [P, HALVES, S])
        S3 = sb("S3", [96, S], BF16)
        S3B = HC[0:96, 0, 0, :].bitcast(BF16)[:, 0:S]
        DT = HC[0:RANK, 0, 1, :]
        R1 = HC[0:96, 1, 1, :]
        causal_f = D1[:, 0, 0:P]
        in_u = Y[:, 0, 0:INNER]
        M0 = sb("M0", [P, S])
        XNB = sb("XNB", [P, S])
        X2 = sb("X2", [P, S])
        XN2 = sb("XN2", [P, S])
        EW = sb("EW", [P, PICKS, EXPERT_COLS])
        REG = sb("REG", [P, 20, S])

        def reg(k):
            return REG[:, k, :]

        CX, CSQ, CR, H, QP, KP, Q, RK, LNI = (reg(k) for k in range(9))
        GK, M1, H2 = reg(9), reg(10), reg(11)
        F1 = REG[:, 12:16, :]
        L0A, XB, YF, TMP = (reg(k) for k in range(16, 20))
        M2, CR2 = QP, YF
        V = REG[:, 0:8, :].rearrange("p (t h) s -> p t (h s)", t=TILES)
        ROT, ROT2 = reg(8), reg(9)
        QK = REG[:, 10:14, :].rearrange("p (r a) s -> p r a s", r=2)
        PR = REG[:, 14:16, :]
        PT = REG[:, 16:18, :]
        O, OT = reg(18), reg(19)
        XNF, X3 = DELTA[:, 0, :], DELTA[:, 1, :]
        gate_s = DU[:, 0, 0:TILES * 64].rearrange("p (t c) -> p t c", t=TILES)
        OUT = DU[:, 1, :]
        XS, SL = D1, HS
        HH = HC[:, :, :, :].rearrange("p a h s -> p (a h) s")
        small = sb("small", [P, 64])
        gate_i = sb("gate_i", [P, TILES, 8], U32)
        pick_i = sb("pick_i", [1, 8], U32)
        maxes = sb("maxes", [P, 2, 2, 8])
        rows = sb("rows", [P, 2, 2, 8])

        FB, FC, FM = (ctx.enter_context(nc.psum_tensor(n, [P, S], F32)) for n in ("FB", "FC", "FM"))
        G = [ctx.enter_context(nc.psum_tensor(f"G{k}", [P, S], F32)) for k in range(5)]

        N_CONST = 15
        n_loads = 16 * N_CONST
        dve_passed, pool_passed, sp_passed = (ctx.enter_context(nc.semaphore(f"{e}_passed")) for e in ("dve", "pool", "sp"))
        s_const = ctx.enter_context(nc.semaphore("const_loaded"))
        s_made = ctx.enter_context(nc.semaphore("const_made"))
        s_alog = ctx.enter_context(nc.semaphore("alog_exp"))
        s_made_pool = ctx.enter_context(nc.semaphore("const_made_pool"))
        x_in = signal("x_in", 1, 16)
        xb_in = signal("xb_in", 1, 16)
        ew_in = [signal(f"ew_in{k}", 1, 16) for k in range(PICKS)]
        out_st = signal("out_st", 1, 16)
        xn_done = signal("xn_done")
        u_mm = signal("u_mm", 2)
        r_mm = signal("r_mm", 2)
        u_silu = signal("u_silu", 2)
        r_silu = signal("r_silu", 2)
        dt_mm, bc_mm = signal("dt_mm"), signal("bc_mm")
        dt_copy = signal("dt_copy")
        bc_split = signal("bc_split", 6)
        dp_mm = signal("dp_mm", 2)
        soft = signal("soft", 4)
        relu_d = signal("relu_d", 2)
        delta_d = signal("delta_d")
        wide_d = signal("wide_d", 3)
        du_d = signal("du_d")
        skip_y = signal("skip_y", 2)
        b_mm, c_mm = signal("b_mm", STATES), signal("c_mm", STATES)
        da_exp = signal("da_exp", 2 * STATES)
        db_mul = signal("db_mul", STATES)
        scan_d = signal("scan_d", STATES)
        hc_mul = signal("hc_mul", STATES)
        y_add = signal("y_add", STATES)
        y_gate = signal("y_gate")
        m_mm = signal("m_mm")
        m0_d = signal("m0_d")
        xnb_d = signal("xnb_d")

        h_d = signal("h_d", 2)
        q_mm, k_mm = signal("q_mm"), signal("k_mm")
        qp_d, qsq_d, kp_d, ksq_d = signal("qp_d"), signal("qsq_d"), signal("kp_d"), signal("ksq_d")
        qss_mm, kss_mm = signal("qss_mm"), signal("kss_mm")
        qk_cl = signal("qk_cl", 2)
        qk_sd, qk_rs = signal("qk_sd", 2), signal("qk_rs", 2)
        qn_d = signal("qn_d")
        q_gelu = signal("q_gelu")
        qw_mm = signal("qw_mm")
        gu_d = signal("gu_d", 4)
        g_act = signal("g_act", 2)
        gk_d = signal("gk_d")
        proj_mm = signal("proj_mm")
        lni_d = signal("lni_d", 2)
        hsm_d = signal("hsm_d")
        fl_mm = signal("fl_mm")
        m1_d = signal("m1_d")
        h2_d = signal("h2_d", 2)
        d1_mm, d1_gelu = signal("d1_mm", CHUNKS), signal("d1_gelu", CHUNKS)
        d2_mm = signal("d2_mm")
        m2_d = signal("m2_d")
        l0a_d = signal("l0a_d", 3)

        xm_d = signal("xm_d", 2)
        lg_mm = signal("lg_mm")
        rt_d = signal("rt_d", 10)
        rt_act = signal("rt_act", 2)
        wb_mm = signal("wb_mm")
        wb_d = signal("wb_d")
        idx_rd = signal("idx_rd")
        e1_mm, e1_gelu = signal("e1_mm", PICKS * CHUNKS), signal("e1_gelu", PICKS * CHUNKS)
        e2_mm = signal("e2_mm", 2 * PICKS)
        yf_d = signal("yf_d", 5)
        l0f_d = signal("l0f_d", 2)
        x2_d = signal("x2_d")
        xn2_d = signal("xn2_d")

        v_mm, v_copy = signal("v_mm", 2 * TILES), signal("v_copy", 2 * TILES)
        pj_mm = signal("pj_mm", 4 * PAIRS)
        rot_d = signal("rot_d", 4 * PAIRS)
        rope_d = signal("rope_d", 2 * PAIRS)
        sc_mm = signal("sc_mm", HEADS * TILES)
        mx_d = signal("mx_d", HEADS * TILES)
        nm_d = signal("nm_d", HEADS * TILES)
        p_exp = signal("p_exp", HEADS * TILES)
        pt_mm = signal("pt_mm", HEADS * TILES)
        pt_copy = signal("pt_copy", HEADS * TILES)
        pv_mm = signal("pv_mm", HEADS * TILES)
        rec_d = signal("rec_d", PAIRS)
        o_d = signal("o_d", PAIRS)
        ot_mm = signal("ot_mm", PAIRS)
        ot_copy = signal("ot_copy", PAIRS)
        wo_mm = signal("wo_mm", PAIRS)
        x3_d = signal("x3_d", 2)
        xnf_d = signal("xnf_d")

        gl_mm = signal("gl_mm")
        gt_d = signal("gt_d", 13)
        gt_act = signal("gt_act")
        wt_mm = signal("wt_mm", EXPERTS)
        xs_d = signal("xs_d", EXPERTS)
        ug_mm = signal("ug_mm", EXPERTS * CHUNKS)
        sl_act = signal("sl_act", EXPERTS * CHUNKS)
        sx_d = signal("sx_d", EXPERTS * CHUNKS)
        hh_d = signal("hh_d", EXPERTS * CHUNKS)
        dn_mm = signal("dn_mm", EXPERTS * CHUNKS)
        out_d = signal("out_d")

        n1 = Norm(ctx, nc, "norm_x", X[:, :], x_in, FM, FM, eps5, HC[:, 0, 0, :], HC[:, 0, 1, :], HC[:, 1, 0, :])
        n0 = Norm(ctx, nc, "norm_0", M0[:, :], m0_d, FB, FC, eps12, CX, CSQ, CR)
        ni = Norm(ctx, nc, "norm_i", H, h_d, FM, FM, eps12, CX, CSQ, CR2)
        n_1 = Norm(ctx, nc, "norm_1", M1, m1_d, FB, FC, eps12, CX, CSQ, CR)
        n_2 = Norm(ctx, nc, "norm_2", M2, m2_d, FB, FC, eps12, CX, CSQ, CR)
        nf = Norm(ctx, nc, "norm_f", YF, yf_d, FB, FC, eps5, CX, CSQ, CR)
        nx = Norm(ctx, nc, "norm_x2", X2[:, :], x2_d, FB, FC, eps5, CX, CSQ, CR)
        norms = (n1, n0, ni, n_1, n_2, nf, nx)

        by_pe = [u_mm, r_mm, dt_mm, bc_mm, dp_mm, b_mm, c_mm, m_mm, q_mm, k_mm, qss_mm, kss_mm, qw_mm, proj_mm, fl_mm,
                 d1_mm, d2_mm, lg_mm, wb_mm, e1_mm, e2_mm, v_mm, pj_mm, sc_mm, pt_mm, pv_mm, ot_mm, wo_mm, gl_mm,
                 wt_mm, ug_mm, dn_mm] + [s for n in norms for s in (n.s_mean, n.s_var)]
        by_act = [u_silu, r_silu, soft, da_exp, qsq_d, ksq_d, qk_sd, q_gelu, g_act, d1_gelu, rt_act,
                  e1_gelu, v_copy, p_exp, pt_copy, ot_copy, gt_act, sl_act, xnf_d] + [s for n in norms for s in (n.s_square, n.s_std)]
        by_dve = [qk_rs, qp_d, kp_d, xn_done, dt_copy, bc_split, relu_d, delta_d, wide_d, db_mul, scan_d, hc_mul, m0_d, h_d, qk_cl, qn_d, gu_d,
                  gk_d, lni_d, hsm_d, m1_d, h2_d, m2_d, l0a_d, xm_d, rt_d, wb_d, yf_d, l0f_d, x2_d, xn2_d, rot_d,
                  mx_d, nm_d, rec_d, o_d, x3_d, gt_d, xs_d, sx_d, hh_d, out_d] + [s for n in norms for s in (n.s_centred, n.s_rstd)]
        by_pool = [du_d, skip_y, y_add, y_gate, xnb_d, rope_d]
        by_sp = [x_in, xb_in, *ew_in, out_st, idx_rd]

        F_STEPS, T_STEPS = 24, EXPERTS * CHUNKS
        PHASE_1 = []
        for p in range(F_STEPS):
            PHASE_1.append(("f", p))
            PHASE_1 += [("t", k) for k in range(p * T_STEPS // F_STEPS, (p + 1) * T_STEPS // F_STEPS)]
        N_TILES = HEADS * TILES
        PER_PAIR = 2 * TILES
        AHEAD = 3
        RING = [G[0], G[1], FM]
        turn_free = {}
        ring_bank, ring_free = {}, {}
        uses = []

        def note_use(key, freed_by):
            ring_bank[key] = RING[len(uses) % len(RING)]
            ring_free[key] = uses[-len(RING)] if len(uses) >= len(RING) else None
            uses.append(freed_by)

        for m in range(4):
            note_use(("proj", m), (rot_d, m + 1))
        for n in range(AHEAD):
            note_use(("score", n), (p_exp, n + 1))
        for n in range(N_TILES):
            if n % PER_PAIR < 4 and n // PER_PAIR + 1 < PAIRS:
                m = 4 * (n // PER_PAIR + 1) + n % PER_PAIR
                note_use(("proj", m), (rot_d, m + 1))
            if n + AHEAD < N_TILES:
                note_use(("score", n + AHEAD), (p_exp, n + AHEAD + 1))

        block = ctx.enter_context(nc.Block())

        def laps(eng, front, phase_1, phase_2):
            front(0)
            phase_1(0, None)
            phase_2(0, 1)
            with eng.Fori(1, B - 1) as b:
                phase_1(b, b - 1)
                phase_2(b, b + 1)
            phase_1(B - 1, B - 2)
            phase_2(B - 1, None)
            phase_1(None, B - 1)

        @block.sync
        def _(sp):
            for s in by_sp:
                s.head_start(sp)
            for dst, src in ((W[:, :], weights), (V_[:, :], vecs), (dt_lhs[:, :], dt_w), (a_neg[:, :, :], a_log),
                             (ident[:, :], identity), (causal_f, causal), (row_of_sb[:, :], row_of),
                             (row_bias[:, :], row_biases.partition_broadcast(P)),
                             (conv_w[:, :, :], conv_rows.partition_broadcast(P)),
                             (cos_t[:, :], cos), (sin_t[:, :], sin), (up_w[:, :, :], moe_up),
                             (gate_w[:, :, :], moe_gate), (down_w[:, :, :, :], moe_down), (in_u, in_u_w)):
                sp.dma_start(dst, src).then_inc(s_const, 16)

            def load_x(b):
                sp.wait_ge(n1.s_centred.sem, n1.s_centred.at(b - 1))
                sp.dma_start(X[:, :], xT[b]).then_inc(x_in.sem, 16)

            def phase_1(b, t):
                if b is not None:
                    sp.wait_ge(wo_mm.sem, wo_mm.at(b - 1))
                    sp.dma_start(XB, xT[b]).then_inc(xb_in.sem, 16)
                    for k in range(PICKS):
                        sp.wait_ge(e2_mm.sem, e2_mm.at(b - 1))
                        sp.sem_inc(sp_passed, 1)
                        sp.wait_ge(x2_d.sem, x2_d.at(b - 1))
                        sp.sem_inc(sp_passed, 1)
                        sp.wait_ge(rt_d.sem, rt_d.at(b, 7))
                        sp.sem_inc(sp_passed, 1)
                        e = sp.value_load(pick_i[0:1, k:k + 1], min_val=0, max_val=EXPERTS - 1)
                        sp.dma_start(EW[:, k, :], experts[bass.ds(e, 1), :, :].rearrange("a p c -> (a p) c")).then_inc(ew_in[k].sem, 16)
                    sp.sem_inc(idx_rd.sem, 1)
                if t is not None:
                    sp.wait_ge(out_d.sem, out_d.at(t))
                    sp.dma_start(outT[t], OUT).then_inc(out_st.sem, 16)

            def phase_2(b, f):
                if f is not None:
                    load_x(f)

            laps(sp, load_x, phase_1, phase_2)
            sp.wait_ge(out_st.sem, out_st.at(B - 1))

        @block.tensor
        def _(pe):
            for s in by_pe:
                s.head_start(pe)
            pe.wait_ge(s_const, n_loads)
            pe.wait_ge(s_made, 14)
            pe.wait_ge(s_made_pool, 1)

            def mean(n, b):
                pe.wait_ge(n.ready.sem, n.ready.at(b))
                pe.matmul(n.mean[:, :], avg[:, :], n.x, start=True, stop=True).then_inc(n.s_mean.sem, 1)

            def var(n, b):
                pe.wait_ge(n.s_square.sem, n.s_square.at(b))
                pe.matmul(n.var[:, :], avg[:, :], n.square, start=True, stop=True).then_inc(n.s_var.sem, 1)

            def front_start(b):
                pe.wait_ge(x2_d.sem, x2_d.at(b - 1))
                pe.wait_ge(xn2_d.sem, xn2_d.at(b - 1))
                mean(n1, b)
                var(n1, b)
                pe.wait_ge(xn_done.sem, xn_done.at(b))
                for h, bank in ((0, FB), (1, FC)):
                    for tap in range(TAPS):
                        mm = pe.matmul(bank[:, :], conv_w[:, tap, h * P:(h + 1) * P], XN[:, tap:tap + S],
                                       start=tap == 0, stop=tap == TAPS - 1)
                    mm.then_inc(u_mm.sem, 1)
                for h in range(HALVES):
                    if h:
                        pe.wait_ge(r_silu.sem, r_silu.at(b, h))
                    pe.matmul(FM[:, :], w("in_res", h * P), xn, start=True, stop=True).then_inc(r_mm.sem, 1)
                pe.wait_ge(u_silu.sem, u_silu.at(b))
                for h in range(HALVES):
                    mm = pe.matmul(FB[0:96, :], w("x_bc", h * 96, 96), US[:, h, :], start=h == 0, stop=h == 1)
                mm.then_inc(bc_mm.sem, 1)
                pe.wait_ge(r_silu.sem, r_silu.at(b))
                for h in range(HALVES):
                    mm = pe.matmul(FM[0:RANK, :], w("x_dt", h * RANK, RANK), US[:, h, :], start=h == 0, stop=h == 1)
                mm.then_inc(dt_mm.sem, 1)
                pe.wait_ge(dt_copy.sem, dt_copy.at(b))
                pe.matmul(FC[:, :], dt_lhs[:, 0:P], DT, start=True, stop=True).then_inc(dp_mm.sem, 1)
                pe.matmul(FM[:, :], dt_lhs[:, P:INNER], DT, start=True, stop=True).then_inc(dp_mm.sem, 1)

            def front_step(b, n):
                if n:
                    pe.wait_ge(db_mul.sem, db_mul.at(b, n))
                else:
                    pe.wait_ge(bc_split.sem, bc_split.at(b))
                pe.matmul(FB[:, :], pick[:, n, :], S3[:, :], start=True, stop=True).then_inc(b_mm.sem, 1)
                if n:
                    pe.wait_ge(hc_mul.sem, hc_mul.at(b, n))
                else:
                    pe.wait_ge(relu_d.sem, relu_d.at(b))
                pe.matmul(FC[:, :], pick[:, STATES + n, :], S3[:, :], start=True, stop=True).then_inc(c_mm.sem, 1)

            def front_end(b):
                pe.wait_ge(y_gate.sem, y_gate.at(b))
                pe.wait_ge(p_exp.sem, p_exp.at(b - 1))
                for h in range(HALVES):
                    mm = pe.matmul(FM[:, :], w("out_proj", h * D), Y[:, h, :], start=h == 0, stop=h == 1)
                mm.then_inc(m_mm.sem, 1)

            def filter_step(b, p):
                if p == 0:
                    pe.wait_ge(hc_mul.sem, hc_mul.at(b))
                    mean(n0, b)
                elif p == 1:
                    pe.wait_ge(xm_d.sem, xm_d.at(b))
                    pe.matmul(FM[0:1, 0:EXPERTS], small[:, 0:1], w("router", 0, EXPERTS), start=True, stop=True).then_inc(lg_mm.sem, 1)
                    var(n0, b)
                elif p == 2:
                    pe.wait_ge(h_d.sem, h_d.at(b))
                    pe.matmul(FB[:, :], w("q"), H, start=True, stop=True).then_inc(q_mm.sem, 1)
                    pe.matmul(FC[:, :], w("k"), H, start=True, stop=True).then_inc(k_mm.sem, 1)
                    pe.wait_ge(rt_d.sem, rt_d.at(b, 1))
                    mean(ni, b)
                elif p == 3:
                    pe.wait_ge(qp_d.sem, qp_d.at(b))
                    pe.matmul(FB[:, :], ones[:, :], TMP, start=True, stop=True).then_inc(qss_mm.sem, 1)
                    pe.wait_ge(kp_d.sem, kp_d.at(b))
                    pe.matmul(FC[:, :], ones[:, :], M1, start=True, stop=True).then_inc(kss_mm.sem, 1)
                    var(ni, b)
                elif p == 4:
                    pe.wait_ge(rt_d.sem, rt_d.at(b, 10))
                    pe.wait_ge(qk_cl.sem, qk_cl.at(b))
                    pe.matmul(FB[:, 16:18], ones[0:1, :], small[0:1, 40:42], start=True, stop=True).then_inc(wb_mm.sem, 1)
                elif p == 5:
                    pe.wait_ge(q_gelu.sem, q_gelu.at(b))
                    pe.matmul(FC[:, :], wg_cols[:, :], Q, start=True, stop=True).then_inc(qw_mm.sem, 1)
                elif p == 6:
                    pe.wait_ge(wb_d.sem, wb_d.at(b))
                    pe.wait_ge(gk_d.sem, gk_d.at(b))
                    pe.matmul(FB[:, :], w("proj"), GK, start=True, stop=True).then_inc(proj_mm.sem, 1)
                elif p == 7:
                    pe.wait_ge(hsm_d.sem, hsm_d.at(b))
                    pe.wait_ge(g_act.sem, g_act.at(b, 1))
                    pe.matmul(FC[:, :], w("fl"), TMP, start=True, stop=True).then_inc(fl_mm.sem, 1)
                elif p == 8:
                    mean(n_1, b)
                elif p == 9:
                    var(n_1, b)
                elif p == 10:
                    pe.wait_ge(h2_d.sem, h2_d.at(b))
                    for c, bank in ((0, FB), (1, FC)):
                        pe.matmul(bank[:, :], w("d1", c * P), H2, start=True, stop=True).then_inc(d1_mm.sem, 1)
                elif p == 11:
                    for c, bank in ((2, FB), (3, FC)):
                        pe.wait_ge(d1_gelu.sem, d1_gelu.at(b, c - 1))
                        pe.matmul(bank[:, :], w("d1", c * P), H2, start=True, stop=True).then_inc(d1_mm.sem, 1)
                    pe.wait_ge(ni.s_rstd.sem, ni.s_rstd.at(b))
                    for c in range(2):
                        pe.matmul(FM[:, :], w("d2", c * D), F1[:, c, :], start=c == 0, stop=False)
                elif p == 12:
                    for c in range(2, CHUNKS):
                        pe.wait_ge(d1_gelu.sem, d1_gelu.at(b, c + 1))
                        mm = pe.matmul(FM[:, :], w("d2", c * D), F1[:, c, :], start=False, stop=c == CHUNKS - 1)
                    mm.then_inc(d2_mm.sem, 1)
                elif p == 13:
                    mean(n_2, b)
                elif p == 14:
                    var(n_2, b)
                elif p == 15:
                    pe.wait_ge(n_2.s_rstd.sem, n_2.s_rstd.at(b))
                    expert_up(b, 0, 0)
                elif p == 16:
                    expert_up(b, 0, 2)
                    expert_down(b, 0, 0)
                elif p == 17:
                    expert_up(b, 1, 0)
                    expert_down(b, 0, 2)
                elif p == 18:
                    expert_up(b, 1, 2)
                    pe.wait_ge(yf_d.sem, yf_d.at(b, 4))
                    expert_down(b, 1, 0)
                elif p == 19:
                    expert_down(b, 1, 2)
                elif p == 20:
                    mean(nf, b)
                elif p == 21:
                    var(nf, b)
                elif p == 22:
                    mean(nx, b)
                elif p == 23:
                    var(nx, b)

            def expert_up(b, k, c0):
                pe.wait_ge(ew_in[k].sem, ew_in[k].at(b))
                for c, bank in ((c0, FB), (c0 + 1, FC)):
                    n = k * CHUNKS + c
                    if n >= 2:
                        pe.wait_ge(e1_gelu.sem, e1_gelu.at(b, n - 1))
                    pe.matmul(bank[:, :], EW[:, k, c * P:(c + 1) * P], XNB[:, :], start=True, stop=True).then_inc(e1_mm.sem, 1)

            def expert_down(b, k, c0):
                for c in (c0, c0 + 1):
                    pe.wait_ge(e1_gelu.sem, e1_gelu.at(b, k * CHUNKS + c + 1))
                    mm = pe.matmul(FM[:, :], EW[:, k, HID + c * D:HID + (c + 1) * D], F1[:, c, :],
                                   start=c == 0, stop=c == CHUNKS - 1)
                mm.then_inc(e2_mm.sem, 1)

            def gate(b):
                pe.wait_ge(o_d.sem, o_d.at(b))
                pe.wait_ge(xnf_d.sem, xnf_d.at(b))
                for t in range(TILES):
                    mm = pe.matmul(G[3][:, t * 8:(t + 1) * 8], XNF[:, t * P:(t + 1) * P], w("gate", 0, EXPERTS), start=True, stop=True)
                mm.then_inc(gl_mm.sem, 1)
                pe.wait_ge(p_exp.sem, p_exp.at(b))
                pe.wait_ge(x3_d.sem, x3_d.at(b))

            def token_step(b, n):
                e, c = n // CHUNKS, n % CHUNKS
                if c == 0:
                    if e == 0:
                        pe.wait_ge(gt_d.sem, gt_d.at(b))
                    else:
                        pe.wait_ge(hh_d.sem, hh_d.at(b, n - 1))
                    g = 2 * ((5 * e) % 2)
                    for t in range(TILES):
                        mm = pe.matmul(G[g][:, t * P:(t + 1) * P], gate_s[:, t, 48 + e:49 + e].to_broadcast([P, P]), ident[:, :],
                                       start=True, stop=True)
                    mm.then_inc(wt_mm.sem, 1)
                    if e:
                        down(b, n - 1)
                    pe.wait_ge(xs_d.sem, xs_d.at(b, e + 1))
                g = 2 * ((5 * e + 1 + c) % 2)
                if n and c < 2:
                    pe.wait_ge(hh_d.sem, hh_d.at(b, n - c))
                elif c >= 2:
                    pe.wait_ge(hh_d.sem, hh_d.at(b, n - 1))
                pe.matmul(G[g][:, :], up_w[:, e, c * P:(c + 1) * P], XS[:, e % 2, :], start=True, stop=True)
                pe.matmul(G[g + 1][:, :], gate_w[:, e, c * P:(c + 1) * P], XS[:, e % 2, :], start=True, stop=True).then_inc(ug_mm.sem, 1)
                if c:
                    down(b, n - 1)

            def down(b, n):
                pe.wait_ge(hh_d.sem, hh_d.at(b, n + 1))
                pe.matmul(G[4][:, :], down_w[:, n // CHUNKS, n % CHUNKS, :], HH[:, n % 4, :], start=n == 0, stop=n == T_STEPS - 1,
                          skip_group_check=True).then_inc(dn_mm.sem, 1)

            def values_in(b):
                pe.wait_ge(out_d.sem, out_d.at(b - 1))
                pe.wait_ge(xn2_d.sem, xn2_d.at(b))
                for n in range(2 * TILES):
                    if n >= 4:
                        pe.wait_ge(v_copy.sem, v_copy.at(b, n - 3))
                    t, c = n // 2, n % 2
                    pe.matmul(G[n % 4][:, :], XN2[:, t * P:(t + 1) * P], w("wv", c * S, S), start=True, stop=True).then_inc(v_mm.sem, 1)

            def take(b, key):
                freed = ring_free[key]
                if freed is not None:
                    pe.wait_ge(freed[0].sem, freed[0].at(b, freed[1]))
                return ring_bank[key]

            def project(b, m):
                j, name = m // 4, ("wq", "wq_swap", "wk", "wk_swap")[m % 4]
                bank = take(b, ("proj", m))
                pe.matmul(bank[:, :], w(name, j * P), XN2[:, :], start=True, stop=True).then_inc(pj_mm.sem, 1)

            def score(b, n):
                j, i = n // PER_PAIR, n % PER_PAIR
                t, lo = i % TILES, (i // TILES) * DK
                width = (t + 1) * P
                bank = take(b, ("score", n))
                if i == 0:
                    pe.wait_ge(rope_d.sem, rope_d.at(b, 2 * j + 2))
                pe.matmul(bank[:, 0:width], QK[lo:lo + DK, j % 2, 0, t * P:(t + 1) * P],
                          QK[lo:lo + DK, j % 2, 1, 0:width], start=True, stop=False)
                pe.matmul(bank[:, t * P:width], ident_bf[:, :], causal_bf[:, :], start=False, stop=True).then_inc(sc_mm.sem, 1)

            def turn(b, n):
                t = n % TILES
                pe.wait_ge(p_exp.sem, p_exp.at(b, n + 1))
                if n:
                    pe.wait_ge(pt_copy.sem, pt_copy.at(b, n))
                if n % PER_PAIR == 2 and n > PER_PAIR:
                    pe.wait_ge(ot_copy.sem, ot_copy.at(b, n // PER_PAIR))
                for c in range(t + 1):
                    mm = pe.transpose(G[2][:, c * P:(c + 1) * P], PR[:, n % 2, c * P:(c + 1) * P], ident[:, :])
                mm.then_inc(pt_mm.sem, 1)

            def weigh_values(b, n):
                j, i = n // PER_PAIR, n % PER_PAIR
                t, h = i % TILES, i // TILES
                pe.wait_ge(pt_copy.sem, pt_copy.at(b, n + 1))
                if i == 0 and j:
                    pe.wait_ge(o_d.sem, o_d.at(b, j))
                col = t * P + h * DK
                for c in range(t + 1):
                    mm = pe.matmul(G[3][:, col:col + DK], PT[:, n % 2, c * P:(c + 1) * P],
                                   V[:, c, j * P + h * DK:j * P + (h + 1) * DK], start=c == 0, stop=c == t)
                mm.then_inc(pv_mm.sem, 1)

            def turn_out(b, j):
                pe.wait_ge(o_d.sem, o_d.at(b, j + 1))
                pe.wait_ge(pt_copy.sem, pt_copy.at(b, min(PER_PAIR * (j + 1) + 2, N_TILES)))
                for t in range(TILES):
                    mm = pe.transpose(G[2][:, t * P:(t + 1) * P], O[:, t * P:(t + 1) * P], ident[:, :])
                mm.then_inc(ot_mm.sem, 1)

            def project_out(b, j):
                pe.wait_ge(ot_copy.sem, ot_copy.at(b, j + 1))
                pe.matmul(G[4][:, :], w("wo", j * D), OT, start=j == 0, stop=j == PAIRS - 1,
                          skip_group_check=True).then_inc(wo_mm.sem, 1)

            def phase_1(b, t):
                if t is not None:
                    gate(t)
                for kind, k in PHASE_1:
                    if kind == "f" and b is not None:
                        filter_step(b, k)
                    if kind == "t" and t is not None:
                        token_step(t, k)
                if t is not None:
                    down(t, T_STEPS - 1)

            def phase_2(b, f):
                values_in(b)
                if f is not None:
                    front_start(f)
                pe.wait_ge(v_copy.sem, v_copy.at(b))
                if f is not None:
                    pe.wait_ge(relu_d.sem, relu_d.at(f))
                for m in range(4):
                    project(b, m)
                for n in range(AHEAD):
                    score(b, n)
                for n in range(N_TILES):
                    j, i = n // PER_PAIR, n % PER_PAIR
                    if i == 2 and j:
                        turn_out(b, j - 1)
                    turn(b, n)
                    if i == 3 and j:
                        project_out(b, j - 1)
                    if f is not None and i % 4 == 0:
                        front_step(f, 2 * j + i // 4)
                    if i < 4 and j + 1 < PAIRS:
                        project(b, 4 * (j + 1) + i)
                    if n + AHEAD < N_TILES:
                        score(b, n + AHEAD)
                    if n:
                        weigh_values(b, n - 1)
                weigh_values(b, N_TILES - 1)
                if f is not None:
                    front_end(f)
                turn_out(b, PAIRS - 1)
                project_out(b, PAIRS - 1)

            def front(b):
                front_start(b)
                for n in range(STATES):
                    front_step(b, n)
                front_end(b)

            laps(pe, front, phase_1, phase_2)

        @block.scalar
        def _(act):
            for s in by_act:
                s.head_start(act)
            act.wait_ge(s_const, n_loads)
            act.activation(a_neg[:, :, :], a_neg[:, :, :], ACT.Exp).then_inc(s_alog, 1)
            act.wait_ge(s_made, 14)

            def square(n, b):
                act.wait_ge(n.s_centred.sem, n.s_centred.at(b))
                act.activation(n.square, n.centred, ACT.Square).then_inc(n.s_square.sem, 1)

            def std(n, b):
                act.wait_ge(n.s_var.sem, n.s_var.at(b))
                act.activation(n.rstd, n.var[:, :], ACT.Sqrt, bias=n.eps[:, 0:1]).then_inc(n.s_std.sem, 1)

            def front_start(b):
                act.wait_ge(y_add.sem, y_add.at(b - 1))
                square(n1, b)
                std(n1, b)
                act.wait_ge(y_gate.sem, y_gate.at(b - 1))
                for h, bank in ((0, FB), (1, FC)):
                    act.wait_ge(u_mm.sem, u_mm.at(b, h + 1))
                    act.activation(US[:, h, :], bank[:, :], ACT.Silu, bias=vec("conv_b", h)).then_inc(u_silu.sem, 1)
                for h in range(HALVES):
                    act.wait_ge(r_mm.sem, r_mm.at(b, h + 1))
                    act.activation(SR[:, h, :], FM[:, :], ACT.Silu).then_inc(r_silu.sem, 1)
                act.wait_ge(scan_d.sem, scan_d.at(b - 1))
                act.wait_ge(ug_mm.sem, ug_mm.at(b - 2))
                for h, bank in ((0, FC), (1, FM)):
                    act.wait_ge(dp_mm.sem, dp_mm.at(b, h + 1))
                    act.activation(D1[:, h, :], bank[:, :], ACT.Abs, bias=vec("dt_b", h)).then_inc(soft.sem, 1)
                act.wait_ge(soft.sem, soft.at(b, 2))
                act.activation(D1[:, :, :], D1[:, :, :], ACT.Exp, scale=-1.0).then_inc(soft.sem, 1)
                act.wait_ge(wide_d.sem, wide_d.at(b, 2))
                act.activation(DELTA[:, :, :], DELTA[:, :, :], ACT.Ln).then_inc(soft.sem, 1)

            def front_step(b, n):
                if n == 0:
                    act.wait_ge(delta_d.sem, delta_d.at(b))
                if n >= 2:
                    act.wait_ge(scan_d.sem, scan_d.at(b, n - 1))
                for h in range(HALVES):
                    act.activation(DA[:, n % 2, h, 1:S], DELTA[:, h, 1:S], ACT.Exp,
                                   scale=a_neg[:, h, n:n + 1]).then_inc(da_exp.sem, 1)

            def filter_step(b, p):
                if p == 0:
                    act.wait_ge(wo_mm.sem, wo_mm.at(b - 1))
                    square(n0, b)
                elif p == 1:
                    std(n0, b)
                elif p == 2:
                    act.wait_ge(q_mm.sem, q_mm.at(b))
                    act.activation(TMP, FB[:, :], ACT.Square, bias=vec("q_b")).then_inc(qsq_d.sem, 1)
                    act.wait_ge(k_mm.sem, k_mm.at(b))
                    act.activation(M1, FC[:, :], ACT.Square, bias=vec("k_b")).then_inc(ksq_d.sem, 1)
                    square(ni, b)
                elif p == 3:
                    act.wait_ge(rt_d.sem, rt_d.at(b, 3))
                    act.activation(small[0:1, 16:24], small[0:1, 8:16], ACT.Exp, bias=small[0:1, 5:6], accum_out=small[0:1, 6:7]).then_inc(rt_act.sem, 1)
                    for k, buf in ((0, CR), (1, RK)):
                        act.wait_ge(qk_cl.sem, qk_cl.at(b, k + 1))
                        act.activation(buf, buf, ACT.Sqrt).then_inc(qk_sd.sem, 1)
                    std(ni, b)
                    act.wait_ge(rt_d.sem, rt_d.at(b, 8))
                    act.activation(small[0:1, 38:40], small[0:1, 24:26], ACT.Exp, bias=small[0:1, 7:8], accum_out=small[0:1, 36:37]).then_inc(rt_act.sem, 1)
                elif p == 4:
                    act.wait_ge(qn_d.sem, qn_d.at(b))
                    act.activation(Q, CR, ACT.Gelu).then_inc(q_gelu.sem, 1)
                elif p == 5:
                    act.wait_ge(gu_d.sem, gu_d.at(b, 1))
                    act.activation(CSQ, FC[:, :], ACT.Square, accum_out=small[:, 43:44]).then_inc(g_act.sem, 1)
                    act.wait_ge(gu_d.sem, gu_d.at(b, 2))
                    act.activation(small[:, 45:46], small[:, 44:45], ACT.Sqrt).then_inc(g_act.sem, 1)
                elif p == 8:
                    square(n_1, b)
                elif p == 9:
                    std(n_1, b)
                elif p in (10, 11):
                    for c, bank in ((2 * (p - 10), FB), (2 * (p - 10) + 1, FC)):
                        act.wait_ge(d1_mm.sem, d1_mm.at(b, c + 1))
                        act.activation(F1[:, c, :], bank[:, :], ACT.Gelu, bias=vec("d1_b", c)).then_inc(d1_gelu.sem, 1)
                elif p == 13:
                    square(n_2, b)
                elif p == 14:
                    std(n_2, b)
                elif p in (15, 16, 17, 18):
                    k, c0 = (p - 15) // 2, 2 * ((p - 15) % 2)
                    for c, bank in ((c0, FB), (c0 + 1, FC)):
                        n = k * CHUNKS + c
                        act.wait_ge(e1_mm.sem, e1_mm.at(b, n + 1))
                        if k:
                            act.wait_ge(e2_mm.sem, e2_mm.at(b, c // 2 + 1))
                        at = HID + CHUNKS * D + c
                        act.activation(F1[:, c, :], bank[:, :], ACT.Gelu, bias=EW[:, k, at:at + 1]).then_inc(e1_gelu.sem, 1)
                elif p == 20:
                    square(nf, b)
                elif p == 21:
                    std(nf, b)
                elif p == 22:
                    square(nx, b)
                elif p == 23:
                    std(nx, b)

            def gate(b):
                act.wait_ge(gt_d.sem, gt_d.at(b, 7))
                act.activation(gate_s[:, :, 26:27], gate_s[:, :, 25:26], ACT.Exp).then_inc(gt_act.sem, 1)

            def token_step(b, n):
                e, c = n // CHUNKS, n % CHUNKS
                act.wait_ge(ug_mm.sem, ug_mm.at(b, n + 1))
                if n >= 2:
                    act.wait_ge(hh_d.sem, hh_d.at(b, n - 1))
                g = 2 * ((5 * e + 1 + c) % 2)
                act.activation(SL[:, n % 2, :], G[g][:, :], ACT.Tanh, scale=0.5).then_inc(sl_act.sem, 1)

            def values_in(b):
                act.wait_ge(xn2_d.sem, xn2_d.at(b))
                for n in range(2 * TILES):
                    act.wait_ge(v_mm.sem, v_mm.at(b, n + 1))
                    act.activation(V[:, n // 2, (n % 2) * S:(n % 2 + 1) * S], G[n % 4][:, :], ACT.Copy).then_inc(v_copy.sem, 1)

            def exponentials(b, n):
                j, i = n // PER_PAIR, n % PER_PAIR
                width = (i % TILES + 1) * P
                act.wait_ge(nm_d.sem, nm_d.at(b, n + 1))
                if n >= 2:
                    act.wait_ge(pt_mm.sem, pt_mm.at(b, n - 1))
                if i == 0 and j >= 2:
                    act.wait_ge(rec_d.sem, rec_d.at(b, j - 1))
                act.activation(PR[:, n % 2, 0:width], ring_bank[("score", n)][:, 0:width], ACT.Exp, scale=DK ** -0.5,
                               bias=maxes[:, j % 2, 1, i:i + 1], accum_out=rows[:, j % 2, 0, i:i + 1]).then_inc(p_exp.sem, 1)

            def copy_turned(b, n):
                width = (n % TILES + 1) * P
                act.wait_ge(pt_mm.sem, pt_mm.at(b, n + 1))
                if n >= 2:
                    act.wait_ge(pv_mm.sem, pv_mm.at(b, n - 1))
                act.activation(PT[:, n % 2, 0:width], G[2][:, 0:width], ACT.Copy).then_inc(pt_copy.sem, 1)

            def copy_out(b, j):
                act.wait_ge(ot_mm.sem, ot_mm.at(b, j + 1))
                if j:
                    act.wait_ge(wo_mm.sem, wo_mm.at(b, j))
                act.activation(OT, G[2][:, :], ACT.Identity, bias=vec("bv", j)).then_inc(ot_copy.sem, 1)

            def phase_1(b, t):
                if t is not None:
                    gate(t)
                for kind, k in PHASE_1:
                    if kind == "f" and b is not None:
                        filter_step(b, k)
                    if kind == "t" and t is not None:
                        token_step(t, k)

            def phase_2(b, f):
                values_in(b)
                if f is not None:
                    front_start(f)
                exponentials(b, 0)
                exponentials(b, 1)
                for n in range(N_TILES):
                    j, i = n // PER_PAIR, n % PER_PAIR
                    if i == 2 and j:
                        copy_out(b, j - 1)
                    copy_turned(b, n)
                    if n + 2 < N_TILES:
                        exponentials(b, n + 2)
                    if f is not None and i % 4 == 0:
                        front_step(f, 2 * j + i // 4)
                copy_out(b, PAIRS - 1)
                if f is not None:
                    act.wait_ge(da_exp.sem, da_exp.at(f))
                    act.wait_ge(du_d.sem, du_d.at(f))
                act.activation(XNF, XN2[:, :], ACT.Copy).then_inc(xnf_d.sem, 1)

            def front(b):
                front_start(b)
                for n in range(STATES):
                    front_step(b, n)

            laps(act, front, phase_1, phase_2)

        @block.vector
        def _(dve):
            for s in by_dve:
                s.head_start(dve)
            dve.wait_ge(s_const, n_loads)
            dve.memset(avg[:, :], 1.0 / P).then_inc(s_made, 1)
            dve.memset(ones[:, :], 1.0).then_inc(s_made, 1)
            dve.memset(eps5[:, :], 1e-5).then_inc(s_made, 1)
            dve.memset(eps12[:, :], 1e-12).then_inc(s_made, 1)
            dve.memset(XN[:, 0:PAD], 0.0).then_inc(s_made, 1)
            dve.memset(DA[:, :, :, 0:1], 0.0).then_inc(s_made, 1)
            dve.tensor_copy(ident_bf[:, :], ident[:, :]).then_inc(s_made, 1)
            dve.tensor_copy(causal_bf[:, :], causal_f).then_inc(s_made, 1)
            dve.tensor_copy(pick[:, :, :], row_of_sb[:, :].unsqueeze(2).to_broadcast([96, 2 * STATES, P])).then_inc(s_made, 1)
            dve.tensor_copy(wg_cols[:, :], vec("w_g").to_broadcast([P, P])).then_inc(s_made, 1)
            for tap in range(TAPS - 1):
                dve.tensor_tensor(conv_w[:, tap, :], conv_w[:, tap, :], in_u, ALU.mult).then_inc(s_made, 1)
            dve.wait_ge(s_alog, 1)
            dve.tensor_scalar(a_neg[:, :, :], a_neg[:, :, :], -1.0, None, ALU.mult).then_inc(s_made, 1)

            def invert(n, b):
                dve.wait_ge(n.s_std.sem, n.s_std.at(b))
                dve.reciprocal(n.rstd, n.rstd).then_inc(n.s_rstd.sem, 1)
                dve.wait_ge(n.s_rstd.sem, n.s_rstd.at(b))

            def centre(n, b):
                dve.wait_ge(n.s_mean.sem, n.s_mean.at(b))
                dve.tensor_tensor(n.centred, n.x, n.mean[:, :], ALU.subtract).then_inc(n.s_centred.sem, 1)

            def affine(n, b, out, gain, bias, done):
                invert(n, b)
                dve.scalar_tensor_tensor(out, n.centred, gain, n.rstd, ALU.mult, ALU.mult).then_inc(done.sem, 1)
                dve.wait_ge(done.sem, done.at(b, 1))
                dve.tensor_scalar(out, out, bias, None, ALU.add).then_inc(done.sem, 1)

            def front_start(b):
                dve.wait_ge(y_add.sem, y_add.at(b - 1))
                dve.wait_ge(dn_mm.sem, dn_mm.at(b - 2))
                centre(n1, b)
                invert(n1, b)
                dve.wait_ge(xnb_d.sem, xnb_d.at(b - 1))
                dve.tensor_tensor(xn, n1.centred, n1.rstd, ALU.mult).then_inc(xn_done.sem, 1)
                dve.wait_ge(c_mm.sem, c_mm.at(b - 1))
                dve.wait_ge(bc_mm.sem, bc_mm.at(b))
                dve.tensor_copy(S3[:, :], FB[0:96, :]).then_inc(bc_split.sem, 1)
                dve.wait_ge(bc_split.sem, bc_split.at(b, 1))
                dve.tensor_tensor(R1, FB[0:96, :], S3[:, :], ALU.subtract).then_inc(bc_split.sem, 1)
                dve.wait_ge(dt_mm.sem, dt_mm.at(b))
                dve.tensor_copy(DT, FM[0:RANK, :]).then_inc(dt_copy.sem, 1)
                dve.wait_ge(bc_split.sem, bc_split.at(b, 2))
                dve.tensor_copy(S3B, R1).then_inc(bc_split.sem, 1)
                dve.wait_ge(bc_split.sem, bc_split.at(b, 3))
                dve.tensor_tensor(R1[64:96, :], R1[64:96, :], S3B[64:96, :], ALU.subtract).then_inc(bc_split.sem, 1)
                dve.tensor_copy(S3[32:64, :], S3B[32:64, :]).then_inc(bc_split.sem, 1)
                dve.wait_ge(bc_split.sem, bc_split.at(b, 5))
                dve.tensor_copy(S3[64:96, :], R1[64:96, :]).then_inc(bc_split.sem, 1)
                for h, bank in ((0, FC), (1, FM)):
                    dve.wait_ge(soft.sem, soft.at(b, h + 1))
                    dve.tensor_scalar(HS[:, h, :], bank[:, :], vec("dt_b", h), 0.0, ALU.add, ALU.max).then_inc(relu_d.sem, 1)
                dve.wait_ge(soft.sem, soft.at(b, 3))
                dve.tensor_scalar(DELTA[:, :, :], D1[:, :, :], 1.0, None, ALU.add).then_inc(wide_d.sem, 1)
                dve.wait_ge(wide_d.sem, wide_d.at(b, 1))
                dve.scalar_tensor_tensor(D1[:, :, :], DELTA[:, :, :], -1.0, D1[:, :, :], ALU.add, ALU.subtract).then_inc(wide_d.sem, 1)
                dve.wait_ge(wide_d.sem, wide_d.at(b, 2))
                dve.wait_ge(relu_d.sem, relu_d.at(b))
                dve.tensor_tensor(HS[:, :, :], HS[:, :, :], D1[:, :, :], ALU.subtract).then_inc(wide_d.sem, 1)
                dve.wait_ge(soft.sem, soft.at(b, 4))
                dve.wait_ge(wide_d.sem, wide_d.at(b, 3))
                dve.tensor_tensor(DELTA[:, :, :], HS[:, :, :], DELTA[:, :, :], ALU.add).then_inc(delta_d.sem, 1)

            def front_step(b, n, part):
                if part == 0:
                    dve.wait_ge(b_mm.sem, b_mm.at(b, n + 1))
                    if n == 0:
                        dve.wait_ge(du_d.sem, du_d.at(b))
                    dve.tensor_tensor(D1[:, :, :], DU[:, :, :], FB[:, :].unsqueeze(1).to_broadcast([P, HALVES, S]), ALU.mult).then_inc(db_mul.sem, 1)
                elif part == 1:
                    dve.wait_ge(db_mul.sem, db_mul.at(b, n + 1))
                    dve.wait_ge(da_exp.sem, da_exp.at(b, 2 * n + 2))
                    dve.tensor_tensor_scan(HS[:, :, :].rearrange("p h s -> p (h s)"), DA[:, n % 2, :, :].rearrange("p h s -> p (h s)"),
                                           D1[:, :, :].rearrange("p h s -> p (h s)"), 0.0, ALU.mult, ALU.add).then_inc(scan_d.sem, 1)
                else:
                    dve.wait_ge(scan_d.sem, scan_d.at(b, n + 1))
                    dve.wait_ge(c_mm.sem, c_mm.at(b, n + 1))
                    if n >= 2:
                        dve.wait_ge(y_add.sem, y_add.at(b, n - 1))
                    dve.tensor_tensor(HC[:, n % 2, :, :], HS[:, :, :], FC[:, :].unsqueeze(1).to_broadcast([P, HALVES, S]), ALU.mult).then_inc(hc_mul.sem, 1)

            def front_end(b):
                dve.wait_ge(m_mm.sem, m_mm.at(b))
                dve.tensor_tensor(M0[:, :], xn, FM[:, :], ALU.add).then_inc(m0_d.sem, 1)

            def filter_step(b, p):
                if p == 0:
                    dve.wait_ge(wo_mm.sem, wo_mm.at(b - 1))
                    centre(n0, b)
                    dve.wait_ge(xnb_d.sem, xnb_d.at(b))
                    dve.tensor_reduce(small[:, 1:2], XNB[:, :], AX.X, ALU.add).then_inc(xm_d.sem, 1)
                    dve.wait_ge(xm_d.sem, xm_d.at(b, 1))
                    dve.tensor_scalar(small[:, 0:1], small[:, 1:2], 1.0 / S, None, ALU.mult).then_inc(xm_d.sem, 1)
                elif p == 1:
                    dve.wait_ge(lg_mm.sem, lg_mm.at(b))
                    dve.tensor_tensor(small[0:1, 8:16], FM[0:1, 0:8], row_bias[0:1, 0:8], ALU.add).then_inc(rt_d.sem, 1)
                    dve.wait_ge(rt_d.sem, rt_d.at(b, 1))
                    dve.tensor_reduce(small[0:1, 4:5], small[0:1, 8:16], AX.X, ALU.max).then_inc(rt_d.sem, 1)
                    dve.wait_ge(rt_d.sem, rt_d.at(b, 2))
                    dve.tensor_scalar(small[0:1, 5:6], small[0:1, 4:5], -1.0, None, ALU.mult).then_inc(rt_d.sem, 1)
                    affine(n0, b, H, vec("ln0_g"), vec("ln0_b"), h_d)
                elif p == 2:
                    centre(ni, b)
                    dve.wait_ge(qsq_d.sem, qsq_d.at(b))
                    dve.tensor_scalar(QP, FB[:, :], vec("q_b"), None, ALU.add).then_inc(qp_d.sem, 1)
                    dve.wait_ge(ksq_d.sem, ksq_d.at(b))
                    dve.tensor_scalar(KP, FC[:, :], vec("k_b"), None, ALU.add).then_inc(kp_d.sem, 1)
                elif p == 3:
                    dve.wait_ge(qss_mm.sem, qss_mm.at(b))
                    dve.tensor_scalar(CR, FB[:, :], TINY, None, ALU.max).then_inc(qk_cl.sem, 1)
                    dve.wait_ge(kss_mm.sem, kss_mm.at(b))
                    dve.tensor_scalar(RK, FC[:, :], TINY, None, ALU.max).then_inc(qk_cl.sem, 1)
                    dve.wait_ge(rt_act.sem, rt_act.at(b, 1))
                    dve.reciprocal(small[0:1, 3:4], small[0:1, 6:7]).then_inc(rt_d.sem, 1)
                    dve.wait_ge(rt_d.sem, rt_d.at(b, 4))
                    dve.tensor_scalar(small[0:1, 48:56], small[0:1, 16:24], small[0:1, 3:4], None, ALU.mult).then_inc(rt_d.sem, 1)
                    dve.wait_ge(idx_rd.sem, idx_rd.at(b - 1))
                    dve.wait_ge(rt_d.sem, rt_d.at(b, 5))
                    dve.sem_inc(dve_passed, 1)
                    dve.max(small[0:1, 24:32], small[0:1, 48:56]).then_inc(rt_d.sem, 1)
                    dve.wait_ge(rt_d.sem, rt_d.at(b, 6))
                    dve.sem_inc(dve_passed, 1)
                    dve.max_index(pick_i[0:1, :], small[0:1, 24:32], small[0:1, 48:56]).then_inc(rt_d.sem, 1)
                    dve.tensor_scalar(small[0:1, 7:8], small[0:1, 24:25], -1.0, None, ALU.mult).then_inc(rt_d.sem, 1)
                elif p == 4:
                    dve.wait_ge(rt_act.sem, rt_act.at(b, 2))
                    dve.reciprocal(small[0:1, 37:38], small[0:1, 36:37]).then_inc(rt_d.sem, 1)
                    dve.wait_ge(rt_d.sem, rt_d.at(b, 9))
                    dve.tensor_scalar(small[0:1, 40:42], small[0:1, 38:40], small[0:1, 37:38], None, ALU.mult).then_inc(rt_d.sem, 1)
                    for k, buf in ((0, CR), (1, RK)):
                        dve.wait_ge(qk_sd.sem, qk_sd.at(b, k + 1))
                        dve.reciprocal(buf, buf).then_inc(qk_rs.sem, 1)
                    dve.wait_ge(qp_d.sem, qp_d.at(b))
                    dve.wait_ge(qk_rs.sem, qk_rs.at(b, 1))
                    dve.tensor_tensor(CR, CR, QP, ALU.mult).then_inc(qn_d.sem, 1)
                    affine(ni, b, LNI, vec("lni_g"), vec("lni_b"), lni_d)
                    dve.wait_ge(wb_mm.sem, wb_mm.at(b))
                    dve.tensor_copy(small[:, 32:34], FB[:, 16:18]).then_inc(wb_d.sem, 1)
                elif p == 5:
                    dve.wait_ge(qw_mm.sem, qw_mm.at(b))
                    dve.tensor_tensor_reduce(out=YF, in0=Q, in1=FC[:, :], scale=1.0, scalar=0.0, op0=ALU.mult, op1=ALU.add,
                                             accum_out=small[:, 42:43]).then_inc(gu_d.sem, 1)
                    dve.wait_ge(g_act.sem, g_act.at(b, 1))
                    dve.tensor_scalar(small[:, 44:45], small[:, 43:44], 1.0 / D, TINY, ALU.mult, ALU.max).then_inc(gu_d.sem, 1)
                    dve.wait_ge(g_act.sem, g_act.at(b, 2))
                    dve.reciprocal(small[:, 46:47], small[:, 45:46]).then_inc(gu_d.sem, 1)
                    dve.wait_ge(gu_d.sem, gu_d.at(b, 3))
                    dve.tensor_scalar(small[:, 47:48], small[:, 42:43], float(D) ** -0.5, small[:, 46:47], ALU.mult, ALU.mult).then_inc(gu_d.sem, 1)
                    dve.wait_ge(kp_d.sem, kp_d.at(b))
                    dve.wait_ge(qk_rs.sem, qk_rs.at(b, 2))
                    dve.wait_ge(gu_d.sem, gu_d.at(b, 4))
                    dve.scalar_tensor_tensor(GK, KP, small[:, 47:48], RK, ALU.mult, ALU.mult).then_inc(gk_d.sem, 1)
                elif p == 6:
                    dve.wait_ge(lni_d.sem, lni_d.at(b))
                    dve.wait_ge(proj_mm.sem, proj_mm.at(b))
                    dve.scalar_tensor_tensor(TMP, FB[:, :], vec("proj_b"), LNI, ALU.add, ALU.mult).then_inc(hsm_d.sem, 1)
                elif p == 7:
                    dve.wait_ge(fl_mm.sem, fl_mm.at(b))
                    dve.scalar_tensor_tensor(M1, FC[:, :], vec("fl_b"), H, ALU.add, ALU.add).then_inc(m1_d.sem, 1)
                elif p == 8:
                    centre(n_1, b)
                elif p == 9:
                    affine(n_1, b, H2, vec("ln1_g"), vec("ln1_b"), h2_d)
                elif p == 12:
                    dve.wait_ge(d2_mm.sem, d2_mm.at(b))
                    dve.scalar_tensor_tensor(M2, FM[:, :], vec("d2_b"), H2, ALU.add, ALU.add).then_inc(m2_d.sem, 1)
                elif p == 13:
                    centre(n_2, b)
                elif p == 14:
                    affine(n_2, b, L0A, vec("ln2_g"), vec("ln2_b"), l0a_d)
                elif p == 15:
                    dve.wait_ge(xb_in.sem, xb_in.at(b))
                    dve.wait_ge(l0a_d.sem, l0a_d.at(b, 2))
                    dve.tensor_tensor(L0A, L0A, XB, ALU.add).then_inc(l0a_d.sem, 1)
                    w0, w1 = small[:, 32:33], small[:, 33:34]
                    at = EXPERT_COLS - 1
                    for k in range(PICKS):
                        dve.wait_ge(ew_in[k].sem, ew_in[k].at(b))
                    dve.wait_ge(wb_d.sem, wb_d.at(b))
                    dve.tensor_scalar(small[:, 34:35], EW[:, 0, at:at + 1], w0, None, ALU.mult).then_inc(yf_d.sem, 1)
                    dve.wait_ge(yf_d.sem, yf_d.at(b, 1))
                    dve.scalar_tensor_tensor(small[:, 35:36], EW[:, 1, at:at + 1], w1, small[:, 34:35], ALU.mult, ALU.add).then_inc(yf_d.sem, 1)
                    dve.wait_ge(yf_d.sem, yf_d.at(b, 2))
                    dve.tensor_scalar(YF, XNB[:, :], small[:, 35:36], None, ALU.add).then_inc(yf_d.sem, 1)
                elif p in (17, 19):
                    k = (p - 17) // 2
                    dve.wait_ge(yf_d.sem, yf_d.at(b, 3 + k))
                    dve.wait_ge(e2_mm.sem, e2_mm.at(b, 2 * k + 2))
                    dve.scalar_tensor_tensor(YF, FM[:, :], small[:, 32 + k:33 + k], YF, ALU.mult, ALU.add).then_inc(yf_d.sem, 1)
                elif p == 20:
                    centre(nf, b)
                elif p == 21:
                    affine(nf, b, YF, vec("gamma"), vec("beta"), l0f_d)
                    dve.wait_ge(l0f_d.sem, l0f_d.at(b))
                    dve.wait_ge(l0a_d.sem, l0a_d.at(b))
                    dve.tensor_tensor(X2[:, :], YF, L0A, ALU.add).then_inc(x2_d.sem, 1)
                elif p == 22:
                    centre(nx, b)
                elif p == 23:
                    invert(nx, b)
                    dve.tensor_tensor(XN2[:, :], nx.centred, nx.rstd, ALU.mult).then_inc(xn2_d.sem, 1)

            def gate(b):
                gs = gate_s
                dve.wait_ge(out_st.sem, out_st.at(b - 1))
                dve.wait_ge(gl_mm.sem, gl_mm.at(b))
                dve.tensor_tensor(gs[:, :, 0:8], G[3][:, 0:32].rearrange("p (t e) -> p t e", e=8),
                                  row_bias[:, 8:16].unsqueeze(1).to_broadcast([P, TILES, 8]), ALU.add).then_inc(gt_d.sem, 1)
                dve.wait_ge(gt_d.sem, gt_d.at(b, 1))
                dve.sem_inc(dve_passed, 1)
                for t in range(TILES):
                    dve.max(gs[:, t, 8:16], gs[:, t, 0:8]).then_inc(gt_d.sem, 1)
                dve.wait_ge(gt_d.sem, gt_d.at(b, 5))
                dve.sem_inc(dve_passed, 1)
                for t in range(TILES):
                    ins = dve.max_index(gate_i[:, t, :], gs[:, t, 8:16], gs[:, t, 0:8])
                ins.then_inc(gt_d.sem, 1)
                dve.tensor_tensor(gs[:, :, 25:26], gs[:, :, 9:10], gs[:, :, 8:9], ALU.subtract).then_inc(gt_d.sem, 1)
                dve.wait_ge(gt_d.sem, gt_d.at(b, 6))
                dve.tensor_copy(gs[:, :, 16:24], gate_i[:, :, :]).then_inc(gt_d.sem, 1)
                dve.wait_ge(gt_act.sem, gt_act.at(b))
                dve.tensor_scalar(gs[:, :, 24:25], gs[:, :, 26:27], 1.0, None, ALU.add).then_inc(gt_d.sem, 1)
                dve.wait_ge(gt_d.sem, gt_d.at(b, 9))
                dve.reciprocal(gs[:, :, 27:28], gs[:, :, 24:25]).then_inc(gt_d.sem, 1)
                dve.wait_ge(gt_d.sem, gt_d.at(b, 10))
                dve.tensor_tensor(gs[:, :, 28:29], gs[:, :, 27:28], gs[:, :, 26:27], ALU.mult).then_inc(gt_d.sem, 1)
                dve.wait_ge(gt_d.sem, gt_d.at(b, 11))
                numbers = row_bias[:, 16:24]
                for t in range(TILES):
                    dve.tensor_scalar(gs[:, t, 32:40], numbers, gs[:, t, 16:17], gs[:, t, 27:28], ALU.is_equal, ALU.mult)
                    ins = dve.tensor_scalar(gs[:, t, 40:48], numbers, gs[:, t, 17:18], gs[:, t, 28:29], ALU.is_equal, ALU.mult)
                ins.then_inc(gt_d.sem, 1)
                dve.wait_ge(gt_d.sem, gt_d.at(b, 12))
                dve.tensor_tensor(gs[:, :, 48:56], gs[:, :, 32:40], gs[:, :, 40:48], ALU.add).then_inc(gt_d.sem, 1)

            def token_step(b, n):
                e, c = n // CHUNKS, n % CHUNKS
                if c == 0:
                    g = 2 * ((5 * e) % 2)
                    dve.wait_ge(wt_mm.sem, wt_mm.at(b, e + 1))
                    if e >= 2:
                        dve.wait_ge(ug_mm.sem, ug_mm.at(b, CHUNKS * (e - 1)))
                    dve.tensor_tensor(XS[:, e % 2, :], XNF, G[g][:, :], ALU.mult).then_inc(xs_d.sem, 1)
                g = 2 * ((5 * e + 1 + c) % 2)
                dve.wait_ge(sl_act.sem, sl_act.at(b, n + 1))
                dve.scalar_tensor_tensor(SL[:, n % 2, :], SL[:, n % 2, :], 1.0, G[g][:, :], ALU.add, ALU.mult).then_inc(sx_d.sem, 1)
                if n >= 4:
                    dve.wait_ge(dn_mm.sem, dn_mm.at(b, n - 3))
                dve.wait_ge(sx_d.sem, sx_d.at(b, n + 1))
                dve.scalar_tensor_tensor(HH[:, n % 4, :], SL[:, n % 2, :], 0.5, G[g + 1][:, :], ALU.mult, ALU.mult).then_inc(hh_d.sem, 1)

            def token_end(b):
                dve.wait_ge(dn_mm.sem, dn_mm.at(b))
                dve.tensor_tensor(OUT, X3, G[4][:, :], ALU.add).then_inc(out_d.sem, 1)

            def rotate(b, m):
                j = m // 4
                name, table, out = (("bq", cos_t, ROT), ("bq_swap", sin_t, ROT2), ("bk", cos_t, ROT), ("bk_swap", sin_t, ROT2))[m % 4]
                if m >= 2:
                    dve.wait_ge(rope_d.sem, rope_d.at(b, m // 2))
                dve.wait_ge(pj_mm.sem, pj_mm.at(b, m + 1))
                dve.scalar_tensor_tensor(out, ring_bank[("proj", m)][:, :], vec(name, j), table[:, :], ALU.add, ALU.mult).then_inc(rot_d.sem, 1)

            def largest(b, n):
                j, i = n // PER_PAIR, n % PER_PAIR
                width = (i % TILES + 1) * P
                dve.wait_ge(sc_mm.sem, sc_mm.at(b, n + 1))
                dve.tensor_reduce(maxes[:, j % 2, 0, i:i + 1], ring_bank[("score", n)][:, 0:width], AX.X, ALU.max).then_inc(mx_d.sem, 1)
                dve.wait_ge(mx_d.sem, mx_d.at(b, n + 1))
                dve.tensor_scalar(maxes[:, j % 2, 1, i:i + 1], maxes[:, j % 2, 0, i:i + 1], -DK ** -0.5, None, ALU.mult).then_inc(nm_d.sem, 1)

            def divide(b, j):
                dve.wait_ge(p_exp.sem, p_exp.at(b, PER_PAIR * (j + 1)))
                dve.reciprocal(rows[:, j % 2, 1, :], rows[:, j % 2, 0, :]).then_inc(rec_d.sem, 1)
                if j:
                    dve.wait_ge(ot_mm.sem, ot_mm.at(b, j))
                dve.wait_ge(pv_mm.sem, pv_mm.at(b, PER_PAIR * (j + 1)))
                dve.wait_ge(rec_d.sem, rec_d.at(b, j + 1))
                dve.tensor_tensor(O.rearrange("p (t h d) -> p t h d", t=TILES, h=2),
                                  G[3][:, :].rearrange("p (t h d) -> p t h d", t=TILES, h=2),
                                  rows[:, j % 2, 1, :].rearrange("p (h t) -> p t h", h=2).unsqueeze(3).to_broadcast([P, TILES, 2, DK]),
                                  ALU.mult).then_inc(o_d.sem, 1)

            def phase_1(b, t):
                if t is not None:
                    gate(t)
                for kind, k in PHASE_1:
                    if kind == "f" and b is not None:
                        filter_step(b, k)
                    if kind == "t" and t is not None:
                        token_step(t, k)
                if t is not None:
                    token_end(t)

            def phase_2(b, f):
                if f is not None:
                    front_start(f)
                for m in range(4):
                    rotate(b, m)
                largest(b, 0)
                largest(b, 1)
                for n in range(N_TILES):
                    j, i = n // PER_PAIR, n % PER_PAIR
                    if n + 2 < N_TILES:
                        largest(b, n + 2)
                    if i == 1 and j:
                        divide(b, j - 1)
                    if i < 4 and j + 1 < PAIRS:
                        rotate(b, 4 * (j + 1) + i)
                    if f is not None and i % 4 > 0:
                        front_step(f, 2 * j + i // 4, i % 4 - 1)
                divide(b, PAIRS - 1)
                if f is not None:
                    front_end(f)
                if f is not None:
                    dve.wait_ge(da_exp.sem, da_exp.at(f))
                    dve.wait_ge(du_d.sem, du_d.at(f))
                dve.wait_ge(wo_mm.sem, wo_mm.at(b))
                dve.scalar_tensor_tensor(X3, G[4][:, :], vec("bo"), X2[:, :], ALU.add, ALU.add).then_inc(x3_d.sem, 1)
                dve.wait_ge(x3_d.sem, x3_d.at(b, 1))
                dve.tensor_tensor(X3, X3, XN2[:, :], ALU.add).then_inc(x3_d.sem, 1)

            def front(b):
                front_start(b)
                for n in range(STATES):
                    for part in range(3):
                        front_step(b, n, part)
                front_end(b)

            laps(dve, front, phase_1, phase_2)

        @block.gpsimd
        def _(pool):
            for s in by_pool:
                s.head_start(pool)
            pool.wait_ge(s_const, n_loads)
            pool.tensor_tensor(conv_w[:, TAPS - 1, :], conv_w[:, TAPS - 1, :], in_u, ALU.mult).then_inc(s_made_pool, 1)

            def front_start(b):
                pool.wait_ge(u_silu.sem, u_silu.at(b))
                pool.sem_inc(pool_passed, 1)
                for h in range(HALVES):
                    pool.tensor_scalar(Y[:, h, :], US[:, h, :], vec("D_skip", h), None, ALU.mult).then_inc(skip_y.sem, 1)
                pool.wait_ge(db_mul.sem, db_mul.at(b - 1))
                pool.wait_ge(out_st.sem, out_st.at(b - 2))
                pool.wait_ge(delta_d.sem, delta_d.at(b))
                pool.tensor_tensor(DU[:, :, :], DELTA[:, :, :], US[:, :, :], ALU.mult).then_inc(du_d.sem, 1)

            def front_step(b, n):
                if n == 0:
                    pool.wait_ge(skip_y.sem, skip_y.at(b))
                else:
                    pool.wait_ge(y_add.sem, y_add.at(b, n))
                pool.wait_ge(hc_mul.sem, hc_mul.at(b, n + 1))
                pool.tensor_tensor(Y[:, :, :], Y[:, :, :], HC[:, n % 2, :, :], ALU.add).then_inc(y_add.sem, 1)

            def front_end(b):
                pool.wait_ge(y_add.sem, y_add.at(b))
                pool.wait_ge(r_silu.sem, r_silu.at(b))
                pool.tensor_tensor(Y[:, :, :], Y[:, :, :], SR[:, :, :], ALU.mult).then_inc(y_gate.sem, 1)
                pool.wait_ge(yf_d.sem, yf_d.at(b - 1))
                pool.wait_ge(xn_done.sem, xn_done.at(b))
                pool.sem_inc(pool_passed, 1)
                pool.tensor_copy(XNB[:, :], xn).then_inc(xnb_d.sem, 1)

            def add_rotated(b, m):
                j = m // 2
                if j >= 2:
                    pool.wait_ge(sc_mm.sem, sc_mm.at(b, PER_PAIR * (j - 1)))
                pool.wait_ge(rot_d.sem, rot_d.at(b, 2 * m + 2))
                pool.tensor_tensor(QK[:, j % 2, m % 2, :], ROT, ROT2, ALU.add).then_inc(rope_d.sem, 1)

            def phase_1(b, t):
                pass

            def phase_2(b, f):
                if f is not None:
                    front_start(f)
                add_rotated(b, 0)
                add_rotated(b, 1)
                for n in range(N_TILES):
                    j, i = n // PER_PAIR, n % PER_PAIR
                    if i in (1, 3) and j + 1 < PAIRS:
                        add_rotated(b, 2 * (j + 1) + i // 2)
                    if f is not None and i % 4 == 3:
                        front_step(f, 2 * j + i // 4)
                if f is not None:
                    front_end(f)

            def front(b):
                front_start(b)
                for n in range(STATES):
                    front_step(b, n)
                front_end(b)

            laps(pool, front, phase_1, phase_2)


def lay_out(inputs):
    L0, L1 = "L0_attn_", "L1_attn_"
    g = {k: np.asarray(v) for k, v in inputs.items()}

    def stack_rows(t):
        n = t.shape[0] // P
        return t.reshape(n, P, -1).transpose(1, 0, 2).reshape(P, -1)

    swap = np.arange(HEADS * DK).reshape(-1, 2)[:, ::-1].reshape(-1)
    in_w, x_w = g[L0 + "in_proj_w"].T, g[L0 + "x_proj_w"].T
    bc = x_w[:, RANK:]
    named = {
        "in_res": in_w[:, INNER:],
        "x_bc": stack_rows(np.concatenate([bc, bc, bc], 1)), "x_dt": stack_rows(x_w[:, :RANK]),
        "out_proj": stack_rows(g[L0 + "out_proj_w"].T), "q": g[L0 + "q_w"].T, "k": g[L0 + "k_w"].T,
        "proj": g[L0 + "proj_w"].T, "fl": g[L0 + "fl_w"].T, "d1": g[L0 + "d1_w"].T, "d2": stack_rows(g[L0 + "d2_w"].T),
        "router": g["L0_ffn_Wr"], "gate": g["L1_ffn_Wg"],
        "wq": g[L1 + "wq"].T, "wq_swap": g[L1 + "wq"][swap].T, "wk": g[L1 + "wk"].T, "wk_swap": g[L1 + "wk"][swap].T,
        "wv": g[L1 + "wv"].T, "wo": stack_rows(g[L1 + "wo"].T),
    }
    weights = np.concatenate([named[k] for k in WEIGHTS], 1)
    vecs = {"dt_b": g[L0 + "dt_proj_b"], "gamma": g["L0_ffn_gamma"], "beta": g["L0_ffn_beta"],
            "bq_swap": g[L1 + "bq"][swap], "bk_swap": g[L1 + "bk"][swap]}
    for k in VECS:
        if k not in vecs:
            vecs[k] = g[(L1 if k in ("bq", "bk", "bv", "bo") else L0) + k]
    columns = np.concatenate([vecs[k].reshape(-1, P).T for k in VECS], 1)
    e_w1, e_w2 = g["L0_ffn_W1"], g["L0_ffn_W2"]
    experts = np.concatenate([
        e_w1, e_w2.reshape(EXPERTS, CHUNKS, P, D).transpose(0, 2, 1, 3).reshape(EXPERTS, P, -1),
        g["L0_ffn_b1"].reshape(EXPERTS, CHUNKS, P).transpose(0, 2, 1), g["L0_ffn_b2"][:, :, None]], 2)
    row_biases = np.concatenate([g["L0_ffn_br"], g["L1_ffn_bg"], np.arange(EXPERTS, dtype=np.float32)])
    theta = np.float32(10000.0) ** (np.arange(0, DK, 2, dtype=np.float32) / np.float32(DK))
    freqs = np.arange(S, dtype=np.float32)[:, None] * (np.float32(1.0) / theta)[None, :]
    angle = np.concatenate([freqs, freqs], -1).T
    sign = np.where(np.arange(DK) % 2 == 0, np.float32(-1), np.float32(1))[:, None]
    cos = np.tile(np.cos(angle), (2, 1)).astype(np.float32)
    sin = np.tile(np.sin(angle) * sign, (2, 1)).astype(np.float32)
    causal = np.where(np.arange(P)[None, :] > np.arange(P)[:, None], np.float32(MASKED), np.float32(0))
    row_of = (np.arange(96)[:, None] % 32 == np.arange(2 * STATES)[None, :]).astype(np.float32)
    arrays = {
        "xT": g[L0 + "input_tensor"].transpose(0, 2, 1), "weights": weights, "vecs": columns,
        "conv_rows": g[L0 + "conv_w"].T, "dt_w": g[L0 + "dt_proj_w"].T,
        "a_log": g[L0 + "A_log"].reshape(HALVES, P, STATES).transpose(1, 0, 2),
        "moe_up": g["L1_ffn_W1"].transpose(1, 0, 2), "moe_gate": g["L1_ffn_W3"].transpose(1, 0, 2),
        "moe_down": g["L1_ffn_W2"].reshape(EXPERTS, CHUNKS, P, D).transpose(2, 0, 1, 3),
        "experts": experts, "row_biases": row_biases, "cos": cos, "sin": sin,
        "identity": np.eye(P, dtype=np.float32), "causal": causal, "row_of": row_of, "in_u_w": in_w[:, :INNER],
    }
    return {k: np.ascontiguousarray(v) for k, v in arrays.items()}


def program(nc, shapes):
    args = [nc.dram_tensor(k, s, F32, kind="ExternalInput").ap() for k, s in shapes.items()]
    out = nc.dram_tensor("outT", (B, D, S), F32, kind="ExternalOutput").ap()
    build(nc, *args, out)


def kernel(**inputs):
    import concourse.bacc as bacc
    from concourse.bass_utils import run_bass_kernel_spmd

    arrays = lay_out(inputs)
    nc = bacc.Bacc("TRN2", target_bir_lowering=False, num_devices=1)
    program(nc, {k: v.shape for k, v in arrays.items()})
    r = run_bass_kernel_spmd(nc, [arrays], core_ids=[0])
    return np.ascontiguousarray(r.results[0]["outT"].transpose(0, 2, 1))
```

```python
from contextlib import ExitStack

import numpy as np
import concourse.bass as bass
from concourse import mybir

ALU = mybir.AluOpType
ACT = mybir.ActivationFunctionType
AX = mybir.AxisListType
F32 = mybir.dt.float32
BF16 = mybir.dt.bfloat16
U32 = mybir.dt.uint32
I32 = mybir.dt.int32

B, S, D = 8, 512, 128
P = 128
TILES = S // P
INNER = 2 * D
HALVES = INNER // P
STATES = 16
RANK = D // 16
TAPS = 4
PAD = TAPS - 1
HEADS, DK = 16, 64
PAIRS = HEADS // 2
EXPERTS = 8
HID = 4 * D
CHUNKS = HID // P
PICKS = 2
EXPERT_COLS = HID + CHUNKS * D + CHUNKS + 1
TINY = 1e-24
MASKED = -1e30

VECS = {}
for _name, _n in (("conv_b", 2), ("dt_b", 2), ("D_skip", 2), ("ln0_g", 1), ("ln0_b", 1), ("q_b", 1), ("k_b", 1),
                  ("proj_b", 1), ("fl_b", 1), ("lni_g", 1), ("lni_b", 1), ("ln1_g", 1), ("ln1_b", 1),
                  ("d1_b", 4), ("d2_b", 1), ("ln2_g", 1), ("ln2_b", 1), ("gamma", 1), ("beta", 1),
                  ("bq", PAIRS), ("bk", PAIRS), ("bv", PAIRS), ("bo", 1),
                  ("w_g", 1)):
    VECS[_name] = (sum(n for _, n in VECS.values()), _n)
N_VECS = sum(n for _, n in VECS.values())

WEIGHTS = {}
for _name, _n in (("in_res", INNER), ("x_bc", HALVES * 96), ("x_dt", HALVES * RANK),
                  ("out_proj", HALVES * D), ("q", D), ("k", D), ("proj", D), ("fl", D), ("d1", HID),
                  ("d2", CHUNKS * D), ("router", EXPERTS), ("gate", EXPERTS),
                  ("wq", HEADS * DK), ("wk", HEADS * DK),
                  ("wv", HEADS * DK), ("wo", PAIRS * D)):
    WEIGHTS[_name] = (sum(n for _, n in WEIGHTS.values()), _n)
N_WEIGHTS = sum(n for _, n in WEIGHTS.values())


class Signal:

    def __init__(self, ctx, nc, name, per, unit=1):
        self.sem, self.per, self.unit = ctx.enter_context(nc.semaphore(name)), per, unit

    def at(self, b, k=None):
        k = self.per if k is None else k
        return b * (self.per * self.unit) + (2 * self.per + k) * self.unit

    def head_start(self, engine):
        engine.sem_inc(self.sem, 2 * self.per * self.unit)


ROOT_STEPS = 3
ROOT_OPS = 1 + 3 * ROOT_STEPS
ROOT_GUESS = float(0x5f3759df)


class Norm:

    def __init__(self, ctx, nc, name, x, ready, eps, centred, square, stats):
        self.x, self.ready, self.eps = x, ready, eps
        self.centred, self.square, self.stats = centred, square, stats
        self.s_mean = Signal(ctx, nc, f"{name}_mean", 1)
        self.s_centred = Signal(ctx, nc, f"{name}_centred", 1)
        self.s_square = Signal(ctx, nc, f"{name}_square", 1)
        self.s_var = Signal(ctx, nc, f"{name}_var", 1)
        self.s_root = Signal(ctx, nc, f"{name}_root", 1 + ROOT_OPS)
        self.s_spread = Signal(ctx, nc, f"{name}_spread", 1)


def build(nc, xT, weights, vecs, conv_rows, dt_w, a_log, moe_up, moe_gate, moe_down, experts,
          row_biases, cos, sin, identity, causal, row_of, in_u_w, outT):
    ctx = ExitStack()
    with ctx:
        def sb(name, shape, dt=F32):
            return ctx.enter_context(nc.sbuf_tensor(name, shape, dt))

        def signal(name, per=1, unit=1):
            return Signal(ctx, nc, name, per, unit)

        W = sb("W", [P, N_WEIGHTS])
        V_ = sb("V_", [P, N_VECS])

        def w(name, lo=0, n=P):
            at = WEIGHTS[name][0] + lo
            return W[:, at:at + n]

        def vec(name, k=0):
            at = VECS[name][0] + k
            return V_[:, at:at + 1]

        conv_w = sb("conv_w", [P, TAPS, INNER])
        dt_lhs = sb("dt_lhs", [RANK, INNER])
        a_neg = sb("a_neg", [P, HALVES, STATES])
        up_w = sb("up_w", [P, EXPERTS, HID])
        gate_w = sb("gate_w", [P, EXPERTS, HID])
        down_w = sb("down_w", [P, EXPERTS, CHUNKS, D])
        cos_t, sin_t = sb("cos_t", [P, S]), sb("sin_t", [P, S])
        ident = sb("ident", [P, P])
        ident_bf = sb("ident_bf", [P, P], BF16)
        causal_bf = sb("causal_bf", [P, P], BF16)
        row_of_sb = sb("row_of_sb", [96, 2 * STATES])
        pick = sb("pick", [96, 2 * STATES, P], BF16)
        row_bias = sb("row_bias", [P, 3 * EXPERTS])
        avg = sb("avg", [P, P])
        ones = sb("ones", [P, P])
        wg_cols = sb("wg_cols", [P, P])

        X = sb("X", [P, S])
        XN = sb("XN", [P, PAD + S])
        xn = XN[:, PAD:PAD + S]
        US = sb("US", [P, HALVES, S])
        SR = sb("SR", [P, HALVES, S])
        DELTA = sb("DELTA", [P, HALVES, S])
        DU = sb("DU", [P, HALVES, S])
        DA = sb("DA", [P, 2, HALVES, S])
        D1 = sb("D1", [P, HALVES, S])
        HS = sb("HS", [P, HALVES, S])
        HC = sb("HC", [P, 2, HALVES, S])
        Y = sb("Y", [P, HALVES, S])
        S3 = sb("S3", [96, S], BF16)
        S3B = sb("S3B", [96, S], BF16)
        FT = sb("FT", [P, S])
        R1, DT = FT[0:96, :], FT[0:RANK, :]
        causal_f = D1[:, 0, 0:P]
        in_u = Y[:, 0, 0:INNER]
        M0 = sb("M0", [P, S])
        XNB = sb("XNB", [P, S])
        X2 = sb("X2", [P, S])
        XN2 = sb("XN2", [P, S])
        EW = sb("EW", [P, PICKS, EXPERT_COLS])
        REG = sb("REG", [P, 20, S])

        def reg(k):
            return REG[:, k, :]

        CX, CSQ, CR, H, QP, KP, Q, KN, LNI = (reg(k) for k in range(9))
        GK, M1, H2 = reg(9), reg(10), reg(11)
        F1 = REG[:, 12:16, :]
        L0A, XB, YF, TMP = (reg(k) for k in range(16, 20))
        M2 = QP
        V = REG[:, 0:8, :].rearrange("p (t h) s -> p t (h s)", t=TILES)
        ROT, ROT2 = reg(8), reg(9)
        QK = REG[:, 10:14, :].rearrange("p (r a) s -> p r a s", r=2)
        PR = REG[:, 14:16, :]
        PT = REG[:, 16:18, :]
        O, OT = reg(18), reg(19)
        XNF, X3 = DELTA[:, 0, :], DELTA[:, 1, :]
        gate_s = sb("gate_s", [P, TILES, 64])
        OUT = DU[:, 1, :]
        XS, SL = D1, HS
        HH = HC[:, :, :, :].rearrange("p a h s -> p (a h) s")
        ROT3 = sb("ROT3", [P, S])
        small = sb("small", [P, 64])
        stats = sb("stats", [P, 8, 3, 3 * TILES])
        gate_i = sb("gate_i", [P, TILES, 8], U32)
        pick_i = sb("pick_i", [1, 8], U32)
        maxes = sb("maxes", [P, 2, 8])
        rows = sb("rows", [P, 2, 2, 8])

        FB, FC, FM = (ctx.enter_context(nc.psum_tensor(n, [P, S], F32)) for n in ("FB", "FC", "FM"))
        G = [ctx.enter_context(nc.psum_tensor(f"G{k}", [P, S], F32)) for k in range(5)]

        n_loads, n_late = 16 * 10, 16 * 6
        dve_passed, pool_passed, sp_passed = (ctx.enter_context(nc.semaphore(f"{e}_passed")) for e in ("dve", "pool", "sp"))
        s_const = ctx.enter_context(nc.semaphore("const_loaded"))
        s_late = ctx.enter_context(nc.semaphore("late_const_loaded"))
        s_made = ctx.enter_context(nc.semaphore("const_made"))
        s_alog = ctx.enter_context(nc.semaphore("alog_exp"))
        x_in = signal("x_in", 1, 16)
        xb_in = signal("xb_in", 1, 16)
        ew_in = [signal(f"ew_in{k}", 1, 16) for k in range(PICKS)]
        out_st = signal("out_st", 1, 16)
        xn_done = signal("xn_done")
        u_mm = signal("u_mm", 2)
        r_mm = signal("r_mm", 2)
        u_silu = signal("u_silu", 2)
        r_silu = signal("r_silu", 2)
        dt_mm, bc_mm = signal("dt_mm"), signal("bc_mm")
        dt_copy = signal("dt_copy")
        bc_split = signal("bc_split", 6)
        dp_mm = signal("dp_mm", 2)
        soft = signal("soft", 4)
        relu_d = signal("relu_d", 2)
        delta_d = signal("delta_d")
        wide_d = signal("wide_d", 3)
        du_d = signal("du_d")
        skip_y = signal("skip_y", 2)
        b_mm, c_mm = signal("b_mm", STATES), signal("c_mm", STATES)
        da_exp = signal("da_exp", 2 * STATES)
        db_mul = signal("db_mul", STATES)
        scan_d = signal("scan_d", STATES)
        hc_mul = signal("hc_mul", STATES)
        y_add = signal("y_add", STATES)
        y_gate = signal("y_gate")
        m_mm = signal("m_mm")
        m0_d = signal("m0_d")
        xnb_d = signal("xnb_d")

        h_d = signal("h_d", 2)
        q_mm, k_mm = signal("q_mm"), signal("k_mm")
        qp_d, qsq_d, kp_d, ksq_d = signal("qp_d"), signal("qsq_d"), signal("kp_d"), signal("ksq_d")
        qk_ss_mm = signal("qk_ss_mm")
        qk_root = signal("qk_root", 2 + ROOT_OPS)
        qs_mm, ks_mm, is_mm = signal("qs_mm"), signal("ks_mm"), signal("is_mm")
        qn_d, kn_d = signal("qn_d"), signal("kn_d")
        q_gelu = signal("q_gelu")
        qw_mm = signal("qw_mm")
        gu_d = signal("gu_d", 2 + ROOT_OPS + 1)
        g_act = signal("g_act")
        gk_d = signal("gk_d")
        proj_mm = signal("proj_mm")
        lni_d = signal("lni_d", 2)
        hsm_d = signal("hsm_d")
        fl_mm = signal("fl_mm")
        m1_d = signal("m1_d")
        h2_d = signal("h2_d", 2)
        d1_mm, d1_gelu = signal("d1_mm", CHUNKS), signal("d1_gelu", CHUNKS)
        d2_mm = signal("d2_mm")
        m2_d = signal("m2_d")
        l0a_d = signal("l0a_d", 3)

        xm_d = signal("xm_d", 2)
        lg_mm = signal("lg_mm")
        rt_d = signal("rt_d", 10)
        rt_act = signal("rt_act", 2)
        wb_mm = signal("wb_mm")
        wb_d = signal("wb_d")
        idx_rd = signal("idx_rd")
        e1_mm, e1_gelu = signal("e1_mm", PICKS * CHUNKS), signal("e1_gelu", PICKS * CHUNKS)
        e2_mm = signal("e2_mm", 2 * PICKS)
        yf_d = signal("yf_d", 5)
        l0f_d = signal("l0f_d", 2)
        x2_d = signal("x2_d")
        xn2_d = signal("xn2_d")

        v_mm, v_copy = signal("v_mm", 2 * TILES), signal("v_copy", 2 * TILES)
        pj_mm = signal("pj_mm", 2 * PAIRS)
        rot_d = signal("rot_d", 2 * 2 * PAIRS)
        rope_d = signal("rope_d", 2 * 2 * PAIRS)
        biased = signal("biased", 2 * PAIRS)
        sc_mm = signal("sc_mm", HEADS * TILES)
        nm_d = signal("nm_d", HEADS * TILES)
        p_exp = signal("p_exp", HEADS * TILES)
        pt_mm = signal("pt_mm", HEADS * TILES)
        pt_copy = signal("pt_copy", HEADS * TILES)
        pv_mm = signal("pv_mm", HEADS * TILES)
        rec_d = signal("rec_d", PAIRS)
        o_d = signal("o_d", PAIRS)
        ot_mm = signal("ot_mm", PAIRS)
        ot_copy = signal("ot_copy", PAIRS)
        wo_mm = signal("wo_mm", PAIRS)
        x3_d = signal("x3_d", 2)
        xnf_d = signal("xnf_d")

        gl_mm = signal("gl_mm")
        gt_d = signal("gt_d", 13)
        gt_act = signal("gt_act")
        wt_mm = signal("wt_mm", EXPERTS)
        xs_d = signal("xs_d", EXPERTS)
        ug_mm = signal("ug_mm", EXPERTS * CHUNKS)
        sl_act = signal("sl_act", EXPERTS * CHUNKS)
        sx_d = signal("sx_d", EXPERTS * CHUNKS)
        hh_d = signal("hh_d", EXPERTS * CHUNKS)
        dn_mm = signal("dn_mm", EXPERTS * CHUNKS)
        out_d = signal("out_d")

        n1 = Norm(ctx, nc, "norm_x", X[:, :], x_in, 1e-5, xn, FT[:, :], stats[:, 0, :, 0:TILES])
        n0 = Norm(ctx, nc, "norm_0", M0[:, :], m0_d, 1e-12, CX, CSQ, stats[:, 1, :, 0:TILES])
        ni = Norm(ctx, nc, "norm_i", H, h_d, 1e-12, CX, CSQ, None)
        n_1 = Norm(ctx, nc, "norm_1", M1, m1_d, 1e-12, CX, CSQ, stats[:, 2, :, 0:TILES])
        n_2 = Norm(ctx, nc, "norm_2", M2, m2_d, 1e-12, CX, CSQ, stats[:, 3, :, 0:TILES])
        nf = Norm(ctx, nc, "norm_f", YF, yf_d, 1e-5, CX, CSQ, stats[:, 4, :, 0:TILES])
        nx = Norm(ctx, nc, "norm_x2", X2[:, :], x2_d, 1e-5, CX, CSQ, stats[:, 5, :, 0:TILES])
        qk_stats = stats[:, 6, :, :]
        g_stats = stats[:, 7, :, 0:1]
        norms = (n1, n0, ni, n_1, n_2, nf, nx)

        by_pe = [u_mm, r_mm, dt_mm, bc_mm, dp_mm, b_mm, c_mm, m_mm, q_mm, k_mm, qk_ss_mm, qs_mm, ks_mm, is_mm, qw_mm, proj_mm, fl_mm,
                 d1_mm, d2_mm, lg_mm, wb_mm, e1_mm, e2_mm, v_mm, pj_mm, sc_mm, pt_mm, pv_mm, ot_mm, wo_mm, gl_mm,
                 wt_mm, ug_mm, dn_mm] + [s for n in norms for s in (n.s_mean, n.s_var, n.s_spread)]
        by_act = [biased, u_silu, r_silu, soft, da_exp, qsq_d, ksq_d, q_gelu, g_act, d1_gelu, rt_act,
                  e1_gelu, v_copy, p_exp, pt_copy, ot_copy, gt_act, sl_act, xnf_d] + [n.s_square for n in norms]
        by_dve = [qk_root, kn_d, qp_d, kp_d, xn_done, dt_copy, bc_split, relu_d, delta_d, wide_d, db_mul, scan_d, hc_mul, m0_d, h_d, qn_d, gu_d,
                  gk_d, lni_d, hsm_d, m1_d, h2_d, m2_d, l0a_d, xm_d, rt_d, wb_d, yf_d, l0f_d, x2_d, xn2_d, rot_d,
                  nm_d, rec_d, o_d, x3_d, gt_d, xs_d, sx_d, hh_d, out_d] + [s for n in norms for s in (n.s_centred, n.s_root)]
        by_pool = [du_d, skip_y, y_add, y_gate, xnb_d, rope_d]
        by_sp = [x_in, xb_in, *ew_in, out_st, idx_rd]

        F_STEPS, T_STEPS = 29, EXPERTS * CHUNKS
        X_AFTER = {0: 1, 1: 2, 2: 3, 6: 4, 7: 5, 8: 6, 10: 7, 11: 8}
        T_USES = [("w", 0)]
        for e in range(EXPERTS):
            T_USES += [("c", CHUNKS * e + c) for c in range(CHUNKS)]
            if e + 1 < EXPERTS:
                T_USES.insert(-1, ("w", e + 1))
        T_PAIR = {use: 2 * (u % 2) for u, use in enumerate(T_USES)}
        weight = [0.5 if 18 <= p <= 21 else 1.1 for p in range(F_STEPS)]

        def t_share(p):
            return 2 + round(sum(weight[:p]) / sum(weight) * (len(T_USES) - 2))

        PHASE_1 = [("o", 0), ("x", 0), ("t", 0), ("f", -1), ("t", 1)]
        for p in range(F_STEPS):
            PHASE_1.append(("f", p))
            PHASE_1 += [("t", u) for u in range(t_share(p), t_share(p + 1))]
            if p in X_AFTER:
                PHASE_1.append(("x", X_AFTER[p]))
        F_USES = {}
        for key, of, bank, read in (
                ("mean_x", "f", FM, (n1.s_centred, 1)), ("mamba", "b", FC, (m0_d, 1)),
                ("mean_0", "b", FB, (n0.s_centred, 1)),
                ("var_x", "f", FM, (n1.s_root, 1)), ("var_0", "b", FC, (rt_d, 1)),
                ("spread_x", "f", FM, (xn_done, 1)), ("spread_0", "b", FB, (h_d, 1)),
                ("u0", "f", FM, (u_silu, 1)), ("q", "b", FC, (qp_d, 1)), ("k", "b", FB, (kp_d, 1)),
                ("mean_i", "b", FM, (ni.s_centred, 1)), ("ss", "b", FM, (qk_root, 2)),
                ("spread_q", "b", FC, (qn_d, 1)), ("spread_k", "b", FB, (kn_d, 1)), ("spread_i", "b", FM, (lni_d, 1)),
                ("qw", "b", FC, (g_act, 1)), ("wb", "b", FB, (wb_d, 1)), ("u1", "f", FM, (u_silu, 2)),
                ("proj", "b", FB, (hsm_d, 1)), ("r0", "f", FM, (r_silu, 1)), ("fl", "b", FC, (m1_d, 1)),
                ("r1", "f", FM, (r_silu, 2)), ("mean_1", "b", FB, (n_1.s_centred, 1)),
                ("var_1", "b", FC, (n_1.s_root, 1)), ("bc", "f", FM, (bc_split, 2)), ("spread_1", "b", FB, (h2_d, 1)),
                ("dt", "f", FM, (dt_copy, 1)), ("d1_0", "b", FB, (d1_gelu, 1)), ("d1_1", "b", FC, (d1_gelu, 2)),
                ("d1_2", "b", FB, (d1_gelu, 3)), ("d1_3", "b", FC, (d1_gelu, 4)), ("d2", "b", FM, (m2_d, 1)),
                ("mean_2", "b", FB, (n_2.s_centred, 1)), ("var_2", "b", FC, (n_2.s_root, 1)),
                ("spread_2", "b", FB, (l0a_d, 1)),
                ("up0", "b", FC, (e1_gelu, 1)), ("up1", "b", FB, (e1_gelu, 2)), ("up2", "b", FC, (e1_gelu, 3)),
                ("up3", "b", FB, (e1_gelu, 4)), ("down0", "b", FM, (yf_d, 4)), ("up4", "b", FC, (e1_gelu, 5)),
                ("up5", "b", FB, (e1_gelu, 6)), ("up6", "b", FC, (e1_gelu, 7)), ("up7", "b", FB, (e1_gelu, 8)),
                ("down1", "b", FM, (yf_d, 5)), ("mean_f", "b", FB, (nf.s_centred, 1)), ("var_f", "b", FC, (nf.s_root, 1)),
                ("spread_f", "b", FB, (l0f_d, 1)), ("mean_n", "b", FC, (nx.s_centred, 1)),
                ("var_n", "b", FB, (nx.s_root, 1)), ("spread_n", "b", FC, (xn2_d, 1))):
            F_USES[key] = (of, bank, read)
        F_BANK = {key: bank for key, (of, bank, read) in F_USES.items()}
        n1.key, n0.key, ni.key, n_1.key, n_2.key, nf.key, nx.key = "x0i12fn"

        def read_before(key, of):
            keys = list(F_USES)
            for k in reversed(keys[:keys.index(key)]):
                if F_USES[k][0] in of and F_USES[k][1] is F_USES[key][1]:
                    return F_USES[k][0], F_USES[k][2]
            return None

        N_TILES = HEADS * TILES
        PER_PAIR = 2 * TILES
        AHEAD = 3
        RING = [G[0], G[1], FM]
        V_BANK = [G[2], G[3], G[0], FM]
        OUT_AT = 2
        PROJECT_AT = (0, 2)
        turn_free = {}
        ring_bank, ring_free = {}, {}
        uses = []

        def note_use(key, freed_by):
            ring_bank[key] = RING[len(uses) % len(RING)]
            ring_free[key] = uses[-len(RING)] if len(uses) >= len(RING) else None
            uses.append(freed_by)

        for m in range(2):
            note_use(("proj", m), (biased, m + 1))
        for n in range(AHEAD):
            note_use(("score", n), (p_exp, n + 1))
        for n in range(N_TILES):
            if n % PER_PAIR in PROJECT_AT and n // PER_PAIR + 1 < PAIRS:
                m = 2 * (n // PER_PAIR + 1) + PROJECT_AT.index(n % PER_PAIR)
                note_use(("proj", m), (biased, m + 1))
            if n + AHEAD < N_TILES:
                note_use(("score", n + AHEAD), (p_exp, n + AHEAD + 1))
            if n % PER_PAIR == OUT_AT and n > PER_PAIR:
                note_use(("out", n // PER_PAIR - 1), (ot_copy, n // PER_PAIR))
        note_use(("out", PAIRS - 1), (ot_copy, PAIRS))

        block = ctx.enter_context(nc.Block())

        def laps(eng, front, phase_1, phase_2, late=None):
            front(0)
            phase_1(0, None, 1)
            if late is not None:
                late()
            phase_2(0, 1)
            with eng.Fori(1, B - 1) as b:
                phase_1(b, b - 1, b + 1)
                phase_2(b, b + 1)
            phase_1(B - 1, B - 2, None)
            phase_2(B - 1, None)
            phase_1(None, B - 1, None)

        def each_step(b, t, f, filter_step, token_use, front_start, attention_end):
            for kind, k in PHASE_1:
                if kind == "f" and b is not None:
                    filter_step(b, k, f)
                if kind == "t" and t is not None:
                    token_use(t, *T_USES[k], b)
                if kind == "o" and t is not None:
                    attention_end(t, b)
                if kind == "x" and f is not None:
                    front_start(f, k, b)

        @block.sync
        def _(sp):
            for s in by_sp:
                s.head_start(sp)
            late = WEIGHTS["wq"][0]
            for dst, src in ((W[:, 0:late], weights[:, 0:late]), (V_[:, :], vecs), (dt_lhs[:, :], dt_w), (a_neg[:, :, :], a_log),
                             (ident[:, :], identity), (causal_f, causal), (row_of_sb[:, :], row_of),
                             (row_bias[:, :], row_biases.partition_broadcast(P)),
                             (conv_w[:, :, :], conv_rows.partition_broadcast(P)),
                             (in_u, in_u_w)):
                sp.dma_start(dst, src).then_inc(s_const, 16)

            def load_x(b):
                sp.wait_ge(n1.s_centred.sem, n1.s_centred.at(b - 1))
                sp.dma_start(X[:, :], xT[b]).then_inc(x_in.sem, 16)

            def phase_1(b, t, f):
                if f is not None:
                    load_x(f)
                if b is not None:
                    sp.wait_ge(wo_mm.sem, wo_mm.at(b - 1))
                    sp.dma_start(XB, xT[b]).then_inc(xb_in.sem, 16)
                    for k in range(PICKS):
                        sp.wait_ge(e2_mm.sem, e2_mm.at(b - 1))
                        sp.sem_inc(sp_passed, 1)
                        sp.wait_ge(x2_d.sem, x2_d.at(b - 1))
                        sp.sem_inc(sp_passed, 1)
                        sp.wait_ge(rt_d.sem, rt_d.at(b, 7))
                        sp.sem_inc(sp_passed, 1)
                        e = sp.value_load(pick_i[0:1, k:k + 1], min_val=0, max_val=EXPERTS - 1)
                        sp.dma_start(EW[:, k, :], experts[bass.ds(e, 1), :, :].rearrange("a p c -> (a p) c")).then_inc(ew_in[k].sem, 16)
                    sp.sem_inc(idx_rd.sem, 1)
                if t is not None:
                    sp.wait_ge(out_d.sem, out_d.at(t))
                    sp.dma_start(outT[t], OUT).then_inc(out_st.sem, 16)

            def phase_2(b, f):
                pass

            def front(b):
                load_x(b)
                for dst, src in ((W[:, late:], weights[:, late:]), (cos_t[:, :], cos), (sin_t[:, :], sin), (up_w[:, :, :], moe_up),
                                 (gate_w[:, :, :], moe_gate), (down_w[:, :, :, :], moe_down)):
                    sp.dma_start(dst, src).then_inc(s_late, 16)

            laps(sp, front, phase_1, phase_2)
            sp.wait_ge(out_st.sem, out_st.at(B - 1))

        @block.tensor
        def _(pe):
            for s in by_pe:
                s.head_start(pe)
            pe.wait_ge(s_const, n_loads)
            pe.wait_ge(s_made, 13)

            def bank(key, b, f):
                before = read_before(key, ("b" if b is not None else "") + ("f" if f is not None else ""))
                if before is None:
                    s = b if b is not None else f - 1
                    if F_BANK[key] is FM:
                        pe.wait_ge(p_exp.sem, p_exp.at(s - 1))
                    else:
                        pe.wait_ge(hc_mul.sem, hc_mul.at(s))
                else:
                    of, (read, k) = before
                    pe.wait_ge(read.sem, read.at(b if of == "b" else f, k))
                return F_BANK[key]

            def mean(n, of, b, f):
                out = bank("mean_" + n.key, b, f)
                pe.wait_ge(n.ready.sem, n.ready.at(of))
                pe.matmul(out[:, :], avg[:, :], n.x, start=True, stop=True).then_inc(n.s_mean.sem, 1)

            def token_sums(out, col, x, weights):
                for t in range(TILES):
                    mm = pe.matmul(out[:, col + t:col + t + 1], x[:, t * P:(t + 1) * P], weights[:, 0:1], start=True, stop=True)
                return mm

            def spread(out, columns, t0=0):
                for t in range(TILES):
                    mm = pe.matmul(out[:, t * P:(t + 1) * P], columns[:, t0 + t:t0 + t + 1].to_broadcast([P, P]), ident[:, :],
                                   start=True, stop=True)
                return mm

            def var(n, of, b, f):
                out = bank("var_" + n.key, b, f)
                pe.wait_ge(n.s_square.sem, n.s_square.at(of))
                token_sums(out, 0, n.square, avg).then_inc(n.s_var.sem, 1)

            def spread_root(n, of, b, f):
                out = bank("spread_" + n.key, b, f)
                pe.wait_ge(n.s_root.sem, n.s_root.at(of))
                spread(out, n.stats[:, 1, :]).then_inc(n.s_spread.sem, 1)

            def front_start(f, p, b):
                if p == 0:
                    mean(n1, f, b, f)
                elif p == 1:
                    var(n1, f, b, f)
                elif p == 2:
                    spread_root(n1, f, b, f)
                elif p in (3, 4):
                    h = p - 3
                    out = bank(f"u{h}", b, f)
                    pe.wait_ge(xn_done.sem, xn_done.at(f))
                    for tap in range(TAPS):
                        mm = pe.matmul(out[:, :], conv_w[:, tap, h * P:(h + 1) * P], XN[:, tap:tap + S],
                                       start=tap == 0, stop=tap == TAPS - 1)
                    mm.then_inc(u_mm.sem, 1)
                elif p in (5, 6):
                    h = p - 5
                    out = bank(f"r{h}", b, f)
                    pe.matmul(out[:, :], w("in_res", h * P), xn, start=True, stop=True).then_inc(r_mm.sem, 1)
                elif p == 7:
                    out = bank("bc", b, f)
                    pe.wait_ge(u_silu.sem, u_silu.at(f))
                    for h in range(HALVES):
                        mm = pe.matmul(out[0:96, :], w("x_bc", h * 96, 96), US[:, h, :], start=h == 0, stop=h == 1)
                    mm.then_inc(bc_mm.sem, 1)
                elif p == 8:
                    out = bank("dt", b, f)
                    for h in range(HALVES):
                        mm = pe.matmul(out[0:RANK, :], w("x_dt", h * RANK, RANK), US[:, h, :], start=h == 0, stop=h == 1)
                    mm.then_inc(dt_mm.sem, 1)

            def front_delta(f, b):
                pe.wait_ge(dt_copy.sem, dt_copy.at(f))
                if b is not None:
                    pe.wait_ge(nx.s_root.sem, nx.s_root.at(b, 1))
                pe.matmul(FB[:, :], dt_lhs[:, 0:P], DT, start=True, stop=True).then_inc(dp_mm.sem, 1)
                if b is not None:
                    pe.wait_ge(xn2_d.sem, xn2_d.at(b))
                pe.matmul(FC[:, :], dt_lhs[:, P:INNER], DT, start=True, stop=True).then_inc(dp_mm.sem, 1)

            def front_b(b, n):
                if n:
                    pe.wait_ge(db_mul.sem, db_mul.at(b, n))
                else:
                    pe.wait_ge(bc_split.sem, bc_split.at(b))
                    pe.wait_ge(relu_d.sem, relu_d.at(b, 1))
                pe.matmul(FB[:, :], pick[:, n, :], S3[:, :], start=True, stop=True).then_inc(b_mm.sem, 1)

            def front_c(b, n):
                if n:
                    pe.wait_ge(hc_mul.sem, hc_mul.at(b, n))
                else:
                    pe.wait_ge(relu_d.sem, relu_d.at(b))
                pe.matmul(FC[:, :], pick[:, STATES + n, :], S3[:, :], start=True, stop=True).then_inc(c_mm.sem, 1)

            def filter_step(b, p, f):
                if p == -1:
                    out = bank("mamba", b, f)
                    pe.wait_ge(y_gate.sem, y_gate.at(b))
                    for h in range(HALVES):
                        mm = pe.matmul(out[:, :], w("out_proj", h * D), Y[:, h, :], start=h == 0, stop=h == 1)
                    mm.then_inc(m_mm.sem, 1)
                elif p == 0:
                    mean(n0, b, b, f)
                elif p == 1:
                    out = bank("var_0", b, f)
                    pe.wait_ge(xm_d.sem, xm_d.at(b))
                    pe.matmul(out[0:1, 16:16 + EXPERTS], small[:, 0:1], w("router", 0, EXPERTS), start=True, stop=True).then_inc(lg_mm.sem, 1)
                    var(n0, b, b, f)
                elif p == 2:
                    spread_root(n0, b, b, f)
                elif p == 3:
                    q_bank, k_bank = bank("q", b, f), bank("k", b, f)
                    pe.wait_ge(h_d.sem, h_d.at(b))
                    pe.matmul(q_bank[:, :], w("q"), H, start=True, stop=True).then_inc(q_mm.sem, 1)
                    pe.matmul(k_bank[:, :], w("k"), H, start=True, stop=True).then_inc(k_mm.sem, 1)
                    mean(ni, b, b, f)
                elif p == 4:
                    out = bank("ss", b, f)
                    pe.wait_ge(qsq_d.sem, qsq_d.at(b))
                    token_sums(out, 0, TMP, ones)
                    pe.wait_ge(ksq_d.sem, ksq_d.at(b))
                    token_sums(out, TILES, M1, ones)
                    pe.wait_ge(ni.s_square.sem, ni.s_square.at(b))
                    token_sums(out, 2 * TILES, CSQ, avg).then_inc(qk_ss_mm.sem, 1)
                elif p == 5:
                    pe.wait_ge(qk_root.sem, qk_root.at(b))
                    for k, (key, done) in enumerate((("spread_q", qs_mm), ("spread_k", ks_mm), ("spread_i", is_mm))):
                        out = bank(key, b, f)
                        spread(out, qk_stats[:, 1, :], k * TILES).then_inc(done.sem, 1)
                elif p == 6:
                    out = bank("wb", b, f)
                    pe.wait_ge(rt_d.sem, rt_d.at(b, 10))
                    pe.matmul(out[:, 0:2], ones[0:1, :], small[0:1, 40:42], start=True, stop=True).then_inc(wb_mm.sem, 1)
                    out = bank("qw", b, f)
                    pe.wait_ge(q_gelu.sem, q_gelu.at(b))
                    pe.matmul(out[:, :], wg_cols[:, :], Q, start=True, stop=True).then_inc(qw_mm.sem, 1)
                elif p == 7:
                    out = bank("proj", b, f)
                    pe.wait_ge(gk_d.sem, gk_d.at(b))
                    pe.matmul(out[:, :], w("proj"), GK, start=True, stop=True).then_inc(proj_mm.sem, 1)
                elif p == 8:
                    out = bank("fl", b, f)
                    pe.wait_ge(hsm_d.sem, hsm_d.at(b))
                    pe.matmul(out[:, :], w("fl"), TMP, start=True, stop=True).then_inc(fl_mm.sem, 1)
                elif p in (9, 15, 23, 26):
                    mean({9: n_1, 15: n_2, 23: nf, 26: nx}[p], b, b, f)
                elif p in (10, 16, 24, 27):
                    var({10: n_1, 16: n_2, 24: nf, 27: nx}[p], b, b, f)
                elif p in (11, 17, 25, 28):
                    spread_root({11: n_1, 17: n_2, 25: nf, 28: nx}[p], b, b, f)
                elif p in (12, 13):
                    for c in (2 * (p - 12), 2 * (p - 12) + 1):
                        out = bank(f"d1_{c}", b, f)
                        pe.wait_ge(h2_d.sem, h2_d.at(b))
                        pe.matmul(out[:, :], w("d1", c * P), H2, start=True, stop=True).then_inc(d1_mm.sem, 1)
                    if p == 13:
                        out = bank("d2", b, f)
                        for c in range(2):
                            pe.wait_ge(d1_gelu.sem, d1_gelu.at(b, c + 1))
                            pe.matmul(out[:, :], w("d2", c * D), F1[:, c, :], start=c == 0, stop=False)
                elif p == 14:
                    for c in range(2, CHUNKS):
                        pe.wait_ge(d1_gelu.sem, d1_gelu.at(b, c + 1))
                        mm = pe.matmul(F_BANK["d2"][:, :], w("d2", c * D), F1[:, c, :], start=False, stop=c == CHUNKS - 1)
                    mm.then_inc(d2_mm.sem, 1)
                elif p == 18:
                    expert_up(b, 0, 0, f)
                elif p == 19:
                    expert_up(b, 0, 2, f)
                    expert_down(b, 0, 0, f)
                elif p == 20:
                    expert_up(b, 1, 0, f)
                    expert_down(b, 0, 2, f)
                elif p == 21:
                    expert_up(b, 1, 2, f)
                    expert_down(b, 1, 0, f)
                elif p == 22:
                    expert_down(b, 1, 2, f)

            def expert_up(b, k, c0, f):
                pe.wait_ge(ew_in[k].sem, ew_in[k].at(b))
                for c in (c0, c0 + 1):
                    out = bank(f"up{k * CHUNKS + c}", b, f)
                    pe.matmul(out[:, :], EW[:, k, c * P:(c + 1) * P], XNB[:, :], start=True, stop=True).then_inc(e1_mm.sem, 1)

            def expert_down(b, k, c0, f):
                out = bank(f"down{k}", b, f) if c0 == 0 else F_BANK[f"down{k}"]
                for c in (c0, c0 + 1):
                    pe.wait_ge(e1_gelu.sem, e1_gelu.at(b, k * CHUNKS + c + 1))
                    mm = pe.matmul(out[:, :], EW[:, k, HID + c * D:HID + (c + 1) * D], F1[:, c, :],
                                   start=c == 0, stop=c == CHUNKS - 1)
                mm.then_inc(e2_mm.sem, 1)

            def token_use(b, kind, k, following):
                use = T_USES.index((kind, k))
                if use >= 2:
                    before, m = T_USES[use - 2]
                    read = xs_d if before == "w" else hh_d
                    pe.wait_ge(read.sem, read.at(b, m + 1))
                g = T_PAIR[(kind, k)]
                if kind == "w":
                    spread(G[g], gate_s[:, :, 48 + k]).then_inc(wt_mm.sem, 1)
                    return
                e, c = k // CHUNKS, k % CHUNKS
                if c == 0:
                    pe.wait_ge(xs_d.sem, xs_d.at(b, e + 1))
                pe.matmul(G[g][:, :], up_w[:, e, c * P:(c + 1) * P], XS[:, e % 2, :], start=True, stop=True)
                pe.matmul(G[g + 1][:, :], gate_w[:, e, c * P:(c + 1) * P], XS[:, e % 2, :], start=True, stop=True).then_inc(ug_mm.sem, 1)
                if k >= 2:
                    down(b, k - 2)

            def down(b, n):
                if n == 0:
                    pe.wait_ge(x3_d.sem, x3_d.at(b))
                pe.wait_ge(hh_d.sem, hh_d.at(b, n + 1))
                pe.matmul(G[4][:, :], down_w[:, n // CHUNKS, n % CHUNKS, :], HH[:, n % 4, :], start=n == 0, stop=n == T_STEPS - 1,
                          skip_group_check=True).then_inc(dn_mm.sem, 1)

            def gate(b):
                pe.wait_ge(out_d.sem, out_d.at(b - 1))
                pe.wait_ge(xn2_d.sem, xn2_d.at(b))
                for t in range(TILES):
                    mm = pe.matmul(G[4][:, t * 8:(t + 1) * 8], XN2[:, t * P:(t + 1) * P], w("gate", 0, EXPERTS), start=True, stop=True)
                mm.then_inc(gl_mm.sem, 1)

            def values_in(b):
                for n in range(2 * TILES):
                    if n >= len(V_BANK):
                        pe.wait_ge(v_copy.sem, v_copy.at(b, n + 1 - len(V_BANK)))
                    elif n == 2:
                        pe.wait_ge(biased.sem, biased.at(b, 1))
                    t, c = n // 2, n % 2
                    pe.matmul(V_BANK[n % len(V_BANK)][:, :], XN2[:, t * P:(t + 1) * P], w("wv", c * S, S), start=True, stop=True).then_inc(v_mm.sem, 1)

            def take(b, key):
                freed = ring_free[key]
                if freed is not None:
                    pe.wait_ge(freed[0].sem, freed[0].at(b, freed[1]))
                return ring_bank[key]

            def project(b, m):
                j, name = m // 2, ("wq", "wk")[m % 2]
                bank = take(b, ("proj", m))
                pe.matmul(bank[:, :], w(name, j * P), XN2[:, :], start=True, stop=True).then_inc(pj_mm.sem, 1)

            def score(b, n):
                j, i = n // PER_PAIR, n % PER_PAIR
                t, lo = i % TILES, (i // TILES) * DK
                width = (t + 1) * P
                bank = take(b, ("score", n))
                if i == 0:
                    pe.wait_ge(rope_d.sem, rope_d.at(b, 4 * j + 4))
                pe.matmul(bank[:, 0:width], QK[lo:lo + DK, j % 2, 0, t * P:(t + 1) * P],
                          QK[lo:lo + DK, j % 2, 1, 0:width], start=True, stop=False)
                pe.matmul(bank[:, t * P:width], ident_bf[:, :], causal_bf[:, :], start=False, stop=True).then_inc(sc_mm.sem, 1)

            def turn(b, n):
                t = n % TILES
                pe.wait_ge(p_exp.sem, p_exp.at(b, n + 1))
                if n:
                    pe.wait_ge(pt_copy.sem, pt_copy.at(b, n))
                for c in range(t + 1):
                    mm = pe.transpose(G[2][:, c * P:(c + 1) * P], PR[:, n % 2, c * P:(c + 1) * P], ident[:, :])
                mm.then_inc(pt_mm.sem, 1)

            def weigh_values(b, n):
                j, i = n // PER_PAIR, n % PER_PAIR
                t, h = i % TILES, i // TILES
                pe.wait_ge(pt_copy.sem, pt_copy.at(b, n + 1))
                if i == 0 and j:
                    pe.wait_ge(o_d.sem, o_d.at(b, j))
                col = t * P + h * DK
                for c in range(t + 1):
                    mm = pe.matmul(G[3][:, col:col + DK], PT[:, n % 2, c * P:(c + 1) * P],
                                   V[:, c, j * P + h * DK:j * P + (h + 1) * DK], start=c == 0, stop=c == t)
                mm.then_inc(pv_mm.sem, 1)

            def turn_out(b, j):
                pe.wait_ge(o_d.sem, o_d.at(b, j + 1))
                bank = take(b, ("out", j))
                for t in range(TILES):
                    mm = pe.transpose(bank[:, t * P:(t + 1) * P], O[:, t * P:(t + 1) * P], ident[:, :])
                mm.then_inc(ot_mm.sem, 1)

            def project_out(b, j):
                if j == 0:
                    pe.wait_ge(gt_d.sem, gt_d.at(b, 1))
                pe.wait_ge(ot_copy.sem, ot_copy.at(b, j + 1))
                pe.matmul(G[4][:, :], w("wo", j * D), OT, start=j == 0, stop=j == PAIRS - 1,
                          skip_group_check=True).then_inc(wo_mm.sem, 1)

            def attention_end(b, following):
                project_out(b, PAIRS - 1)
                pe.wait_ge(p_exp.sem, p_exp.at(b))
                pe.wait_ge(ot_copy.sem, ot_copy.at(b))
                pe.wait_ge(gt_d.sem, gt_d.at(b))

            def phase_1(b, t, f):
                each_step(b, t, f, filter_step, token_use, front_start, attention_end)
                if t is not None:
                    down(t, T_STEPS - 2)
                    down(t, T_STEPS - 1)

            def phase_2(b, f):
                if f is not None:
                    front_delta(f, b)
                pe.wait_ge(xn2_d.sem, xn2_d.at(b))
                for m in range(2):
                    project(b, m)
                gate(b)
                values_in(b)
                pe.wait_ge(v_copy.sem, v_copy.at(b))
                pe.wait_ge(yf_d.sem, yf_d.at(b))
                for n in range(AHEAD):
                    score(b, n)
                for n in range(N_TILES):
                    j, i = n // PER_PAIR, n % PER_PAIR
                    turn(b, n)
                    if i == OUT_AT + 3 and j:
                        project_out(b, j - 1)
                    if f is not None and i % 4 == 0:
                        front_b(f, 2 * j + i // 4)
                    if f is not None and i % 4 == 1:
                        front_c(f, 2 * j + i // 4)
                    if i in PROJECT_AT and j + 1 < PAIRS:
                        project(b, 2 * (j + 1) + PROJECT_AT.index(i))
                    if n + AHEAD < N_TILES:
                        score(b, n + AHEAD)
                    if i == OUT_AT and j:
                        turn_out(b, j - 1)
                    if n:
                        weigh_values(b, n - 1)
                weigh_values(b, N_TILES - 1)
                turn_out(b, PAIRS - 1)

            def front(b):
                for p in range(9):
                    front_start(b, p, None)
                front_delta(b, None)
                for n in range(STATES):
                    front_b(b, n)
                    front_c(b, n)

            def late():
                pe.wait_ge(s_late, n_late)
                pe.wait_ge(s_made, 15)

            laps(pe, front, phase_1, phase_2, late)

        @block.scalar
        def _(act):
            for s in by_act:
                s.head_start(act)
            act.wait_ge(s_const, n_loads)
            act.activation(a_neg[:, :, :], a_neg[:, :, :], ACT.Exp).then_inc(s_alog, 1)
            act.wait_ge(s_made, 13)

            def square(n, b):
                act.wait_ge(n.s_centred.sem, n.s_centred.at(b))
                act.activation(n.square, n.centred, ACT.Square).then_inc(n.s_square.sem, 1)

            def front_start(f, p, b):
                if p == 0:
                    act.wait_ge(dp_mm.sem, dp_mm.at(f - 1))
                    square(n1, f)
                elif p in (3, 4):
                    h = p - 3
                    if h == 0:
                        act.wait_ge(y_gate.sem, y_gate.at(f - 1))
                    act.wait_ge(u_mm.sem, u_mm.at(f, h + 1))
                    act.activation(US[:, h, :], F_BANK[f"u{h}"][:, :], ACT.Silu, bias=vec("conv_b", h)).then_inc(u_silu.sem, 1)
                elif p in (5, 6):
                    h = p - 5
                    act.wait_ge(r_mm.sem, r_mm.at(f, h + 1))
                    act.activation(SR[:, h, :], F_BANK[f"r{h}"][:, :], ACT.Silu).then_inc(r_silu.sem, 1)

            def softplus(b, part):
                if part == 0:
                    act.wait_ge(scan_d.sem, scan_d.at(b - 1))
                    act.wait_ge(ug_mm.sem, ug_mm.at(b - 2))
                    for h, bank in ((0, FB), (1, FC)):
                        act.wait_ge(dp_mm.sem, dp_mm.at(b, h + 1))
                        act.activation(D1[:, h, :], bank[:, :], ACT.Abs, bias=vec("dt_b", h)).then_inc(soft.sem, 1)
                    act.wait_ge(soft.sem, soft.at(b, 2))
                    act.activation(D1[:, :, :], D1[:, :, :], ACT.Exp, scale=-1.0).then_inc(soft.sem, 1)
                else:
                    act.wait_ge(wide_d.sem, wide_d.at(b, 2))
                    act.activation(DELTA[:, :, :], DELTA[:, :, :], ACT.Ln).then_inc(soft.sem, 1)

            def front_step(b, n, halves=(0, 1)):
                if n == 0 and halves[0] == 0:
                    act.wait_ge(delta_d.sem, delta_d.at(b))
                if n >= 2 and halves[0] == 0:
                    act.wait_ge(scan_d.sem, scan_d.at(b, n - 1))
                for h in halves:
                    act.activation(DA[:, n % 2, h, 1:S], DELTA[:, h, 1:S], ACT.Exp,
                                   scale=a_neg[:, h, n:n + 1]).then_inc(da_exp.sem, 1)

            def filter_step(b, p, f):
                if p == 0:
                    act.wait_ge(wo_mm.sem, wo_mm.at(b - 1))
                    square(n0, b)
                elif p == 3:
                    act.wait_ge(q_mm.sem, q_mm.at(b))
                    act.activation(TMP, F_BANK["q"][:, :], ACT.Square, bias=vec("q_b")).then_inc(qsq_d.sem, 1)
                    act.wait_ge(k_mm.sem, k_mm.at(b))
                    act.activation(M1, F_BANK["k"][:, :], ACT.Square, bias=vec("k_b")).then_inc(ksq_d.sem, 1)
                    square(ni, b)
                elif p == 2:
                    act.wait_ge(rt_d.sem, rt_d.at(b, 3))
                    act.activation(small[0:1, 16:24], small[0:1, 8:16], ACT.Exp, bias=small[0:1, 5:6], accum_out=small[0:1, 6:7]).then_inc(rt_act.sem, 1)
                elif p == 4:
                    act.wait_ge(rt_d.sem, rt_d.at(b, 8))
                    act.activation(small[0:1, 38:40], small[0:1, 24:26], ACT.Exp, bias=small[0:1, 7:8], accum_out=small[0:1, 36:37]).then_inc(rt_act.sem, 1)
                elif p == 5:
                    act.wait_ge(qn_d.sem, qn_d.at(b))
                    act.activation(Q, CR, ACT.Gelu).then_inc(q_gelu.sem, 1)
                elif p == 6:
                    act.wait_ge(gu_d.sem, gu_d.at(b, 1))
                    act.activation(YF, F_BANK["qw"][:, :], ACT.Square, accum_out=small[:, 43:44]).then_inc(g_act.sem, 1)
                elif p in (9, 15, 23, 26):
                    square({9: n_1, 15: n_2, 23: nf, 26: nx}[p], b)
                elif p in (12, 13):
                    for c in (2 * (p - 12), 2 * (p - 12) + 1):
                        act.wait_ge(d1_mm.sem, d1_mm.at(b, c + 1))
                        act.activation(F1[:, c, :], F_BANK[f"d1_{c}"][:, :], ACT.Gelu, bias=vec("d1_b", c)).then_inc(d1_gelu.sem, 1)
                elif p in (18, 19, 20, 21):
                    k, c0 = (p - 18) // 2, 2 * ((p - 18) % 2)
                    for c in (c0, c0 + 1):
                        n = k * CHUNKS + c
                        act.wait_ge(e1_mm.sem, e1_mm.at(b, n + 1))
                        if k:
                            act.wait_ge(e2_mm.sem, e2_mm.at(b, c // 2 + 1))
                        at = HID + CHUNKS * D + c
                        act.activation(F1[:, c, :], F_BANK[f"up{n}"][:, :], ACT.Gelu, bias=EW[:, k, at:at + 1]).then_inc(e1_gelu.sem, 1)

            def token_use(b, kind, n, following):
                if kind == "c":
                    act.wait_ge(ug_mm.sem, ug_mm.at(b, n + 1))
                    if n >= 2:
                        act.wait_ge(hh_d.sem, hh_d.at(b, n - 1))
                    act.activation(SL[:, n % 2, :], G[T_PAIR[(kind, n)]][:, :], ACT.Tanh, scale=0.5).then_inc(sl_act.sem, 1)

            def gate(b):
                act.wait_ge(gt_d.sem, gt_d.at(b, 7))
                act.activation(gate_s[:, :, 26:27], gate_s[:, :, 25:26], ACT.Exp).then_inc(gt_act.sem, 1)

            def values_in(b, n0, n1):
                for n in range(n0, n1):
                    act.wait_ge(v_mm.sem, v_mm.at(b, n + 1))
                    act.activation(V[:, n // 2, (n % 2) * S:(n % 2 + 1) * S], V_BANK[n % len(V_BANK)][:, :], ACT.Copy).then_inc(v_copy.sem, 1)

            def add_bias(b, m):
                if m:
                    act.wait_ge(rope_d.sem, rope_d.at(b, 2 * m))
                act.wait_ge(rot_d.sem, rot_d.at(b, 2 * m + 1))
                act.activation(ROT, ring_bank[("proj", m)][:, :], ACT.Identity, bias=vec(("bq", "bk")[m % 2], m // 2)).then_inc(biased.sem, 1)

            def exponentials(b, n):
                j, i = n // PER_PAIR, n % PER_PAIR
                width = (i % TILES + 1) * P
                act.wait_ge(nm_d.sem, nm_d.at(b, n + 1))
                if n >= 2:
                    act.wait_ge(pt_mm.sem, pt_mm.at(b, n - 1))
                if i == 0 and j >= 2:
                    act.wait_ge(rec_d.sem, rec_d.at(b, j - 1))
                act.activation(PR[:, n % 2, 0:width], ring_bank[("score", n)][:, 0:width], ACT.Exp,
                               bias=maxes[:, j % 2, i:i + 1], accum_out=rows[:, j % 2, 0, i:i + 1]).then_inc(p_exp.sem, 1)

            def copy_turned(b, n):
                width = (n % TILES + 1) * P
                act.wait_ge(pt_mm.sem, pt_mm.at(b, n + 1))
                if n >= 2:
                    act.wait_ge(pv_mm.sem, pv_mm.at(b, n - 1))
                act.activation(PT[:, n % 2, 0:width], G[2][:, 0:width], ACT.Copy).then_inc(pt_copy.sem, 1)

            def copy_out(b, j):
                act.wait_ge(ot_mm.sem, ot_mm.at(b, j + 1))
                if j:
                    act.wait_ge(wo_mm.sem, wo_mm.at(b, j))
                act.activation(OT, ring_bank[("out", j)][:, :], ACT.Identity, bias=vec("bv", j)).then_inc(ot_copy.sem, 1)

            def phase_1(b, t, f):
                each_step(b, t, f, filter_step, token_use, front_start, lambda t, b: None)

            def phase_2(b, f):
                if f is not None:
                    softplus(f, 0)
                add_bias(b, 0)
                values_in(b, 0, 2)
                add_bias(b, 1)
                values_in(b, 2, 4)
                if f is not None:
                    softplus(f, 1)
                values_in(b, 4, 2 * TILES)
                exponentials(b, 0)
                exponentials(b, 1)
                gate(b)
                if f is not None:
                    front_step(f, 0, (0,))
                for n in range(N_TILES):
                    j, i = n // PER_PAIR, n % PER_PAIR
                    copy_turned(b, n)
                    if n + 2 < N_TILES:
                        exponentials(b, n + 2)
                    if i in PROJECT_AT and j + 1 < PAIRS:
                        add_bias(b, 2 * (j + 1) + PROJECT_AT.index(i))
                    if i == OUT_AT and j:
                        copy_out(b, j - 1)
                    if f is not None and i % 4 == 0:
                        front_step(f, n // 4, (1,))
                    if f is not None and i % 4 == 3 and n // 4 + 1 < STATES:
                        front_step(f, n // 4 + 1, (0,))
                copy_out(b, PAIRS - 1)
                if f is not None:
                    act.wait_ge(da_exp.sem, da_exp.at(f))
                    act.wait_ge(du_d.sem, du_d.at(f))
                act.activation(XNF, XN2[:, :], ACT.Copy).then_inc(xnf_d.sem, 1)

            def front(b):
                for p in range(9):
                    front_start(b, p, None)
                softplus(b, 0)
                softplus(b, 1)
                for n in range(STATES):
                    front_step(b, n)

            laps(act, front, phase_1, phase_2)

        @block.vector
        def _(dve):
            for s in by_dve:
                s.head_start(dve)
            dve.wait_ge(s_const, n_loads)
            dve.memset(avg[:, :], 1.0 / P).then_inc(s_made, 1)
            dve.memset(ones[:, :], 1.0).then_inc(s_made, 1)
            dve.memset(XN[:, 0:PAD], 0.0).then_inc(s_made, 1)
            dve.memset(DA[:, :, :, 0:1], 0.0).then_inc(s_made, 1)
            dve.tensor_copy(ident_bf[:, :], ident[:, :]).then_inc(s_made, 1)
            dve.tensor_copy(causal_bf[:, :], causal_f).then_inc(s_made, 1)
            dve.tensor_copy(pick[:, :, :], row_of_sb[:, :].unsqueeze(2).to_broadcast([96, 2 * STATES, P])).then_inc(s_made, 1)
            dve.tensor_copy(wg_cols[:, :], vec("w_g").to_broadcast([P, P])).then_inc(s_made, 1)
            for tap in range(TAPS - 1):
                dve.tensor_tensor(conv_w[:, tap, :], conv_w[:, tap, :], in_u, ALU.mult).then_inc(s_made, 1)
            dve.wait_ge(s_alog, 1)
            dve.tensor_scalar(a_neg[:, :, :], a_neg[:, :, :], -1.0, None, ALU.mult).then_inc(s_made, 1)

            def inverse_root(b, stats, done, k):
                x, y, xyy = stats[:, 0, :], stats[:, 1, :], stats[:, 2, :]
                dve.wait_ge(done.sem, done.at(b, k))
                dve.tensor_scalar(y.bitcast(I32), x.bitcast(I32), -0.5, ROOT_GUESS, ALU.mult, ALU.add).then_inc(done.sem, 1)
                for step in range(ROOT_STEPS):
                    at = k + 1 + 3 * step
                    dve.wait_ge(done.sem, done.at(b, at))
                    dve.tensor_tensor(xyy, x, y, ALU.mult).then_inc(done.sem, 1)
                    dve.wait_ge(done.sem, done.at(b, at + 1))
                    dve.scalar_tensor_tensor(xyy, xyy, -0.5, y, ALU.mult, ALU.mult).then_inc(done.sem, 1)
                    dve.wait_ge(done.sem, done.at(b, at + 2))
                    dve.scalar_tensor_tensor(y, xyy, 1.5, y, ALU.add, ALU.mult).then_inc(done.sem, 1)

            def centre(n, b):
                dve.wait_ge(n.s_mean.sem, n.s_mean.at(b))
                dve.tensor_tensor(n.centred, n.x, F_BANK["mean_" + n.key][:, :], ALU.subtract).then_inc(n.s_centred.sem, 1)

            def root(n, b):
                dve.wait_ge(n.s_var.sem, n.s_var.at(b))
                dve.tensor_scalar(n.stats[:, 0, :], F_BANK["var_" + n.key][:, 0:TILES], n.eps, None, ALU.add).then_inc(n.s_root.sem, 1)
                inverse_root(b, n.stats, n.s_root, 1)

            def affine(n, b, out, gain, bias, done):
                dve.wait_ge(n.s_spread.sem, n.s_spread.at(b))
                dve.scalar_tensor_tensor(out, n.centred, gain, F_BANK["spread_" + n.key][:, :], ALU.mult, ALU.mult).then_inc(done.sem, 1)
                dve.wait_ge(done.sem, done.at(b, 1))
                dve.tensor_scalar(out, out, bias, None, ALU.add).then_inc(done.sem, 1)

            def front_start(f, p, b):
                if p == 0:
                    dve.wait_ge(xnb_d.sem, xnb_d.at(f - 1))
                    dve.wait_ge(r_mm.sem, r_mm.at(f - 1))
                    centre(n1, f)
                elif p == 1:
                    root(n1, f)
                elif p == 2:
                    dve.wait_ge(n1.s_spread.sem, n1.s_spread.at(f))
                    dve.tensor_tensor(xn, xn, F_BANK["spread_x"][:, :], ALU.mult).then_inc(xn_done.sem, 1)
                elif p == 7:
                    out = F_BANK["bc"]
                    dve.wait_ge(c_mm.sem, c_mm.at(f - 1))
                    dve.wait_ge(bc_mm.sem, bc_mm.at(f))
                    dve.tensor_copy(S3[:, :], out[0:96, :]).then_inc(bc_split.sem, 1)
                    dve.wait_ge(bc_split.sem, bc_split.at(f, 1))
                    dve.tensor_tensor(R1, out[0:96, :], S3[:, :], ALU.subtract).then_inc(bc_split.sem, 1)
                    dve.wait_ge(bc_split.sem, bc_split.at(f, 2))
                    dve.tensor_copy(S3B[:, :], R1).then_inc(bc_split.sem, 1)
                    dve.wait_ge(bc_split.sem, bc_split.at(f, 3))
                    dve.tensor_tensor(R1[64:96, :], R1[64:96, :], S3B[64:96, :], ALU.subtract).then_inc(bc_split.sem, 1)
                    dve.tensor_copy(S3[32:64, :], S3B[32:64, :]).then_inc(bc_split.sem, 1)
                    dve.wait_ge(bc_split.sem, bc_split.at(f, 5))
                    dve.tensor_copy(S3[64:96, :], R1[64:96, :]).then_inc(bc_split.sem, 1)
                elif p == 8:
                    dve.wait_ge(bc_split.sem, bc_split.at(f))
                    dve.wait_ge(dt_mm.sem, dt_mm.at(f))
                    dve.tensor_copy(DT, F_BANK["dt"][0:RANK, :]).then_inc(dt_copy.sem, 1)

            def softplus_relu(b):
                for h, bank in ((0, FB), (1, FC)):
                    dve.wait_ge(soft.sem, soft.at(b, h + 1))
                    dve.tensor_scalar(HS[:, h, :], bank[:, :], vec("dt_b", h), 0.0, ALU.add, ALU.max).then_inc(relu_d.sem, 1)

            def softplus(b):
                dve.wait_ge(out_d.sem, out_d.at(b - 2))
                dve.wait_ge(soft.sem, soft.at(b, 3))
                dve.tensor_scalar(DELTA[:, :, :], D1[:, :, :], 1.0, None, ALU.add).then_inc(wide_d.sem, 1)
                dve.wait_ge(wide_d.sem, wide_d.at(b, 1))
                dve.scalar_tensor_tensor(D1[:, :, :], DELTA[:, :, :], -1.0, D1[:, :, :], ALU.add, ALU.subtract).then_inc(wide_d.sem, 1)

            def softplus_sum(b):
                dve.wait_ge(wide_d.sem, wide_d.at(b, 2))
                dve.wait_ge(relu_d.sem, relu_d.at(b))
                dve.tensor_tensor(HS[:, :, :], HS[:, :, :], D1[:, :, :], ALU.subtract).then_inc(wide_d.sem, 1)

            def softplus_end(b):
                dve.wait_ge(soft.sem, soft.at(b, 4))
                dve.wait_ge(wide_d.sem, wide_d.at(b, 3))
                dve.tensor_tensor(DELTA[:, :, :], HS[:, :, :], DELTA[:, :, :], ALU.add).then_inc(delta_d.sem, 1)

            def front_step(b, n, part):
                if part == 0:
                    dve.wait_ge(b_mm.sem, b_mm.at(b, n + 1))
                    if n == 0:
                        dve.wait_ge(du_d.sem, du_d.at(b))
                    dve.tensor_tensor(D1[:, :, :], DU[:, :, :], FB[:, :].unsqueeze(1).to_broadcast([P, HALVES, S]), ALU.mult).then_inc(db_mul.sem, 1)
                elif part == 1:
                    dve.wait_ge(db_mul.sem, db_mul.at(b, n + 1))
                    dve.wait_ge(da_exp.sem, da_exp.at(b, 2 * n + 2))
                    dve.tensor_tensor_scan(HS[:, :, :].rearrange("p h s -> p (h s)"), DA[:, n % 2, :, :].rearrange("p h s -> p (h s)"),
                                           D1[:, :, :].rearrange("p h s -> p (h s)"), 0.0, ALU.mult, ALU.add).then_inc(scan_d.sem, 1)
                else:
                    dve.wait_ge(scan_d.sem, scan_d.at(b, n + 1))
                    dve.wait_ge(c_mm.sem, c_mm.at(b, n + 1))
                    if n >= 2:
                        dve.wait_ge(y_add.sem, y_add.at(b, n - 1))
                    elif n == 0:
                        dve.wait_ge(y_add.sem, y_add.at(b - 1))
                        dve.wait_ge(dn_mm.sem, dn_mm.at(b - 2))
                    dve.tensor_tensor(HC[:, n % 2, :, :], HS[:, :, :], FC[:, :].unsqueeze(1).to_broadcast([P, HALVES, S]), ALU.mult).then_inc(hc_mul.sem, 1)

            def filter_step(b, p, f):
                if p == -1:
                    dve.wait_ge(xnb_d.sem, xnb_d.at(b))
                    dve.wait_ge(m_mm.sem, m_mm.at(b))
                    dve.tensor_tensor(M0[:, :], XNB[:, :], F_BANK["mamba"][:, :], ALU.add).then_inc(m0_d.sem, 1)
                elif p == 0:
                    dve.wait_ge(wo_mm.sem, wo_mm.at(b - 1))
                    dve.wait_ge(m0_d.sem, m0_d.at(b))
                    centre(n0, b)
                    dve.tensor_reduce(small[:, 1:2], XNB[:, :], AX.X, ALU.add).then_inc(xm_d.sem, 1)
                    dve.wait_ge(xm_d.sem, xm_d.at(b, 1))
                    dve.tensor_scalar(small[:, 0:1], small[:, 1:2], 1.0 / S, None, ALU.mult).then_inc(xm_d.sem, 1)
                elif p == 1:
                    root(n0, b)
                    dve.wait_ge(lg_mm.sem, lg_mm.at(b))
                    dve.tensor_tensor(small[0:1, 8:16], F_BANK["var_0"][0:1, 16:24], row_bias[0:1, 0:8], ALU.add).then_inc(rt_d.sem, 1)
                    dve.wait_ge(rt_d.sem, rt_d.at(b, 1))
                    dve.tensor_reduce(small[0:1, 4:5], small[0:1, 8:16], AX.X, ALU.max).then_inc(rt_d.sem, 1)
                    dve.wait_ge(rt_d.sem, rt_d.at(b, 2))
                    dve.tensor_scalar(small[0:1, 5:6], small[0:1, 4:5], -1.0, None, ALU.mult).then_inc(rt_d.sem, 1)
                elif p == 2:
                    affine(n0, b, H, vec("ln0_g"), vec("ln0_b"), h_d)
                elif p == 3:
                    dve.wait_ge(qsq_d.sem, qsq_d.at(b))
                    dve.tensor_scalar(QP, F_BANK["q"][:, :], vec("q_b"), None, ALU.add).then_inc(qp_d.sem, 1)
                    dve.wait_ge(ksq_d.sem, ksq_d.at(b))
                    dve.tensor_scalar(KP, F_BANK["k"][:, :], vec("k_b"), None, ALU.add).then_inc(kp_d.sem, 1)
                    centre(ni, b)
                    dve.wait_ge(rt_act.sem, rt_act.at(b, 1))
                    dve.reciprocal(small[0:1, 3:4], small[0:1, 6:7]).then_inc(rt_d.sem, 1)
                    dve.wait_ge(rt_d.sem, rt_d.at(b, 4))
                    dve.tensor_scalar(small[0:1, 48:56], small[0:1, 16:24], small[0:1, 3:4], None, ALU.mult).then_inc(rt_d.sem, 1)
                    dve.wait_ge(idx_rd.sem, idx_rd.at(b - 1))
                    dve.wait_ge(rt_d.sem, rt_d.at(b, 5))
                    dve.sem_inc(dve_passed, 1)
                    dve.max(small[0:1, 24:32], small[0:1, 48:56]).then_inc(rt_d.sem, 1)
                    dve.wait_ge(rt_d.sem, rt_d.at(b, 6))
                    dve.sem_inc(dve_passed, 1)
                    dve.max_index(pick_i[0:1, :], small[0:1, 24:32], small[0:1, 48:56]).then_inc(rt_d.sem, 1)
                    dve.tensor_scalar(small[0:1, 7:8], small[0:1, 24:25], -1.0, None, ALU.mult).then_inc(rt_d.sem, 1)
                elif p == 4:
                    dve.wait_ge(qk_ss_mm.sem, qk_ss_mm.at(b))
                    out = F_BANK["ss"]
                    dve.tensor_scalar(qk_stats[:, 0, 0:2 * TILES], out[:, 0:2 * TILES], TINY, None, ALU.max).then_inc(qk_root.sem, 1)
                    dve.tensor_scalar(qk_stats[:, 0, 2 * TILES:], out[:, 2 * TILES:3 * TILES], ni.eps, None, ALU.add).then_inc(qk_root.sem, 1)
                    inverse_root(b, qk_stats, qk_root, 2)
                    dve.wait_ge(rt_act.sem, rt_act.at(b, 2))
                    dve.reciprocal(small[0:1, 37:38], small[0:1, 36:37]).then_inc(rt_d.sem, 1)
                    dve.wait_ge(rt_d.sem, rt_d.at(b, 9))
                    dve.tensor_scalar(small[0:1, 40:42], small[0:1, 38:40], small[0:1, 37:38], None, ALU.mult).then_inc(rt_d.sem, 1)
                elif p == 5:
                    dve.wait_ge(qp_d.sem, qp_d.at(b))
                    dve.wait_ge(qs_mm.sem, qs_mm.at(b))
                    dve.tensor_tensor(CR, QP, F_BANK["spread_q"][:, :], ALU.mult).then_inc(qn_d.sem, 1)
                    dve.wait_ge(kp_d.sem, kp_d.at(b))
                    dve.wait_ge(ks_mm.sem, ks_mm.at(b))
                    dve.tensor_tensor(KN, KP, F_BANK["spread_k"][:, :], ALU.mult).then_inc(kn_d.sem, 1)
                    dve.wait_ge(is_mm.sem, is_mm.at(b))
                    dve.scalar_tensor_tensor(LNI, CX, vec("lni_g"), F_BANK["spread_i"][:, :], ALU.mult, ALU.mult).then_inc(lni_d.sem, 1)
                    dve.wait_ge(lni_d.sem, lni_d.at(b, 1))
                    dve.tensor_scalar(LNI, LNI, vec("lni_b"), None, ALU.add).then_inc(lni_d.sem, 1)
                elif p == 6:
                    dve.wait_ge(wb_mm.sem, wb_mm.at(b))
                    dve.tensor_copy(small[:, 32:34], F_BANK["wb"][:, 0:2]).then_inc(wb_d.sem, 1)
                    dve.wait_ge(qw_mm.sem, qw_mm.at(b))
                    dve.tensor_tensor_reduce(out=CX, in0=Q, in1=F_BANK["qw"][:, :], scale=1.0, scalar=0.0, op0=ALU.mult, op1=ALU.add,
                                             accum_out=small[:, 42:43]).then_inc(gu_d.sem, 1)
                    dve.wait_ge(g_act.sem, g_act.at(b))
                    dve.tensor_scalar(g_stats[:, 0, :], small[:, 43:44], 1.0 / D, TINY, ALU.mult, ALU.max).then_inc(gu_d.sem, 1)
                    inverse_root(b, g_stats, gu_d, 2)
                    dve.wait_ge(gu_d.sem, gu_d.at(b, 2 + ROOT_OPS))
                    dve.tensor_scalar(small[:, 47:48], small[:, 42:43], float(D) ** -0.5, g_stats[:, 1, :], ALU.mult, ALU.mult).then_inc(gu_d.sem, 1)
                    dve.wait_ge(gu_d.sem, gu_d.at(b))
                    dve.wait_ge(kn_d.sem, kn_d.at(b))
                    dve.tensor_scalar(GK, KN, small[:, 47:48], None, ALU.mult).then_inc(gk_d.sem, 1)
                elif p == 7:
                    dve.wait_ge(lni_d.sem, lni_d.at(b))
                    dve.wait_ge(proj_mm.sem, proj_mm.at(b))
                    dve.scalar_tensor_tensor(TMP, F_BANK["proj"][:, :], vec("proj_b"), LNI, ALU.add, ALU.mult).then_inc(hsm_d.sem, 1)
                elif p == 8:
                    dve.wait_ge(fl_mm.sem, fl_mm.at(b))
                    dve.scalar_tensor_tensor(M1, F_BANK["fl"][:, :], vec("fl_b"), H, ALU.add, ALU.add).then_inc(m1_d.sem, 1)
                elif p in (9, 15, 23, 26):
                    centre({9: n_1, 15: n_2, 23: nf, 26: nx}[p], b)
                elif p in (10, 16, 24, 27):
                    root({10: n_1, 16: n_2, 24: nf, 27: nx}[p], b)
                elif p == 11:
                    affine(n_1, b, H2, vec("ln1_g"), vec("ln1_b"), h2_d)
                elif p == 14:
                    dve.wait_ge(d2_mm.sem, d2_mm.at(b))
                    dve.scalar_tensor_tensor(M2, F_BANK["d2"][:, :], vec("d2_b"), H2, ALU.add, ALU.add).then_inc(m2_d.sem, 1)
                elif p == 17:
                    affine(n_2, b, L0A, vec("ln2_g"), vec("ln2_b"), l0a_d)
                elif p == 18:
                    dve.wait_ge(xb_in.sem, xb_in.at(b))
                    dve.wait_ge(l0a_d.sem, l0a_d.at(b, 2))
                    dve.tensor_tensor(L0A, L0A, XB, ALU.add).then_inc(l0a_d.sem, 1)
                    w0, w1 = small[:, 32:33], small[:, 33:34]
                    at = EXPERT_COLS - 1
                    for k in range(PICKS):
                        dve.wait_ge(ew_in[k].sem, ew_in[k].at(b))
                    dve.wait_ge(wb_d.sem, wb_d.at(b))
                    dve.tensor_scalar(small[:, 34:35], EW[:, 0, at:at + 1], w0, None, ALU.mult).then_inc(yf_d.sem, 1)
                    dve.wait_ge(yf_d.sem, yf_d.at(b, 1))
                    dve.scalar_tensor_tensor(small[:, 35:36], EW[:, 1, at:at + 1], w1, small[:, 34:35], ALU.mult, ALU.add).then_inc(yf_d.sem, 1)
                    dve.wait_ge(yf_d.sem, yf_d.at(b, 2))
                    dve.tensor_scalar(YF, XNB[:, :], small[:, 35:36], None, ALU.add).then_inc(yf_d.sem, 1)
                elif p in (20, 22):
                    k = (p - 20) // 2
                    dve.wait_ge(yf_d.sem, yf_d.at(b, 3 + k))
                    dve.wait_ge(e2_mm.sem, e2_mm.at(b, 2 * k + 2))
                    dve.scalar_tensor_tensor(YF, F_BANK["down0"][:, :], small[:, 32 + k:33 + k], YF, ALU.mult, ALU.add).then_inc(yf_d.sem, 1)
                elif p == 25:
                    affine(nf, b, YF, vec("gamma"), vec("beta"), l0f_d)
                    dve.wait_ge(l0f_d.sem, l0f_d.at(b))
                    dve.wait_ge(l0a_d.sem, l0a_d.at(b))
                    dve.tensor_tensor(X2[:, :], YF, L0A, ALU.add).then_inc(x2_d.sem, 1)
                elif p == 28:
                    dve.wait_ge(nx.s_spread.sem, nx.s_spread.at(b))
                    dve.tensor_tensor(XN2[:, :], nx.centred, F_BANK["spread_n"][:, :], ALU.mult).then_inc(xn2_d.sem, 1)

            def token_use(b, kind, n, following):
                g = T_PAIR[(kind, n)]
                if kind == "w":
                    dve.wait_ge(wt_mm.sem, wt_mm.at(b, n + 1))
                    if n >= 2:
                        dve.wait_ge(ug_mm.sem, ug_mm.at(b, CHUNKS * (n - 1)))
                    if n == 0:
                        dve.wait_ge(xnf_d.sem, xnf_d.at(b))
                    dve.tensor_tensor(XS[:, n % 2, :], XNF, G[g][:, :], ALU.mult).then_inc(xs_d.sem, 1)
                    return
                dve.wait_ge(sl_act.sem, sl_act.at(b, n + 1))
                dve.scalar_tensor_tensor(SL[:, n % 2, :], SL[:, n % 2, :], 1.0, G[g][:, :], ALU.add, ALU.mult).then_inc(sx_d.sem, 1)
                if n >= 4:
                    dve.wait_ge(dn_mm.sem, dn_mm.at(b, n - 3))
                elif following is not None and n % 2 == 0:
                    dve.wait_ge(y_add.sem, y_add.at(following, STATES - 1 + n // 2))
                dve.wait_ge(sx_d.sem, sx_d.at(b, n + 1))
                dve.scalar_tensor_tensor(HH[:, n % 4, :], SL[:, n % 2, :], 0.5, G[g + 1][:, :], ALU.mult, ALU.mult).then_inc(hh_d.sem, 1)

            def token_end(b):
                dve.wait_ge(out_st.sem, out_st.at(b - 1))
                dve.wait_ge(dn_mm.sem, dn_mm.at(b))
                dve.tensor_tensor(OUT, X3, G[4][:, :], ALU.add).then_inc(out_d.sem, 1)

            def gate_top(b):
                gs = gate_s
                dve.wait_ge(wt_mm.sem, wt_mm.at(b - 1))
                dve.wait_ge(gl_mm.sem, gl_mm.at(b))
                dve.tensor_tensor(gs[:, :, 0:8], G[4][:, 0:32].rearrange("p (t e) -> p t e", e=8),
                                  row_bias[:, 8:16].unsqueeze(1).to_broadcast([P, TILES, 8]), ALU.add).then_inc(gt_d.sem, 1)
                dve.wait_ge(gt_d.sem, gt_d.at(b, 1))
                dve.sem_inc(dve_passed, 1)
                for t in range(TILES):
                    dve.max(gs[:, t, 8:16], gs[:, t, 0:8]).then_inc(gt_d.sem, 1)
                dve.wait_ge(gt_d.sem, gt_d.at(b, 5))
                dve.sem_inc(dve_passed, 1)
                for t in range(TILES):
                    ins = dve.max_index(gate_i[:, t, :], gs[:, t, 8:16], gs[:, t, 0:8])
                ins.then_inc(gt_d.sem, 1)
                dve.tensor_tensor(gs[:, :, 25:26], gs[:, :, 9:10], gs[:, :, 8:9], ALU.subtract).then_inc(gt_d.sem, 1)
                dve.wait_ge(gt_d.sem, gt_d.at(b, 6))
                dve.tensor_copy(gs[:, :, 16:24], gate_i[:, :, :]).then_inc(gt_d.sem, 1)
            def gate_weights(b):
                gs = gate_s
                dve.wait_ge(gt_act.sem, gt_act.at(b))
                dve.tensor_scalar(gs[:, :, 24:25], gs[:, :, 26:27], 1.0, None, ALU.add).then_inc(gt_d.sem, 1)
                dve.wait_ge(gt_d.sem, gt_d.at(b, 9))
                dve.reciprocal(gs[:, :, 27:28], gs[:, :, 24:25]).then_inc(gt_d.sem, 1)
                dve.wait_ge(gt_d.sem, gt_d.at(b, 10))
                dve.tensor_tensor(gs[:, :, 28:29], gs[:, :, 27:28], gs[:, :, 26:27], ALU.mult).then_inc(gt_d.sem, 1)
                dve.wait_ge(gt_d.sem, gt_d.at(b, 11))
                numbers = row_bias[:, 16:24]
                for t in range(TILES):
                    dve.tensor_scalar(gs[:, t, 32:40], numbers, gs[:, t, 16:17], gs[:, t, 27:28], ALU.is_equal, ALU.mult)
                    ins = dve.tensor_scalar(gs[:, t, 40:48], numbers, gs[:, t, 17:18], gs[:, t, 28:29], ALU.is_equal, ALU.mult)
                ins.then_inc(gt_d.sem, 1)
                dve.wait_ge(gt_d.sem, gt_d.at(b, 12))
                dve.tensor_tensor(gs[:, :, 48:56], gs[:, :, 32:40], gs[:, :, 40:48], ALU.add).then_inc(gt_d.sem, 1)

            def rotate(b, m):
                j, bias = m // 2, ("bq", "bk")[m % 2]
                x = ring_bank[("proj", m)]
                if m:
                    dve.wait_ge(rope_d.sem, rope_d.at(b, 2 * m))
                dve.wait_ge(pj_mm.sem, pj_mm.at(b, m + 1))
                dve.scalar_tensor_tensor(ROT3[:, :], x[:, :], vec(bias, j), sin_t[:, :], ALU.add, ALU.mult).then_inc(rot_d.sem, 1)
                dve.wait_ge(rot_d.sem, rot_d.at(b, 2 * m + 1))
                dve.sem_inc(dve_passed, 1)
                dve.stream_shuffle(ROT2, ROT3[:, :], [k ^ 1 for k in range(32)]).then_inc(rot_d.sem, 1)

            def largest(b, n):
                j, i = n // PER_PAIR, n % PER_PAIR
                width = (i % TILES + 1) * P
                dve.wait_ge(sc_mm.sem, sc_mm.at(b, n + 1))
                dve.tensor_reduce(maxes[:, j % 2, i:i + 1], ring_bank[("score", n)][:, 0:width], AX.X, ALU.max,
                                  negate=True).then_inc(nm_d.sem, 1)

            def divide(b, j):
                dve.wait_ge(p_exp.sem, p_exp.at(b, PER_PAIR * (j + 1)))
                dve.reciprocal(rows[:, j % 2, 1, :], rows[:, j % 2, 0, :]).then_inc(rec_d.sem, 1)
                if j:
                    dve.wait_ge(ot_mm.sem, ot_mm.at(b, j))
                dve.wait_ge(pv_mm.sem, pv_mm.at(b, PER_PAIR * (j + 1)))
                dve.wait_ge(rec_d.sem, rec_d.at(b, j + 1))
                dve.tensor_tensor(O.rearrange("p (t h d) -> p t h d", t=TILES, h=2),
                                  G[3][:, :].rearrange("p (t h d) -> p t h d", t=TILES, h=2),
                                  rows[:, j % 2, 1, :].rearrange("p (h t) -> p t h", h=2).unsqueeze(3).to_broadcast([P, TILES, 2, DK]),
                                  ALU.mult).then_inc(o_d.sem, 1)

            def attention_end(b, following):
                if following is not None:
                    dve.wait_ge(da_exp.sem, da_exp.at(following))
                    dve.wait_ge(du_d.sem, du_d.at(following))
                dve.wait_ge(wo_mm.sem, wo_mm.at(b))
                dve.scalar_tensor_tensor(X3, G[4][:, :], vec("bo"), X2[:, :], ALU.add, ALU.add).then_inc(x3_d.sem, 1)
                dve.wait_ge(x3_d.sem, x3_d.at(b, 1))
                dve.tensor_tensor(X3, X3, XN2[:, :], ALU.add).then_inc(x3_d.sem, 1)

            def phase_1(b, t, f):
                each_step(b, t, f, filter_step, token_use, front_start, attention_end)
                if t is not None:
                    token_end(t)

            def phase_2(b, f):
                rotate(b, 0)
                if f is not None:
                    softplus_relu(f)
                    softplus(f)
                rotate(b, 1)
                if f is not None:
                    softplus_sum(f)
                    softplus_end(f)
                gate_top(b)
                largest(b, 0)
                largest(b, 1)
                for n in range(N_TILES):
                    j, i = n // PER_PAIR, n % PER_PAIR
                    if i == 1 and j:
                        divide(b, j - 1)
                    if n == 2:
                        gate_weights(b)
                    if n + 2 < N_TILES:
                        largest(b, n + 2)
                    if i in PROJECT_AT and j + 1 < PAIRS:
                        rotate(b, 2 * (j + 1) + PROJECT_AT.index(i))
                    if f is not None and i % 4 > 0:
                        front_step(f, 2 * j + i // 4, i % 4 - 1)
                divide(b, PAIRS - 1)

            def front(b):
                for p in range(9):
                    front_start(b, p, None)
                softplus_relu(b)
                softplus(b)
                softplus_sum(b)
                softplus_end(b)
                for n in range(STATES):
                    for part in range(3):
                        front_step(b, n, part)

            def late():
                dve.wait_ge(s_late, n_late)
                q_w, q_b = w("wq", 0, HEADS * DK), V_[:, VECS["bq"][0]:VECS["bq"][0] + PAIRS]
                dve.tensor_scalar(q_w, q_w, DK ** -0.5, None, ALU.mult).then_inc(s_made, 1)
                dve.tensor_scalar(q_b, q_b, DK ** -0.5, None, ALU.mult).then_inc(s_made, 1)
                dve.wait_ge(s_made, 15)

            laps(dve, front, phase_1, phase_2, late)

        @block.gpsimd
        def _(pool):
            for s in by_pool:
                s.head_start(pool)
            pool.wait_ge(s_const, n_loads)
            pool.tensor_tensor(conv_w[:, TAPS - 1, :], conv_w[:, TAPS - 1, :], in_u, ALU.mult).then_inc(s_made, 1)

            def front_start(b):
                pool.wait_ge(yf_d.sem, yf_d.at(b - 1))
                pool.wait_ge(xn_done.sem, xn_done.at(b))
                pool.sem_inc(pool_passed, 1)
                pool.tensor_copy(XNB[:, :], xn).then_inc(xnb_d.sem, 1)
                pool.wait_ge(m_mm.sem, m_mm.at(b - 1))
                pool.wait_ge(u_silu.sem, u_silu.at(b))
                pool.sem_inc(pool_passed, 1)
                for h in range(HALVES):
                    pool.tensor_scalar(Y[:, h, :], US[:, h, :], vec("D_skip", h), None, ALU.mult).then_inc(skip_y.sem, 1)

            def front_du(b):
                pool.wait_ge(db_mul.sem, db_mul.at(b - 1))
                pool.wait_ge(out_st.sem, out_st.at(b - 2))
                pool.wait_ge(delta_d.sem, delta_d.at(b))
                pool.tensor_tensor(DU[:, :, :], DELTA[:, :, :], US[:, :, :], ALU.mult).then_inc(du_d.sem, 1)

            def front_step(b, n):
                if n == 0:
                    pool.wait_ge(skip_y.sem, skip_y.at(b))
                else:
                    pool.wait_ge(y_add.sem, y_add.at(b, n))
                pool.wait_ge(hc_mul.sem, hc_mul.at(b, n + 1))
                pool.tensor_tensor(Y[:, :, :], Y[:, :, :], HC[:, n % 2, :, :], ALU.add).then_inc(y_add.sem, 1)

            def front_end(b):
                pool.wait_ge(y_add.sem, y_add.at(b))
                pool.wait_ge(r_silu.sem, r_silu.at(b))
                pool.tensor_tensor(Y[:, :, :], Y[:, :, :], SR[:, :, :], ALU.mult).then_inc(y_gate.sem, 1)

            def add_rotated(b, m):
                j = m // 2
                if j >= 2:
                    pool.wait_ge(sc_mm.sem, sc_mm.at(b, PER_PAIR * (j - 1)))
                pool.wait_ge(biased.sem, biased.at(b, m + 1))
                pool.tensor_tensor(ROT, ROT, cos_t[:, :], ALU.mult).then_inc(rope_d.sem, 1)
                pool.wait_ge(rope_d.sem, rope_d.at(b, 2 * m + 1))
                pool.wait_ge(rot_d.sem, rot_d.at(b, 2 * m + 2))
                pool.tensor_tensor(QK[:, j % 2, m % 2, :], ROT, ROT2, ALU.add).then_inc(rope_d.sem, 1)

            def phase_1(b, t, f):
                pass

            def phase_2(b, f):
                if f is not None:
                    front_start(f)
                add_rotated(b, 0)
                add_rotated(b, 1)
                if f is not None:
                    front_du(f)
                for n in range(N_TILES):
                    j, i = n // PER_PAIR, n % PER_PAIR
                    if i in PROJECT_AT and j + 1 < PAIRS:
                        add_rotated(b, 2 * (j + 1) + PROJECT_AT.index(i))
                    if f is not None and i % 4 == 3:
                        front_step(f, 2 * j + i // 4)
                if f is not None:
                    front_end(f)

            def front(b):
                front_start(b)
                front_du(b)
                for n in range(STATES):
                    front_step(b, n)
                front_end(b)

            def late():
                pool.wait_ge(s_late, n_late)

            laps(pool, front, phase_1, phase_2, late)


def lay_out(inputs):
    L0, L1 = "L0_attn_", "L1_attn_"
    g = {k: np.asarray(v) for k, v in inputs.items()}

    def stack_rows(t):
        n = t.shape[0] // P
        return t.reshape(n, P, -1).transpose(1, 0, 2).reshape(P, -1)

    in_w, x_w = g[L0 + "in_proj_w"].T, g[L0 + "x_proj_w"].T
    bc = x_w[:, RANK:]
    named = {
        "in_res": in_w[:, INNER:],
        "x_bc": stack_rows(np.concatenate([bc, bc, bc], 1)), "x_dt": stack_rows(x_w[:, :RANK]),
        "out_proj": stack_rows(g[L0 + "out_proj_w"].T), "q": g[L0 + "q_w"].T, "k": g[L0 + "k_w"].T,
        "proj": g[L0 + "proj_w"].T, "fl": g[L0 + "fl_w"].T, "d1": g[L0 + "d1_w"].T, "d2": stack_rows(g[L0 + "d2_w"].T),
        "router": g["L0_ffn_Wr"], "gate": g["L1_ffn_Wg"],
        "wq": g[L1 + "wq"].T, "wk": g[L1 + "wk"].T,
        "wv": g[L1 + "wv"].T, "wo": stack_rows(g[L1 + "wo"].T),
    }
    weights = np.concatenate([named[k] for k in WEIGHTS], 1)
    vecs = {"dt_b": g[L0 + "dt_proj_b"], "gamma": g["L0_ffn_gamma"], "beta": g["L0_ffn_beta"]}
    for k in VECS:
        if k not in vecs:
            vecs[k] = g[(L1 if k in ("bq", "bk", "bv", "bo") else L0) + k]
    columns = np.concatenate([vecs[k].reshape(-1, P).T for k in VECS], 1)
    e_w1, e_w2 = g["L0_ffn_W1"], g["L0_ffn_W2"]
    experts = np.concatenate([
        e_w1, e_w2.reshape(EXPERTS, CHUNKS, P, D).transpose(0, 2, 1, 3).reshape(EXPERTS, P, -1),
        g["L0_ffn_b1"].reshape(EXPERTS, CHUNKS, P).transpose(0, 2, 1), g["L0_ffn_b2"][:, :, None]], 2)
    row_biases = np.concatenate([g["L0_ffn_br"], g["L1_ffn_bg"], np.arange(EXPERTS, dtype=np.float32)])
    theta = np.float32(10000.0) ** (np.arange(0, DK, 2, dtype=np.float32) / np.float32(DK))
    freqs = np.arange(S, dtype=np.float32)[:, None] * (np.float32(1.0) / theta)[None, :]
    angle = np.concatenate([freqs, freqs], -1).T
    sign = np.where(np.arange(DK) % 2 == 0, np.float32(-1), np.float32(1))[:, None]
    cos = np.tile(np.cos(angle), (2, 1)).astype(np.float32)
    sin = np.tile((np.sin(angle) * sign).reshape(DK // 2, 2, S)[:, ::-1].reshape(DK, S), (2, 1)).astype(np.float32)
    causal = np.where(np.arange(P)[None, :] > np.arange(P)[:, None], np.float32(MASKED), np.float32(0))
    row_of = (np.arange(96)[:, None] % 32 == np.arange(2 * STATES)[None, :]).astype(np.float32)
    arrays = {
        "xT": g[L0 + "input_tensor"].transpose(0, 2, 1), "weights": weights, "vecs": columns,
        "conv_rows": g[L0 + "conv_w"].T, "dt_w": g[L0 + "dt_proj_w"].T,
        "a_log": g[L0 + "A_log"].reshape(HALVES, P, STATES).transpose(1, 0, 2),
        "moe_up": g["L1_ffn_W1"].transpose(1, 0, 2), "moe_gate": g["L1_ffn_W3"].transpose(1, 0, 2),
        "moe_down": g["L1_ffn_W2"].reshape(EXPERTS, CHUNKS, P, D).transpose(2, 0, 1, 3),
        "experts": experts, "row_biases": row_biases, "cos": cos, "sin": sin,
        "identity": np.eye(P, dtype=np.float32), "causal": causal, "row_of": row_of, "in_u_w": in_w[:, :INNER],
    }
    return {k: np.ascontiguousarray(v) for k, v in arrays.items()}


def program(nc, shapes):
    args = [nc.dram_tensor(k, s, F32, kind="ExternalInput").ap() for k, s in shapes.items()]
    out = nc.dram_tensor("outT", (B, D, S), F32, kind="ExternalOutput").ap()
    build(nc, *args, out)


def kernel(**inputs):
    import concourse.bacc as bacc
    from concourse.bass_utils import run_bass_kernel_spmd

    arrays = lay_out(inputs)
    nc = bacc.Bacc("TRN2", target_bir_lowering=False, num_devices=1)
    program(nc, {k: v.shape for k, v in arrays.items()})
    r = run_bass_kernel_spmd(nc, [arrays], core_ids=[0])
    return np.ascontiguousarray(r.results[0]["outT"].transpose(0, 2, 1))
```
